# Optimizing a Trainium2 kernel written in Bass

```python
import numpy as np
import jax
import jax.numpy as jnp

def _softmax(x, axis=-1):
    return jax.nn.softmax(x, axis=axis)

def _gelu(x):
    return jax.nn.gelu(x, approximate=True)

def _silu(x):
    return jax.nn.silu(x)

def _sigmoid(x):
    return jax.nn.sigmoid(x)

def _layernorm(x, axis=-1, eps=1e-05):
    m = jnp.mean(x, axis=axis, keepdims=True)
    v = jnp.var(x, axis=axis, keepdims=True)
    return (x - m) / jnp.sqrt(v + eps)

def _scatter_add(tgt, idx, src, axis=0):
    return tgt.at[idx].add(src)

def _segment_sum(src, seg, n):
    return jax.ops.segment_sum(src, seg, n)
kernel_name = 'mk_gnn_ffn_d1_gnn_r8_6c62c5'

def setup_inputs(seed: int=0):
    np.random.seed(seed)
    _w = jnp.asarray

    def _rec_inputs():
        import jax
        import jax.numpy as jnp
        _gk = jax.random.key(seed)
        x = -6.415e-05 + 1 * jax.random.normal(jax.random.fold_in(_gk, 1), (1250, 1024), jnp.float32)
        src = jax.random.randint(jax.random.fold_in(_gk, 2), (20000,), 0, 1250, jnp.int32)
        dst = jnp.minimum((1250 * jax.random.uniform(jax.random.fold_in(_gk, 3), (20000,)) ** 2.0).astype(jnp.int32), 9999)
        _o = jnp.argsort(dst, stable=True)
        src = src[_o]
        dst = dst[_o]
        edge_type_8 = jax.random.randint(jax.random.fold_in(_gk, 12), (20000,), 0, 8, jnp.int32)
        return (x, src, dst, edge_type_8)
    x, src, dst, edge_type_8 = _rec_inputs()

    def _L0_gnn_setup():
        import jax, jax.numpy as jnp
        import numpy as np
        N, D, R, E = (1250, 1024, 8, 10000)

        def _rgcn(x, edge_index, edge_type, weight, root, bias):
            src, dst = (edge_index[0], edge_index[1])
            msgs = x[src]
            out = x @ root + bias
            n = x.shape[0]
            for r in range(weight.shape[0]):
                mask = (edge_type == r).astype(x.dtype)
                sums = jax.ops.segment_sum(msgs * mask[:, None], dst, num_segments=n)
                cnt = jax.ops.segment_sum(mask, dst, num_segments=n)
                mean = sums / jnp.maximum(cnt, 1.0)[:, None]
                out = out + mean @ weight[r]
            return out
        key = jax.random.key(seed)
        ks = jax.random.split(key, 8)
        s = 1.0 / np.sqrt(D)
        x = jax.random.normal(ks[0], (N, D), dtype=jnp.float32)
        edge_index = jax.random.randint(ks[1], (2, E), 0, N, dtype=jnp.int64)
        edge_type = jax.random.randint(ks[2], (E,), 0, R, dtype=jnp.int64)
        weight = jax.random.normal(ks[3], (R, D, D), dtype=jnp.float32) * s
        root = jax.random.normal(ks[4], (D, D), dtype=jnp.float32) * s
        bias = jnp.zeros((D,), dtype=jnp.float32)
        w_gate = jax.random.normal(ks[5], (2 * D, D), dtype=jnp.float32) * (1.0 / np.sqrt(2 * D))
        b_gate = jnp.zeros((D,), dtype=jnp.float32)
        return {'x': x, 'edge_index': edge_index, 'edge_type': edge_type, 'weight': weight, 'root': root, 'bias': bias, 'w_gate': w_gate, 'b_gate': b_gate}
    _L0_gnn_all = _L0_gnn_setup()
    _L0_gnn_in = {k: v for k, v in _L0_gnn_all.items() if k in ('weight', 'root', 'bias', 'w_gate', 'b_gate')}
    del _L0_gnn_all

    def _L0_ffn_setup():
        import jax, jax.numpy as jnp
        import numpy as np
        import math
        E = 16
        TOP_K = 2
        D = 1024
        F = 512
        SH = 256
        key = jax.random.key(seed)
        ks = jax.random.split(key, 10)
        s = lambda k, shape, fan: jax.random.normal(k, shape, jnp.float32) / np.sqrt(fan)
        return {'x': jax.random.normal(ks[0], (32, 256, D), jnp.float32), 'gate_w': s(ks[1], (E, D), D), 'up_w': s(ks[2], (E, F, D), D), 'up_b': s(ks[3], (E, F), D), 'gw': s(ks[4], (E, F, D), D), 'gb': s(ks[5], (E, F), D), 'down_w': s(ks[6], (E, D, F), F), 'down_b': s(ks[7], (E, D), F), 'sh_gate_w': s(ks[8], (SH, D), D), 'sh_up_w': s(ks[9], (SH, D), D), 'sh_down_w': s(jax.random.fold_in(key, 11), (D, SH), SH)}
    _L0_ffn_all = _L0_ffn_setup()
    _L0_ffn_in = {k: v for k, v in _L0_ffn_all.items() if k in ('gate_w', 'up_w', 'up_b', 'gw', 'gb', 'down_w', 'down_b', 'sh_gate_w', 'sh_up_w', 'sh_down_w')}
    del _L0_ffn_all
    return {'x': x, 'src': src, 'dst': dst, 'edge_type_8': edge_type_8, 'L0_gnn_weight': _L0_gnn_in['weight'], 'L0_gnn_root': _L0_gnn_in['root'], 'L0_gnn_bias': _L0_gnn_in['bias'], 'L0_gnn_w_gate': _L0_gnn_in['w_gate'], 'L0_gnn_b_gate': _L0_gnn_in['b_gate'], 'L0_ffn_gate_w': _L0_ffn_in['gate_w'], 'L0_ffn_up_w': _L0_ffn_in['up_w'], 'L0_ffn_up_b': _L0_ffn_in['up_b'], 'L0_ffn_gw': _L0_ffn_in['gw'], 'L0_ffn_gb': _L0_ffn_in['gb'], 'L0_ffn_down_w': _L0_ffn_in['down_w'], 'L0_ffn_down_b': _L0_ffn_in['down_b'], 'L0_ffn_sh_gate_w': _L0_ffn_in['sh_gate_w'], 'L0_ffn_sh_up_w': _L0_ffn_in['sh_up_w'], 'L0_ffn_sh_down_w': _L0_ffn_in['sh_down_w']}

def reference(x, src, dst, edge_type_8, L0_gnn_weight, L0_gnn_root, L0_gnn_bias, L0_gnn_w_gate, L0_gnn_b_gate, L0_ffn_gate_w, L0_ffn_up_w, L0_ffn_up_b, L0_ffn_gw, L0_ffn_gb, L0_ffn_down_w, L0_ffn_down_b, L0_ffn_sh_gate_w, L0_ffn_sh_up_w, L0_ffn_sh_down_w):
    import jax
    import jax.numpy as jnp

    def _L0_gnn_ref(x, edge_index, edge_type, weight, root, bias, w_gate, b_gate):
        import jax, jax.numpy as jnp
        import numpy as np
        N, D, R, E = (1250, 1024, 8, 10000)

        def _rgcn(x, edge_index, edge_type, weight, root, bias):
            src, dst = (edge_index[0], edge_index[1])
            msgs = x[src]
            out = x @ root + bias
            n = x.shape[0]
            for r in range(weight.shape[0]):
                mask = (edge_type == r).astype(x.dtype)
                sums = jax.ops.segment_sum(msgs * mask[:, None], dst, num_segments=n)
                cnt = jax.ops.segment_sum(mask, dst, num_segments=n)
                mean = sums / jnp.maximum(cnt, 1.0)[:, None]
                out = out + mean @ weight[r]
            return out
        u = _rgcn(x, edge_index, edge_type, weight, root, bias)
        z = jnp.concatenate([u, x], axis=1) @ w_gate + b_gate
        h = jnp.tanh(u) * z + x * (1.0 - z)
        return h

    def _L0_ffn_ref(x, gate_w, up_w, up_b, gw, gb, down_w, down_b, sh_gate_w, sh_up_w, sh_down_w):
        import jax, jax.numpy as jnp
        import numpy as np
        import math
        E = 16
        TOP_K = 2
        D = 1024
        F = 512
        SH = 256
        B, S, Dm = x.shape
        h = x.reshape(-1, Dm)
        T = h.shape[0]
        scores = jax.nn.sigmoid(h @ gate_w.T)
        cap = math.ceil(T / E * TOP_K)
        topk_score, topk_ids = jax.lax.top_k(scores.T, cap)
        xin = h[topk_ids]
        up = jnp.einsum('ecd,efd->ecf', xin, up_w) + up_b[:, None, :]
        g = jnp.einsum('ecd,efd->ecf', xin, gw) + gb[:, None, :]
        eo = jax.nn.silu(g) * up
        eo = jnp.einsum('ecf,edf->ecd', eo, down_w) + down_b[:, None, :]
        flat = (eo * topk_score[..., None]).reshape(-1, Dm)
        out = jnp.zeros_like(h).at[topk_ids.reshape(-1)].add(flat)
        out = out.reshape(B, S, Dm)
        shared = jax.nn.silu(jnp.einsum('bsd,fd->bsf', x, sh_gate_w)) * jnp.einsum('bsd,fd->bsf', x, sh_up_w)
        shared = jnp.einsum('bsf,df->bsd', shared, sh_down_w)
        return out + shared
    edge_index = jnp.stack([src, dst])
    x = x + _L0_gnn_ref(_layernorm(x, axis=-1), edge_index, edge_type_8, L0_gnn_weight, L0_gnn_root, L0_gnn_bias, L0_gnn_w_gate, L0_gnn_b_gate)
    x = x + _L0_ffn_ref(_layernorm(x, axis=-1)[None], L0_ffn_gate_w, L0_ffn_up_w, L0_ffn_up_b, L0_ffn_gw, L0_ffn_gb, L0_ffn_down_w, L0_ffn_down_b, L0_ffn_sh_gate_w, L0_ffn_sh_up_w, L0_ffn_sh_down_w)[0]
    return x

_drawn_inputs = setup_inputs


def setup_inputs(seed=0):
    import zlib

    import numpy as np

    out = dict(_drawn_inputs(seed))
    spreads = {'L0_gnn_bias': (0.0, 0.1), 'L0_gnn_b_gate': (0.0, 0.1)}
    factors = {'L0_ffn_up_b': 8.0, 'L0_ffn_gb': 7.76, 'L0_ffn_down_b': 3.391}
    for name, (base, spread) in spreads.items():
        noise = np.random.default_rng([zlib.crc32(name.encode()), seed]).standard_normal(out[name].shape)
        drawn = base * np.exp(spread * noise) if base else spread * noise
        out[name] = jnp.asarray(drawn.astype(out[name].dtype))
    for name, factor in factors.items():
        out[name] = (out[name] * factor).astype(out[name].dtype)
    return out
```

```python
import concourse.bass as bass
from concourse import mybir
from contextlib import ExitStack

FP32 = mybir.dt.float32
FP16 = mybir.dt.float16
I32 = mybir.dt.int32
U32 = mybir.dt.uint32
ALU = mybir.AluOpType
ACT = mybir.ActivationFunctionType
AX_X = mybir.AxisListType.X

P = 128
N = 1250
D = 1024
NT = -(-N // P)
NP = NT * P
LAST = N - (NT - 1) * P
KD = D // P
HALF = D // 2
R = 8
E = 20000
EPART = 125
ECOL = E // EPART
GROUP = 2 * P
NG = (E + NT * (GROUP - 1)) // GROUP
ST = 2 * NG
NX = 16
F = 512
KF = F // P
SH = 256
KS = SH // P
CAP = -(-2 * N // NX)
REST = CAP - P
TOP8 = -(-CAP // 8)
EPS = 1e-5
WSC = 64.0
SSC = 1024.0
HALVES = 2 * (R + 3)
M_ROOT, M_GX, M_GU = 2 * R, 2 * R + 2, 2 * R + 4
CW = 2
CPH = KD // CW
COUNT_MAT = 3
MARK = -1.0e30


def build(nc, x, src, dst, etype, wall, bias, b_gate, gate_wT, upT, up_b, gT, gb, downT, down_b,
          sgT, suT, sdT, out):
    ctx = ExitStack()
    with ctx:
        FIXED = 196608
        MEM = ctx.enter_context(nc.sbuf_tensor("mem", [P, (FIXED + 16128) // 2], FP16))

        def at(off, shape, dt, parts=P):
            n = 1
            for s in shape:
                n *= s
            size = 2 if dt == FP16 else 4
            v = MEM[0:parts, off // 2:(off + n * size) // 2]
            if dt != FP16:
                v = v.bitcast(dt)
            if len(shape) == 2:
                v = v.rearrange("p (a b) -> p a b", a=shape[0])
            elif len(shape) == 3:
                v = v.rearrange("p (a b c) -> p a b c", a=shape[0], b=shape[1])
            elif len(shape) == 4:
                v = v.rearrange("p (a b c d) -> p a b c d", a=shape[0], b=shape[1], c=shape[2])
            return v

        XT, ZX, ACC, WB, WST, RING = 0, 40960, 81920, 122880, 155648, 163840
        xT = at(XT, [2, KD, NP], FP16)
        acc = at(ACC, [NT, D], FP32)
        zx = at(ZX, [NT, D], FP32)
        wb = at(WB, [2, 2, KD, HALF], FP16)
        wst = at(WST, [2, CW, HALF], FP32)
        ring = at(RING, [8, 2, D], FP16)
        xin = acc
        xn32 = at(ZX, [2, D], FP32)
        xnp = at(ZX + 8192, [2, 2, D], FP16)
        e_src = at(RING, [ECOL], I32, EPART)
        e_dst = at(RING + 640, [ECOL], I32, EPART)
        e_typ = at(RING + 1280, [ECOL], I32, EPART)
        e_key = at(RING + 1920, [ECOL], I32, EPART)
        e_ones = at(RING + 2560, [ECOL], FP32, EPART)
        e_rec = at(RING + 3200, [ECOL, 4], I32, EPART)
        e_posf = at(RING + 5760, [ECOL], FP32, EPART)
        e_pos = at(RING + 6400, [ECOL], I32, EPART)
        e_lane = at(RING + 7040, [ECOL], I32, EPART)
        e_tile = at(RING + 7680, [ECOL], I32, EPART)
        e_row = at(RING + 8320, [ECOL], I32, EPART)
        e_is = at(RING + 8960, [NT, ECOL], FP32, EPART)
        e_cum = at(RING + 15360, [NT, ECOL], FP32, EPART)
        rec0 = at(RING + 21760, [ST, 4], I32)
        tri = at(RING + 24576, [P], FP16)
        ones16 = at(RING + 24832, [P], FP16)
        tot16 = at(RING + 25088, [16], FP16)
        tot = at(RING + 25120, [4, NT], FP32)
        toti = at(RING + 25280, [NT], I32)
        iota_g = at(RING + 25344, [NG], FP32, 1)
        gmapf = at(RING + 25696, [NG], FP32, 1)
        ones10 = at(RING + 26048, [NT], FP32)
        is_type = at(RING + 26112, [ST, R], FP16)
        cnt = at(RING + 28928, [NT * R], FP32)
        rinv = at(RING + 29248, [NT * R], FP32)
        gw32 = at(RING + 29568, [KD, NX], FP32)
        s_h16 = at(RING + 30080, [ST], FP16)
        up_pair = at(WST, [2, 2, D], FP16)
        uT = at(WST + 8192, [2, 2, KD, P], FP16)
        xt2 = at(WST + 16384, [2, D], FP32)
        xn2 = at(WST + 24576, [2, D], FP32)
        h_pair = at(WST + 32768, [2, 2, D], FP16)
        off = FIXED
        def fixed(shape, dt, parts=P):
            nonlocal off
            v = at(off, shape, dt, parts)
            n = 1
            for s in shape:
                n *= s
            off += (n * (2 if dt == FP16 else 4) + 31) // 32 * 32
            assert off <= FIXED + 16128
            return v
        rec = fixed([ST, 4], I32)
        dloc = fixed([ST], FP32)
        etf = fixed([ST], FP32)
        s_lo = etf
        s_all = fixed([ST], FP32)
        gmap = fixed([NG], I32, 1)
        iota16 = fixed([P], FP16)
        ident = fixed([P], FP16)
        ident32 = fixed([16], FP32, 16)
        stats = fixed([2, 2, 6], FP32)
        mv = fixed([NT, 2], FP32)
        nr_y = fixed([NT], FP32)
        nr_t = fixed([NT], FP32)
        rstd = fixed([NT], FP32)
        nmr = fixed([NT], FP32)
        mv2 = fixed([2], FP32)
        nr2 = fixed([4], FP32)
        ln2 = fixed([2, 2], FP32)
        gw = fixed([2, KD, NX], FP16)
        ub_s = fixed([NX, KF], FP32)
        gb_s = fixed([NX, KF], FP32)
        gbh = fixed([NX, KF], FP32)
        sco_e = fixed([2], FP32)
        SLOTS = off
        stile = fixed([8, 2, P], FP16)
        yst = fixed([2, 2, HALF], FP16)
        bgate = at(SLOTS + 4096, [D], FP32)
        sc = at(SLOTS, [NP], FP32, NX)
        top_v = at(SLOTS + 5120, [TOP8 * 8], FP32, NX)
        top_i = at(SLOTS + 5760, [TOP8 * 8], U32, NX)
        top_f = at(SLOTS + 6400, [2, TOP8 * 8], FP32, NX)
        idx = at(SLOTS + 7680, [2, NX], I32)
        sco = at(SLOTS + 7808, [2, NX], FP32)
        sc_work = at(FIXED, [NP], FP32, NX)
        EW1 = ACC + 2 * 3 * 4096 * 2
        EST = ACC + 2 * 2 * 3 * 4096 * 2
        ew = at(ACC, [2, 2, 3 * 4096], FP16)
        est = at(EST, [2, 2048], FP32)
        sw = at(EW1, [2, 3, 2048], FP16)
        sact = at(EW1 + 24576, [2, KS, NP], FP16)
        s_t = at(EW1 + 34816, [3, 512], FP32)
        smask = at(EW1 + 34816, [2, NP], FP16, NX)
        db = at(EW1 + 40960, [2, D], FP16, NX)
        db32 = at(EW1 + 45056, [D], FP32, NX)
        xg = at(XT, [2, 2, 2, D], FP16)
        xgT = at(XT + 16384, [2, 2, KD, 160], FP16)
        a_pair = at(XT + 26624, [2, 2, KF, 160], FP16)
        a_t = at(XT + 31744, [2, 4, 160], FP32)
        eo = at(ZX, [2, 2, D], FP32)

        PT = [ctx.enter_context(nc.psum_tensor(f"pt{i}", [P, D], FP16))[:, :] for i in range(2)]
        PU = [ctx.enter_context(nc.psum_tensor(f"pu{i}", [P, 512], FP32))[:, :] for i in range(2)]
        PG = [[ctx.enter_context(nc.psum_tensor(f"pg{i}{j}", [P, 512], FP32))[:, :] for j in range(2)] for i in range(2)]

        y_tab = nc.dram_tensor("y_tab", [R * NP, 2 * D], FP16, kind="Internal").ap()
        rec_tab = nc.dram_tensor("rec_tab", [P * ST, 4], I32, kind="Internal").ap()
        rinv_tab = nc.dram_tensor("rinv_tab", [NP * R, 1], FP32, kind="Internal").ap()
        h_tab = nc.dram_tensor("h_tab", [NP, 2 * D], FP16, kind="Internal").ap()

        sem = lambda name: ctx.enter_context(nc.semaphore(name))
        x_in = [sem(f"x_in{t}") for t in range(NT)]
        edges_in = sem("edges_in"); small_in = sem("small_in"); bias_in = sem("bias_in"); bgate_in = sem("bgate_in")
        consts = sem("consts"); dve = sem("dve"); pool_own = sem("pool_own")
        mv_set = sem("mv_set"); ln1_set = sem("ln1_set"); xn_hi = sem("xn_hi"); xn_lo = sem("xn_lo")
        xt_done = sem("xt_done"); xT_hi = sem("xT_hi"); xT_lo = sem("xT_lo"); gw_hi = sem("gw_hi"); gw_lo = sem("gw_lo")
        wst_in = [sem("wst_in0"), sem("wst_in1")]; w_hi = sem("w_hi"); w_lo = sem("w_lo")
        unit_done = sem("unit_done"); y_hi = sem("y_hi"); pu_free = [sem("pu_free0"), sem("pu_free1")]
        y_out = [sem("y_out0"), sem("y_out1")]
        tot_set = sem("tot_set"); prefix_done = sem("prefix_done"); pos_set = sem("pos_set")
        rec0_set = sem("rec0_set"); rec0_out = sem("rec0_out"); rec_out = sem("rec_out"); rec_in = sem("rec_in")
        st_set = sem("st_set"); grp_done = sem("grp_done"); pg_free = [sem("pg_free0"), sem("pg_free1")]
        tables_used = sem("tables_used"); rinv_set = sem("rinv_set"); rinv_out = sem("rinv_out"); s_in = sem("s_in")
        row_in = [sem(f"row_in{b}") for b in range(8)]
        acc_all = sem("acc_all")
        u_hi = sem("u_hi"); u_lo = sem("u_lo"); tu_done = sem("tu_done"); uT_set = sem("uT_set")
        x2_in = [sem("x2_in0"), sem("x2_in1")]; xn_set = sem("xn_set"); tanh_set = sem("tanh_set")
        xx_set = sem("xx_set"); d_set = sem("d_set"); mm_done = sem("mm_done"); z_set = sem("z_set")
        x1_set = sem("x1_set"); h_set = sem("h_set"); h_hi = sem("h_hi"); h_lo = sem("h_lo")
        th_done = sem("th_done"); hT_set = sem("hT_set"); h_out = [sem("h_out0"), sem("h_out1")]
        sc_done = sem("sc_done"); sc_set = sem("sc_set")
        est_in = [sem("est_in0"), sem("est_in1")]; est_hi = sem("est_hi"); est_lo = sem("est_lo")
        db_in = sem("db_in"); db_hi = sem("db_hi"); db_lo = sem("db_lo")
        su_done = sem("su_done"); su_t = sem("su_t"); su_a = sem("su_a"); sa_hi = sem("sa_hi"); sa_lo = sem("sa_lo")
        sd_done = sem("sd_done"); sd_t = sem("sd_t"); sd_set = sem("sd_set")
        top_set = sem("top_set"); topf_i = sem("topf_i"); topf_s = sem("topf_s"); topT_done = sem("topT_done"); idx_set = sem("idx_set")
        sig_set = sem("sig_set"); mask_set = sem("mask_set"); mask_hi = sem("mask_hi"); mask_lo = sem("mask_lo")
        base_done = sem("base_done"); base_set = sem("base_set"); base_out = sem("base_out")
        xg_in = [sem("xg_in0"), sem("xg_in1")]; xgT_done = sem("xgT_done"); xgT_hi = sem("xgT_hi"); xgT_lo = sem("xgT_lo")
        ug_done = sem("ug_done"); ug_free = [sem("ug_free0"), sem("ug_free1")]; at_set = sem("at_set")
        a_set = sem("a_set"); a_hi = sem("a_hi"); a_lo = sem("a_lo")
        dn_done = sem("dn_done"); sco_set = sem("sco_set"); dn_a = sem("dn_a"); dn_d = sem("dn_d"); dve_gate = sem("dve_gate"); a_mid = sem("a_mid"); eo_out = sem("eo_out")

        def wait(eng, s, value):
            if not isinstance(value, int) or value > 0:
                eng.wait_ge(s, value)

        def there(t):
            return not isinstance(t, int) or 0 <= t < NT

        def row(v, t):
            return v[:, t, :] if isinstance(t, int) else v[:, bass.ds(t, 1), :].rearrange("p a n -> p (a n)")

        def cols(v, first, n):
            return v[..., first:first + n] if isinstance(first, int) else v[..., bass.ds(first, n)]

        def chain(eng, s, base=0):
            count = [0]
            def link(ins):
                count[0] += 1
                ins.then_inc(s, 1)
                eng.wait_ge(s, base + count[0])
            link.count = count
            return link


        def steps(eng, body):
            for st in range(-2, NT + 2):
                body(st, st % 2, st // 2)

        def experts(eng, body):
            for e in range(2):
                body(e, e, 0, False)
            with eng.Fori(0, NX // 2 - 2) as i:
                for j in range(2):
                    body(i * 2 + (2 + j), j, i + 1, False)
            for e in range(NX - 2, NX):
                body(e, e % 2, e // 2, e == NX - 1)

        def col(v, i):
            return v[:, i:i + 1] if isinstance(i, int) else v[:, bass.ds(i, 1)]

        def of_expert(v, e, j):
            return v[:, e, j:j + 1] if isinstance(e, int) else \
                v[:, bass.ds(e, 1), j:j + 1].rearrange("p a b -> p (a b)")

        PR = [pu.bitcast(FP16)[:, 0:KD * 32].rearrange("p (k c) -> p k c", k=KD) for pu in PU]
        TQ = NP // 4

        block = ctx.enter_context(nc.Block())

        @block.sync
        def _(sp):
            for v, a in ((e_src, src), (e_dst, dst), (e_typ, etype)):
                sp.dma_start(v, a).then_inc(edges_in, 16)
            for t in range(NT):
                sp.dma_start(xin[:, t, :], x[t * P:(t + 1) * P, :]).then_inc(x_in[t], 16)

            def load_w(mat, h, k0, b):
                rows = bass.ds(k0 * P, CW * P)
                s = wall[mat, rows, h * HALF:(h + 1) * HALF] if isinstance(mat, int) else \
                    wall[bass.ds(mat, 1), rows, h * HALF:(h + 1) * HALF].rearrange("a r n -> (a r) n")
                sp.dma_start(wst[:, b], s.rearrange("(c p) n -> p c n", p=P)).then_inc(wst_in[b], 16)

            for n in range(CPH + 2):
                if n >= 2:
                    sp.wait_ge(w_hi, n - 1)
                    sp.wait_ge(w_lo, n - 1)
                load_w(n // (2 * CPH), n // CPH % 2, n % CPH * CW, n % 2)
            for v, a in ((ub_s, up_b), (gb_s, gb)):
                sp.dma_start(v.rearrange("p a b -> p (a b)"), a).then_inc(small_in, 16)
            sp.dma_start(gw32.rearrange("p a b -> p (a b)"), gate_wT).then_inc(small_in, 16)
            sp.wait_ge(xn_lo, NT)
            sp.wait_ge(xn_hi, NT)
            for t in range(NT):
                sp.dma_start(acc[:, t, :], bias.partition_broadcast(P)).then_inc(bias_in, 16)

            def store_unit(m, h, mat, q, t, j):
                sp.wait_ge(pu_free[j], m * 5 + (q + 2))
                dst_ = y_tab[bass.ds(mat * NP + t * P, P), :].rearrange(
                    "p (a f) -> p a f", a=2)[:, :, h * HALF:(h + 1) * HALF]
                sp.dma_start(dst_, yst[:, j]).then_inc(y_out[j], 16)

            def sp_body(mat, store):
                for h in range(2):
                    m = mat * 2 + h
                    for qq in range(2):
                        for b in range(2):
                            q = qq * 2 + b
                            if store:
                                for j in range(2):
                                    store_unit(m, h, mat, q, q * 2 + j, j)
                            n = (m + 1) * CPH + q
                            if isinstance(n, int) and n + 2 >= HALVES * CPH:
                                continue
                            sp.wait_ge(w_hi, n + 1)
                            sp.wait_ge(w_lo, n + 1)
                            mm, hh = divmod(h + (1 if q < 2 else 2), 2)
                            load_w(mat + mm, hh, (q + 2) % 4 * CW, b)
                    if store:
                        for j in range(2):
                            store_unit(m, h, mat, 4, 8 + j, j)

            with sp.Fori(0, R) as mat:
                sp_body(mat, True)
            sp.wait_ge(y_out[0], 16 * R * 2 * 5)
            sp.wait_ge(y_out[1], 16 * R * 2 * 5)
            sp.dma_start(bgate, b_gate.partition_broadcast(P)).then_inc(bgate_in, 16)
            sp_body(R, False)
            sp_body(R + 1, False)
            for n in range(21 * CPH, HALVES * CPH - 2):
                sp.wait_ge(w_hi, n + 1)
                sp.wait_ge(w_lo, n + 1)
                load_w((n + 2) // (2 * CPH), (n + 2) // CPH % 2, (n + 2) % CPH * CW, n % 2)

            sp.wait_ge(acc_all, 1)
            def step(s, j, half):
                if there(s + 2):
                    t = s + 2
                    wait(sp, x1_set, s + 1)
                    sp.dma_start(xt2[:, j], x[t * P:(t + 1) * P, :] if isinstance(t, int) else x[bass.ds(t * P, P), :]
                                 ).then_inc(x2_in[j], 16)
                if there(s - 1):
                    t = s - 1
                    sp.wait_ge(h_hi, s)
                    sp.wait_ge(h_lo, s)
                    d_ = h_tab[t * P:(t + 1) * P, :] if isinstance(t, int) else h_tab[bass.ds(t * P, P), :]
                    sp.dma_start(d_, h_pair[:, 1 - j].rearrange("p a n -> p (a n)")).then_inc(h_out[1 - j], 16)
            steps(sp, step)

            sp.wait_ge(h_set, NT)
            sp.wait_ge(h_lo, NT)
            sp.wait_ge(h_hi, NT)
            sp.wait_ge(th_done, NT)
            sp.wait_ge(mm_done, NT)
            sp.wait_ge(h_out[0], 16 * NT // 2)
            sp.wait_ge(h_out[1], 16 * NT // 2)
            sp.dma_start(db32, down_b).then_inc(db_in, 16)

            def load(seq, b, w, half):
                if not (isinstance(seq, int) and seq < 2):
                    sp.wait_ge(est_hi, seq - 1)
                    sp.wait_ge(est_lo, seq - 1)
                sp.dma_start(est[:, b], w if half is None else w[:, half * 2048:(half + 1) * 2048]
                             ).then_inc(est_in[b], 16)
            for seq, w in enumerate((sgT, suT, sdT)):
                load(seq, seq % 2, w, None)

            def expert_chunk(e, c):
                w = (upT, gT, downT)[c // 2]
                load(e * 6 + (3 + c), (3 + c) % 2,
                     w[e] if isinstance(e, int) else w[bass.ds(e, 1)].rearrange("a p n -> (a p) n"), c % 2)
            for c in range(6):
                expert_chunk(0, c)
            for t in range(NT):
                rows = min(P, N - t * P)
                sp.wait_ge(base_set, 2 * t + 2)
                sp.dma_start(out[t * P:t * P + rows, :], zx[0:rows, t, :]).then_inc(base_out, 16)
            with sp.Fori(1, NX) as e:
                for c in range(6):
                    expert_chunk(e, c)

        @block.gpsimd
        def _(pool):
            g = nc.gpsimd
            own = chain(pool, pool_own)
            own(g.memset(ident, 0.0))
            own(g.memset(ident32, 0.0))
            own(g.memset(tri, 1.0))
            own(g.affine_select(out=ident, in_=ident, compare_op=ALU.not_equal, fill=1.0, base=0,
                                pattern=[[-1, P]], channel_multiplier=1))
            g.affine_select(out=ident32, in_=ident32, compare_op=ALU.not_equal, fill=1.0, base=0,
                            pattern=[[-1, 16]], channel_multiplier=1).then_inc(consts, 1)
            g.affine_select(out=tri, in_=tri, compare_op=ALU.is_gt, fill=0.0, base=0,
                            pattern=[[1, P]], channel_multiplier=-1).then_inc(consts, 1)
            g.memset(ones16, 1.0).then_inc(consts, 1)
            g.memset(e_ones, 1.0).then_inc(consts, 1)
            g.memset(ones10, 1.0).then_inc(consts, 1)
            g.iota(iota16, pattern=[[1, P]], base=0, channel_multiplier=0,
                   allow_small_or_imprecise_dtypes=True).then_inc(consts, 1)
            g.iota(iota_g, pattern=[[1, NG]], base=0, channel_multiplier=0,
                   allow_small_or_imprecise_dtypes=True).then_inc(consts, 1)
            own(g.memset(rec0, 0))
            g.memset(rec0[:, :, 1:2], -1).then_inc(rec0_set, 1)
            pool.wait_ge(rec0_set, 1)
            pool.dma_start(rec_tab.rearrange("(p t) f -> p (t f)", p=P),
                           rec0.rearrange("p t f -> p (t f)")).then_inc(rec0_out, 16)
            pool.wait_ge(rec0_out, 16)
            pool.wait_ge(pos_set, 1)
            for c in range(ECOL):
                pool.indirect_dma_start(rec_tab, bass.IndirectOffsetOnAxis(e_row[:, c:c + 1], 0),
                                        e_rec[:, c, :], None).then_inc(rec_out, 16)
            pool.wait_ge(rec_out, 16 * ECOL)
            pool.dma_start(rec.rearrange("p t f -> p (t f)"),
                           rec_tab.rearrange("(p t) f -> p (t f)", p=P)).then_inc(rec_in, 16)
            pool.wait_ge(rinv_set, 1)
            pool.dma_start(rinv_tab.rearrange("(d p r) f -> p d (r f)", d=NT, p=P),
                           rinv.rearrange("p (d r) -> p d r", r=R)).then_inc(rinv_out, 16)
            pool.wait_ge(rinv_out, 16)
            for T in range(ST):
                pool.indirect_dma_start(s_all[:, T:T + 1], None, rinv_tab,
                                        bass.IndirectOffsetOnAxis(rec[:, T, 3:4], 0)).then_inc(s_in, 16)
            pool.wait_ge(y_out[0], 16 * R * 2 * 5)
            pool.wait_ge(y_out[1], 16 * R * 2 * 5)
            pool.wait_ge(tables_used, 1)
            for T in range(ST):
                if T >= 8:
                    pool.wait_ge(grp_done, NG + (T - 8) // 2 + 1)
                pool.indirect_dma_start(ring[:, T % 8].rearrange("p a n -> p (a n)"), None, y_tab,
                                        bass.IndirectOffsetOnAxis(rec[:, T, 0:1], 0)).then_inc(row_in[T % 8], 16)

            pool.wait_ge(acc_all, 1)
            def step(s, j, half):
                if there(s + 2):
                    t = s + 2
                    pool.wait_ge(u_hi, s + 3)
                    g.tensor_tensor(out=up_pair[:, j, 1], in0=row(acc, t), in1=up_pair[:, j, 0],
                                    op=ALU.subtract).then_inc(u_lo, 1)
                if there(s + 1):
                    t = s + 1
                    pool.wait_ge(xn_set, s + (NT + 2))
                    g.tensor_tensor(out=xt2[:, 1 - j], in0=xt2[:, 1 - j], in1=xn2[:, 1 - j],
                                    op=ALU.add).then_inc(xx_set, 1)
                    pool.wait_ge(tanh_set, s + 2)
                    g.tensor_tensor(out=row(acc, t), in0=row(acc, t), in1=xn2[:, 1 - j],
                                    op=ALU.subtract).then_inc(d_set, 1)
                if there(s - 1):
                    t = s - 1
                    pool.wait_ge(h_hi, s)
                    g.tensor_tensor(out=h_pair[:, 1 - j, 1], in0=row(acc, t), in1=h_pair[:, 1 - j, 0],
                                    op=ALU.subtract).then_inc(h_lo, 1)
            steps(pool, step)

            def low(seq, dst_):
                pool.wait_ge(est_hi, seq + 1)
                own(g.tensor_scalar(est[:, seq % 2], est[:, seq % 2], WSC, None, ALU.mult))
                g.tensor_tensor(out=dst_[:, 1], in0=est[:, seq % 2], in1=dst_[:, 0], op=ALU.subtract).then_inc(est_lo, 1)
            def sw_at(c):
                return sw[:, :, c, :]
            def ew_at(which, c):
                return ew[:, which, :, c * 2048:(c + 1) * 2048]
            for c in range(3):
                low(c, sw_at(c))
            pool.wait_ge(db_hi, 1)
            own(g.tensor_scalar(db32, db32, WSC, None, ALU.mult))
            g.tensor_tensor(out=db[:, 1], in0=db32, in1=db[:, 0], op=ALU.subtract).then_inc(db_lo, 1)

            def shared_unit(i):
                pool.wait_ge(su_t, 3 * i + 3)
                own(g.tensor_scalar(s_t[:, 0, 0:TQ], s_t[:, 0, 0:TQ], 1.0, None, ALU.add))
                own(g.tensor_tensor(out=s_t[:, 1, 0:TQ], in0=s_t[:, 0, 0:TQ], in1=s_t[:, 1, 0:TQ], op=ALU.mult))
                g.tensor_tensor(out=s_t[:, 1, 0:TQ], in0=s_t[:, 1, 0:TQ], in1=s_t[:, 2, 0:TQ], op=ALU.mult).then_inc(su_a, 1)
                pool.wait_ge(sa_hi, i + 1)
                c, n = divmod(i, NT * P // TQ)
                g.tensor_tensor(out=sact[:, 1, c, n * TQ:(n + 1) * TQ], in0=s_t[:, 1, 0:TQ],
                                in1=sact[:, 0, c, n * TQ:(n + 1) * TQ], op=ALU.subtract).then_inc(sa_lo, 1)
            for i in range(8):
                shared_unit(i)
                if i < 6:
                    low(3 + i, ew_at(0, i))
            for i in range(2 * NT):
                t, h = divmod(i, 2)
                pool.wait_ge(sd_t, i + 1)
                a = zx[:, t, h * HALF:(h + 1) * HALF]
                g.tensor_tensor(out=a, in0=a, in1=s_t[:, i % 2], op=ALU.add).then_inc(sd_set, 1)

            pool.wait_ge(h_out[0], 16 * NT // 2)
            pool.wait_ge(h_out[1], 16 * NT // 2)
            pool.wait_ge(su_done, 8)
            pool.wait_ge(sc_done, NT)
            pool.wait_ge(idx_set, 4)

            def gather(e):
                if e >= 2:
                    pool.wait_ge(xgT_done, e - 1)
                for m, n in ((0, P), (1, REST)):
                    pool.indirect_dma_start(xg[0:n, e % 2, m].rearrange("p a n -> p (a n)"), None, h_tab,
                                            bass.IndirectOffsetOnAxis(idx[0:n, m, e:e + 1], 0)).then_inc(xg_in[e % 2], 16)
            gather(0)
            for e in range(NX):
                if e + 1 < NX:
                    gather(e + 1)
                if e == 0:
                    pool.wait_ge(base_out, 16 * NT)
                else:
                    pool.wait_ge(eo_out, 32 * e)
                pool.wait_ge(dn_a, 2 * e + 2)
                pool.wait_ge(dn_d, 2 * e + 2)
                for m, n in ((0, P), (1, REST)):
                    pool.indirect_dma_start(out, bass.IndirectOffsetOnAxis(idx[0:n, m, e:e + 1], 0),
                                            eo[0:n, e % 2, m], None, compute_op=ALU.add).then_inc(eo_out, 16)
            pool.wait_ge(eo_out, 32 * NX)

        @block.scalar
        def _(act):
            s = nc.scalar
            act.wait_ge(ln1_set, 1)
            for t in range(NT):
                if t >= 2:
                    act.wait_ge(xn_lo, t - 1)
                    act.wait_ge(xt_done, t - 1)
                s.activation(xn32[:, t % 2], xin[:, t, :], ACT.Identity, scale=rstd[:, t:t + 1],
                             bias=nmr[:, t:t + 1]).then_inc(xn_set, 1)
                act.wait_ge(xn_set, t + 1)
                s.activation(xnp[:, t % 2, 0], xn32[:, t % 2], ACT.Copy).then_inc(xn_hi, 1)
                if t >= 1:
                    evac_t = t - 1
                    act.wait_ge(xt_done, evac_t + 1)
                    s.activation(xT[:, 0, :, evac_t * P:(evac_t + 1) * P],
                                 PT[0].rearrange("p (k c) -> p k c", k=KD), ACT.Copy).then_inc(xT_hi, 1)
            act.wait_ge(xt_done, NT)
            s.activation(xT[:, 0, :, (NT - 1) * P:NT * P], PT[0].rearrange("p (k c) -> p k c", k=KD),
                         ACT.Copy).then_inc(xT_hi, 1)

            def split_n(n, ordinal, buf, q, b):
                act.wait_ge(wst_in[b], 16 * (ordinal + 1))
                ks = slice(q * CW, q * CW + CW) if isinstance(q, int) else bass.ds(q * CW, CW)
                s.activation(wb[:, buf, 0, ks, :], wst[:, b], ACT.Copy, scale=WSC).then_inc(w_hi, 1)

            for n in range(CPH):
                split_n(n, n // 2, 0, n, n % 2)

            def body(mat, evac):
                for h in range(2):
                    m = mat * 2 + h
                    def unit(q, j):
                        u = m * 10 + q * 2 + j
                        act.wait_ge(unit_done, u + 1)
                        wait(act, y_out[j], 16 * (m * 5 + q))
                        s.activation(yst[:, j, 0], PU[j], ACT.Copy, scale=1.0 / WSC).then_inc(y_hi, 1)
                    def pair(q, qq, b):
                        if evac:
                            unit(q, 0)
                            unit(q, 1)
                        else:
                            act.wait_ge(unit_done, m * 10 + q * 2 + 2)
                        if b is not None and not (isinstance(m, int) and m + 1 >= HALVES):
                            split_n(None, (m + 1) * 2 + qq, (h + 1) % 2, q, b)
                    if isinstance(m, int) and m == 0:
                        for q in range(CPH):
                            pair(q, q // 2, q % 2)
                    else:
                        with act.Fori(0, 2) as qq:
                            for b in range(2):
                                pair(qq * 2 + b, qq, b)
                    pair(4, 2, None)
            body(0, True)
            with act.Fori(1, R) as mat:
                body(mat, True)
            body(R, False)
            body(R + 1, False)
            act.wait_ge(unit_done, (M_GU) * 10)
            for n in range(21 * CPH, 22 * CPH):
                split_n(n, n // 2, 1, n % CPH, n % 2)

            act.wait_ge(acc_all, 1)
            def step(s_, j, half):
                if there(s_ + 1):
                    act.wait_ge(tu_done, s_ + 2)
                    wait(act, mm_done, s_)
                    for a in range(2):
                        ins = s.activation(uT[:, 1 - j, a], PT[a].rearrange("p (k c) -> p k c", k=KD), ACT.Copy)
                    ins.then_inc(uT_set, 1)
                if there(s_ + 2):
                    wait(act, tu_done, s_ + 1)
                    s.activation(up_pair[:, j, 0], row(acc, s_ + 2), ACT.Copy).then_inc(u_hi, 1)
                if there(s_ + 1):
                    t = s_ + 1
                    act.wait_ge(x2_in[1 - j], (half + (j + 1)) * 16)
                    wait(act, xx_set, s_)
                    wait(act, d_set, s_)
                    s.activation(xn2[:, 1 - j], xt2[:, 1 - j], ACT.Identity, scale=col(rstd, t),
                                 bias=col(nmr, t)).then_inc(xn_set, 1)
                    act.wait_ge(u_lo, s_ + 2)
                    s.activation(row(acc, t), row(acc, t), ACT.Tanh).then_inc(tanh_set, 1)
                if there(s_ - 2):
                    act.wait_ge(th_done, s_ - 1)
                    for a in range(2):
                        ins = s.activation(cols(xT[:, a], (s_ - 2) * P, P), PT[a].rearrange("p (k c) -> p k c", k=KD),
                                           ACT.Copy)
                    ins.then_inc(hT_set, 1)
                if there(s_ - 1):
                    act.wait_ge(h_set, s_)
                    wait(act, th_done, s_ - 2)
                    wait(act, h_out[1 - j], (half + (j - 1)) * 16)
                    s.activation(h_pair[:, 1 - j, 0], row(acc, s_ - 1), ACT.Copy).then_inc(h_hi, 1)
            steps(act, step)

            def high(seq, b, dst_, uses):
                act.wait_ge(est_in[b], uses * 16)
                s.activation(dst_, est[:, b], ACT.Copy, scale=WSC).then_inc(est_hi, 1)
            for c in range(3):
                high(c, c % 2, sw[:, 0, c, :], c // 2 + 1)
            act.wait_ge(db_in, 16)
            s.activation(db[:, 0], db32, ACT.Copy, scale=WSC).then_inc(db_hi, 1)
            for i in range(8):
                act.wait_ge(su_done, i + 1)
                wait(act, sa_lo, i)
                g_, u_ = PG[i % 2]
                s.activation(s_t[:, 0, 0:TQ], g_[:, 0:TQ], ACT.Tanh, scale=0.5 / WSC).then_inc(su_t, 1)
                s.activation(s_t[:, 1, 0:TQ], g_[:, 0:TQ], ACT.Copy, scale=0.5 / WSC).then_inc(su_t, 1)
                s.activation(s_t[:, 2, 0:TQ], u_[:, 0:TQ], ACT.Copy, scale=1.0 / WSC).then_inc(su_t, 1)
                if i < 6:
                    high(3 + i, (3 + i) % 2, ew[:, 0, 0, i * 2048:(i + 1) * 2048], (3 + i) // 2 + 1)
                act.wait_ge(su_a, i + 1)
                c, n = divmod(i, NT * P // TQ)
                s.activation(sact[:, 0, c, n * TQ:(n + 1) * TQ], s_t[:, 1, 0:TQ], ACT.Copy).then_inc(sa_hi, 1)
            act.wait_ge(sa_lo, 8)
            for i in range(2 * NT):
                act.wait_ge(sd_done, i + 1)
                wait(act, sd_set, i - 1)
                s.activation(s_t[:, i % 2], PU[i % 2], ACT.Copy, scale=1.0 / WSC).then_inc(sd_t, 1)
            act.wait_ge(top_set, 1)
            s.activation(top_f[:, 1], top_v, ACT.Tanh, scale=0.5).then_inc(topf_s, 1)
            s.activation(sc[:, 0:N], sc[:, 0:N], ACT.Tanh, scale=0.5).then_inc(sig_set, 1)
            act.wait_ge(mask_set, 1)
            act.wait_ge(sd_t, 2 * NT)
            act.wait_ge(sd_set, 2 * NT)
            s.activation(smask[:, 0], sc_work, ACT.Copy).then_inc(mask_hi, 1)

            def evac_xg(e, par):
                act.wait_ge(xgT_done, e + 1)
                s.activation(xgT[:, par, 0, :, 0:P], PT[0].rearrange("p (k c) -> p k c", k=KD), ACT.Copy)
                s.activation(xgT[:, par, 0, :, P:CAP], PR[0][:, :, 0:REST], ACT.Copy).then_inc(xgT_hi, 1)

            def expert(e, par, half, last):
                def gate_up(j):
                    act.wait_ge(ug_done, e * 4 + (j + 1))
                    wait(act, a_lo, e * 4 + (j - 1))
                    ps = PG[0][j % 2]
                    b_g, b_u = of_expert(gbh, e, j), of_expert(ub_s, e, j)
                    s.activation(a_t[:, j % 2, 0, 0:CAP], ps[:, 160:160 + CAP], ACT.Tanh, scale=0.5 / WSC, bias=b_g)
                    s.activation(a_t[:, j % 2, 1, 0:CAP], ps[:, 160:160 + CAP], ACT.Identity, scale=0.5 / WSC, bias=b_g)
                    s.activation(a_t[:, j % 2, 2, 0:CAP], ps[:, 0:CAP], ACT.Identity, scale=1.0 / WSC,
                                 bias=b_u).then_inc(at_set, 1)
                def a_high(j):
                    act.wait_ge(a_set, e * 4 + (j + 1))
                    s.activation(a_pair[:, par, 0, j, 0:CAP], a_t[:, j % 2, 3, 0:CAP], ACT.Copy).then_inc(a_hi, 1)
                def next_w(c):
                    if last:
                        return
                    if c == 0:
                        wait(act, dn_done, e * 4)
                    high(None, (3 + c) % 2, ew[:, 1 - par, 0, c * 2048:(c + 1) * 2048], (e + 1) * 3 + ((3 + c) // 2 + 1))
                for j in range(4):
                    gate_up(j)
                    next_w(j)
                    a_high(j)
                if not last:
                    evac_xg(e + 1, 1 - par)
                next_w(4)
                s.activation(sco_e[:, par:par + 1], col(sco[:, 0], e), ACT.Copy).then_inc(sco_set, 1)
                next_w(5)
                act.wait_ge(sco_set, e + 1)
                for h in range(2):
                    act.wait_ge(dn_done, e * 4 + (h + 1))
                    wait(act, eo_out, e * 32 - 32)
                    s.activation(eo[:, par, 0, h * HALF:(h + 1) * HALF], PG[1][h], ACT.Copy,
                                 scale=sco_e[:, par:par + 1]).then_inc(dn_a, 1)
            act.wait_ge(idx_set, 4)
            act.wait_ge(base_out, 16 * NT)
            evac_xg(0, 0)
            experts(act, expert)

        @block.tensor
        def _(pe):
            mm = nc.tensor.matmul

            def product(ps, lhs, rhs, ks, first=True, last=True):
                for i, k in enumerate(range(ks)):
                    for a, b in ((0, 0), (0, 1), (1, 0)):
                        ins = mm(ps, lhs(a, k), rhs(b, k), start=first and i == 0 and (a, b) == (0, 0),
                                 stop=last and i == ks - 1 and (a, b) == (1, 0))
                return ins

            pe.wait_ge(consts, 7)
            pe.wait_ge(tot_set, 1)
            mm(PG[0][0][:, 0:NT], tri[0:EPART], tot16[0:EPART, 0:NT], start=True, stop=True)
            mm(PG[0][0][:, 16:16 + NT], ones16[0:EPART], tot16[0:EPART, 0:NT],
               start=True, stop=True).then_inc(prefix_done, 1)
            for t in range(NT):
                pe.wait_ge(xn_hi, t + 1)
                pe.wait_ge(xn_lo, t + 1)
                wait(pe, xT_hi, t)
                wait(pe, xT_lo, t)
                for a in range(2):
                    for k in range(KD):
                        ins = nc.tensor.transpose(PT[a][:, k * P:(k + 1) * P],
                                                  xnp[:, t % 2, a, k * P:(k + 1) * P], ident)
                ins.then_inc(xt_done, 1)
            pe.wait_ge(xT_hi, NT)
            pe.wait_ge(xT_lo, NT)

            def unit(m, h, q, j):
                pe.wait_ge(w_hi, m * CPH + CPH)
                pe.wait_ge(w_lo, m * CPH + CPH)
                pe.wait_ge(pu_free[j], m * 5 + q + 1)
                first = (q * 2 + j) * P
                product(PU[j], lambda a, k: cols(xT[:, a, k, :], first, P),
                        lambda b, k: wb[:, h, b, k, :], KD).then_inc(unit_done, 1)

            def count_group(Q, i, base):
                pe.wait_ge(st_set, Q * 4 + i + 1)
                pe.wait_ge(pg_free[i % 2], Q * 2 + (i // 2 + 1))
                for s in range(2):
                    ins = mm(PG[i % 2][0][:, 0:R], stile[:, i * 2 + s, 0], cols_t(is_type, Q * 8 + i * 2 + s),
                             start=s == 0, stop=s == 1)
                ins.then_inc(grp_done, 1)

            def cols_t(v, T):
                return v[:, T, :] if isinstance(T, int) else v[:, bass.ds(T, 1), :].rearrange("p a n -> p (a n)")

            def sum_group(Q, i, base):
                pe.wait_ge(st_set, Q * 4 + (NG + i + 1))
                pe.wait_ge(pg_free[i % 2], Q * 2 + (NG // 2 + i // 2 + 1))
                for s in range(2):
                    pe.wait_ge(row_in[i * 2 + s], Q * 16 + 16)
                for h in range(2):
                    for s in range(2):
                        b = i * 2 + s
                        for a, c in ((0, 0), (0, 1), (1, 0)):
                            ins = mm(PG[i % 2][h], stile[:, b, a], ring[:, b, c, h * HALF:(h + 1) * HALF],
                                     start=s == 0 and (a, c) == (0, 0), stop=s == 1 and (a, c) == (1, 0))
                ins.then_inc(grp_done, 1)

            def body(mat, group=None, m0=0):
                for h in range(2):
                    m = mat * 2 + h
                    def pair(q):
                        for j in range(2):
                            if group:
                                for i in (2 * j, 2 * j + 1):
                                    group((m - m0) * 5 + q, i, None)
                            unit(m, h, q, j)
                    with pe.Fori(0, 2) as qq:
                        for b in range(2):
                            pair(qq * 2 + b)
                    pair(4)

            def tail(group):
                for Q in (20, 21):
                    for i in range(4):
                        group(Q, i, None)

            with pe.Fori(0, COUNT_MAT) as mat:
                body(mat)
            with pe.Fori(COUNT_MAT, COUNT_MAT + 2) as mat:
                body(mat, count_group, COUNT_MAT * 2)
            tail(count_group)
            with pe.Fori(COUNT_MAT + 2, R) as mat:
                body(mat)
            body(R, sum_group, 2 * R)
            body(R + 1, sum_group, 2 * R)
            tail(sum_group)

            pe.wait_ge(acc_all, 1)
            pe.wait_ge(w_hi, HALVES * CPH)
            pe.wait_ge(w_lo, HALVES * CPH)
            pe.wait_ge(gw_lo, 2)
            def transpose_pair(pair):
                for a in range(2):
                    for k in range(KD):
                        ins = nc.tensor.transpose(PT[a][:, k * P:(k + 1) * P], pair[:, a, k * P:(k + 1) * P], ident)
                return ins
            def step(s, j, half):
                if there(s + 1):
                    pe.wait_ge(u_hi, s + 2)
                    pe.wait_ge(u_lo, s + 2)
                    wait(pe, hT_set, s - 2)
                    transpose_pair(up_pair[:, 1 - j]).then_inc(tu_done, 1)
                def gate_half(h):
                    if h == 0:
                        pe.wait_ge(uT_set, s + 1)
                        wait(pe, z_set, s - 1)
                    return product(PG[j][h], lambda a, k: uT[:, j, a, k, :], lambda b, k: wb[:, h, b, k, :], KD)
                if there(s):
                    gate_half(0)
                if there(s - 2):
                    pe.wait_ge(h_hi, s - 1)
                    pe.wait_ge(h_lo, s - 1)
                    if there(s + 1):
                        pe.wait_ge(uT_set, s + 2)
                    wait(pe, hT_set, s - 2)
                    transpose_pair(h_pair[:, j]).then_inc(th_done, 1)
                if there(s):
                    gate_half(1).then_inc(mm_done, 1)
                if there(s - 2):
                    pe.wait_ge(hT_set, s - 1)
                    wait(pe, sc_set, s - 2)
                    product(PU[0][0:NX, 0:P], lambda a, k: gw[:, a, k, :],
                            lambda b, k: cols(xT[:, b, k, :], (s - 2) * P, P), KD).then_inc(sc_done, 1)
            steps(pe, step)

            pe.wait_ge(est_hi, 2)
            pe.wait_ge(est_lo, 2)
            pe.wait_ge(sc_set, NT)
            for i in range(8):
                c, n = divmod(i, NP // TQ)
                wait(pe, su_t, 3 * (i - 1))
                for w in range(2):
                    ins = product(PG[i % 2][w][:, 0:TQ], lambda a, k: sw[:, a, w, k * SH + c * P:k * SH + (c + 1) * P],
                                  lambda b, k: xT[:, b, k, n * TQ:(n + 1) * TQ], KD)
                ins.then_inc(su_done, 1)
            pe.wait_ge(est_hi, 3)
            pe.wait_ge(est_lo, 3)
            pe.wait_ge(sa_hi, 8)
            pe.wait_ge(sa_lo, 8)
            for i in range(2 * NT):
                t, h = divmod(i, 2)
                wait(pe, sd_t, i - 1)
                product(PU[i % 2], lambda a, k: sact[:, a, k, t * P:(t + 1) * P],
                        lambda b, k: sw[:, b, 2, k * D + h * HALF:k * D + (h + 1) * HALF], KS).then_inc(sd_done, 1)
            pe.wait_ge(topf_i, 1)
            pe.wait_ge(topf_s, 1)
            for w in range(2):
                nc.tensor.transpose(PG[1][0][:, w * 32:w * 32 + NX], top_f[:, w, 0:P], ident32)
                ins = nc.tensor.transpose(PG[1][0][0:REST, w * 32 + NX:w * 32 + 2 * NX], top_f[:, w, P:CAP], ident32)
            ins.then_inc(topT_done, 1)
            pe.wait_ge(db_hi, 1)
            pe.wait_ge(db_lo, 1)
            pe.wait_ge(mask_hi, 1)
            pe.wait_ge(mask_lo, 1)
            pe.wait_ge(sd_t, 2 * NT)
            for i in range(2 * NT):
                t, h = divmod(i, 2)
                wait(pe, base_set, i - 1)
                product(PU[i % 2], lambda a, k: smask[:, a, t * P:(t + 1) * P],
                        lambda b, k: db[:, b, h * HALF:(h + 1) * HALF], 1).then_inc(base_done, 1)

            def transpose_rows(e, par, half):
                pe.wait_ge(xg_in[par], half * 32 + 32)
                wait(pe, xgT_hi, e)
                wait(pe, xgT_lo, e)
                for a in range(2):
                    for k in range(KD):
                        nc.tensor.transpose(PT[a][:, k * P:(k + 1) * P], xg[:, par, 0, a, k * P:(k + 1) * P], ident)
                        ins = nc.tensor.transpose(PR[a][:, k, 0:REST], xg[0:REST, par, 1, a, k * P:(k + 1) * P],
                                                  ident[0:REST, 0:REST])
                ins.then_inc(xgT_done, 1)

            def expert(e, par, half, last):
                pe.wait_ge(xgT_hi, e + 1)
                pe.wait_ge(xgT_lo, e + 1)
                pe.wait_ge(est_hi, e * 6 + 7)
                pe.wait_ge(est_lo, e * 6 + 7)
                for j in range(4):
                    wait(pe, at_set, e * 4 + (j - 1))
                    for w in range(2):
                        ins = product(PG[0][j % 2][:, w * 160:w * 160 + CAP],
                                      lambda a, k: ew[:, par, a, w * 4096 + k * F + j * P:w * 4096 + k * F + (j + 1) * P],
                                      lambda b, k: xgT[:, par, b, k, 0:CAP], KD)
                    ins.then_inc(ug_done, 1)
                if not last:
                    transpose_rows(e + 1, 1 - par, half + par)
                pe.wait_ge(est_hi, e * 6 + 9)
                pe.wait_ge(est_lo, e * 6 + 9)
                pe.wait_ge(a_hi, e * 4 + 4)
                pe.wait_ge(a_lo, e * 4 + 4)
                for m, n in ((0, P), (1, REST)):
                    for h in range(2):
                        if m:
                            pe.wait_ge(dn_a, e * 2 + (h + 1))
                        else:
                            wait(pe, dn_d, e * 2 + (h - 1))
                        product(PG[1][h][0:n], lambda a, k: a_pair[:, par, a, k, m * P:m * P + n],
                                lambda b, k: ew[:, par, b, 8192 + k * D + h * HALF:8192 + k * D + (h + 1) * HALF],
                                KF).then_inc(dn_done, 1)
            pe.wait_ge(base_set, 2 * NT)
            pe.wait_ge(idx_set, 4)
            transpose_rows(0, 0, 0)
            experts(pe, expert)

        @block.vector
        def _(dve_):
            v = nc.vector
            link = chain(dve_, dve)
            for bank in (*pu_free, *pg_free):
                dve_.sem_inc(bank, 1)
            dve_.wait_ge(edges_in, 48)
            dve_.wait_ge(consts, 7)
            v.tensor_single_scalar(e_key, e_dst, 7, op=ALU.arith_shift_right)
            v.tensor_single_scalar(e_lane, e_dst, P - 1, op=ALU.bitwise_and)
            v.scalar_tensor_tensor(out=e_rec[:, :, 0], in0=e_typ, scalar=float(NP), in1=e_src, op0=ALU.mult, op1=ALU.add)
            v.scalar_tensor_tensor(out=e_rec[:, :, 3], in0=e_dst, scalar=float(R), in1=e_typ, op0=ALU.mult, op1=ALU.add)
            link(v.tensor_copy(e_rec[:, :, 2], e_typ))
            v.tensor_copy(e_rec[:, :, 1], e_lane)
            for k in range(NT):
                v.tensor_scalar(e_is[:, k, :], e_key, float(k), None, ALU.is_equal)
            link(v.memset(tot16[:, :], 0.0))
            for k in range(NT):
                last = v.tensor_tensor_scan(e_cum[:, k, :], e_ones, e_is[:, k, :], 0.0, ALU.mult, ALU.add)
            link(last)
            v.tensor_copy(tot16[0:EPART, 0:NT], e_cum[:, :, ECOL - 1]).then_inc(tot_set, 1)
            dve_.wait_ge(prefix_done, 1)
            link(v.tensor_scalar(toti, PG[0][0][:, 16:16 + NT], float(GROUP - 1), None, ALU.add))
            link(v.tensor_single_scalar(toti, toti, 8, op=ALU.arith_shift_right))
            link(v.tensor_copy(tot[:, 0, :], toti))
            link(v.tensor_tensor_scan(tot[:, 1, :], ones10, tot[:, 0, :], 0.0, ALU.mult, ALU.add))
            link(v.tensor_tensor(tot[:, 2, :], tot[:, 1, :], tot[:, 0, :], ALU.subtract))
            link(v.scalar_tensor_tensor(out=tot[:, 3, :], in0=tot[:, 2, :], scalar=float(GROUP),
                                        in1=PG[0][0][:, 0:NT], op0=ALU.mult, op1=ALU.add))
            link(v.tensor_scalar(tot[:, 2, :], tot[:, 3, :], -1.0, None, ALU.add))
            for k in range(NT):
                last = v.scalar_tensor_tensor(out=e_cum[:, k, :], in0=e_cum[:, k, :], scalar=tot[0:EPART, 2, k:k + 1],
                                              in1=e_is[:, k, :], op0=ALU.add, op1=ALU.mult)
            link(last)
            link(v.tensor_reduce(out=e_posf, in_=e_cum.rearrange("p k t -> p t k"), op=ALU.add, axis=AX_X))
            link(v.tensor_copy(e_pos, e_posf))
            v.tensor_single_scalar(e_lane, e_pos, P - 1, op=ALU.bitwise_and)
            link(v.tensor_single_scalar(e_tile, e_pos, 7, op=ALU.arith_shift_right))
            v.scalar_tensor_tensor(out=e_row, in0=e_lane, scalar=float(ST), in1=e_tile,
                                   op0=ALU.mult, op1=ALU.add).then_inc(pos_set, 1)
            link(v.tensor_scalar(gmapf, iota_g, tot[0:1, 1, 0:1], None, ALU.is_ge))
            for k in range(1, NT):
                link(v.scalar_tensor_tensor(out=gmapf, in0=iota_g, scalar=tot[0:1, 1, k:k + 1], in1=gmapf,
                                            op0=ALU.is_ge, op1=ALU.add))
            link(v.tensor_scalar(gmap, gmapf, float(NT - 1), None, ALU.min))

            def newton(link, y, t, ve, var):
                link(v.tensor_scalar(ve, var, EPS, None, ALU.add))
                link(v.tensor_single_scalar(t.bitcast(I32), ve.bitcast(I32), 1, op=ALU.arith_shift_right))
                link(v.tensor_scalar(y.bitcast(I32), t.bitcast(I32), -1.0, float(0x5F3759DF), ALU.mult, ALU.add))
                for _ in range(3):
                    link(v.tensor_tensor(t, y, y, ALU.mult))
                    link(v.scalar_tensor_tensor(out=t, in0=t, scalar=-0.5, in1=ve, op0=ALU.mult, op1=ALU.mult))
                    link(v.scalar_tensor_tensor(out=y, in0=t, scalar=1.5, in1=y, op0=ALU.add, op1=ALU.mult))

            for t in range(NT):
                dve_.wait_ge(x_in[t], 16)
                v.bn_stats(stats[:, t % 2, 0, :], xin[:, t, 0:HALF])
                link(v.bn_stats(stats[:, t % 2, 1, :], xin[:, t, HALF:D]))
                last = v.bn_aggr(mv[:, t, :], stats[:, t % 2].rearrange("p a b -> p (a b)"))
            link(last)
            newton(link, rstd, nr_t, nr_y, mv[:, :, 1])
            v.scalar_tensor_tensor(out=nmr, in0=mv[:, :, 0], scalar=-1.0, in1=rstd,
                                   op0=ALU.mult, op1=ALU.mult).then_inc(ln1_set, 1)
            for t in range(NT):
                dve_.wait_ge(xn_hi, t + 1)
                wait(dve_, xt_done, t - 1)
                v.tensor_tensor(xnp[:, t % 2, 1], xn32[:, t % 2], xnp[:, t % 2, 0], ALU.subtract).then_inc(xn_lo, 1)
                if t >= 1:
                    dve_.wait_ge(xt_done, t)
                    v.tensor_copy(xT[:, 1, :, (t - 1) * P:t * P],
                                  PT[1].rearrange("p (k c) -> p k c", k=KD)).then_inc(xT_lo, 1)
            dve_.wait_ge(xt_done, NT)
            v.tensor_copy(xT[:, 1, :, (NT - 1) * P:NT * P],
                          PT[1].rearrange("p (k c) -> p k c", k=KD)).then_inc(xT_lo, 1)

            def split(m1, buf, q, b, ordinal):
                dve_.wait_ge(w_hi, m1 * CPH + q + 1)
                ks = slice(q * CW, q * CW + CW) if isinstance(q, int) else bass.ds(q * CW, CW)
                v.scalar_tensor_tensor(out=wb[:, buf, 1, ks, :], in0=wst[:, b], scalar=WSC, in1=wb[:, buf, 0, ks, :],
                                       op0=ALU.mult, op1=ALU.subtract).then_inc(w_lo, 1)

            for n in range(CPH):
                split(0, 0, n, n % 2, n // 2)
            dve_.wait_ge(small_in, 48)
            link(v.tensor_scalar(gw[:, 0], gw32, WSC, None, ALU.mult))
            v.scalar_tensor_tensor(out=gw[:, 1], in0=gw32, scalar=WSC, in1=gw[:, 0], op0=ALU.mult, op1=ALU.subtract).then_inc(gw_lo, 1)
            v.tensor_scalar(gbh, gb_s, 0.5, None, ALU.mult).then_inc(gw_lo, 1)

            def count_tiles(Q, i):
                wait(dve_, grp_done, (Q - 1) * 4 + i + 1)
                for s in range(2):
                    ins = v.tensor_scalar(stile[:, i * 2 + s, 0], iota16, col(dloc, Q * 8 + i * 2 + s), None, ALU.is_equal)
                ins.then_inc(st_set, 1)

            def sum_tiles(Q, i):
                if not (isinstance(Q, int) and Q == 0):
                    dve_.wait_ge(grp_done, (Q - 1) * 4 + (NG + i + 1))
                for s in range(2):
                    T = Q * 8 + i * 2 + s
                    v.tensor_scalar(stile[:, i * 2 + s, 0], iota16, col(dloc, T), col(s_all, T), ALU.is_equal, ALU.mult)
                    ins = v.tensor_scalar(stile[:, i * 2 + s, 1], iota16, col(dloc, T), col(s_lo, T), ALU.is_equal, ALU.mult)
                ins.then_inc(st_set, 1)

            def tile_of(Q, i):
                g_ = Q * 4 + i
                return v.value_load(gmap[0:1, g_:g_ + 1] if isinstance(g_, int) else gmap[0:1, bass.ds(g_, 1)],
                                    min_val=0, max_val=NT - 1)

            def count_add(Q, i):
                dve_.wait_ge(grp_done, Q * 4 + i + 1)
                dve_.wait_ge(pg_free[(i - 1) % 2], Q * 2 + ((i + 1) // 2 + 1))
                d = tile_of(Q, i)
                c = cnt[:, bass.ds(d * R, R)]
                v.tensor_tensor(c, PG[i % 2][0][:, 0:R], c, ALU.add).then_inc(pg_free[i % 2], 1)

            def sum_add(Q, i):
                dve_.wait_ge(grp_done, Q * 4 + (NG + i + 1))
                dve_.wait_ge(pg_free[(i - 1) % 2], Q * 2 + (NG // 2 + (i + 1) // 2 + 1))
                d = tile_of(Q, i)
                for h in range(2):
                    a = acc[:, bass.ds(d, 1), h * HALF:(h + 1) * HALF].rearrange("p a n -> p (a n)")
                    ins = v.scalar_tensor_tensor(out=a, in0=PG[i % 2][h], scalar=1.0 / SSC, in1=a, op0=ALU.mult, op1=ALU.add)
                ins.then_inc(pg_free[i % 2], 1)

            def half_row(x_, t, h):
                return row(x_, t)[:, h * HALF:(h + 1) * HALF]

            def body(mat, kind, group=None, tiles=None, m0=0):
                for h in range(2):
                    m = mat * 2 + h
                    def unit(q, j):
                        t = q * 2 + j
                        if kind == "y":
                            dve_.wait_ge(y_hi, m * 10 + t + 1)
                            v.scalar_tensor_tensor(out=yst[:, j, 1], in0=PU[j], scalar=1.0 / WSC, in1=yst[:, j, 0],
                                                   op0=ALU.mult, op1=ALU.subtract).then_inc(pu_free[j], 1)
                        elif kind == "root":
                            dve_.wait_ge(unit_done, m * 10 + t + 1)
                            dve_.wait_ge(pg_free[1], ((m - m0) * 5 + q) * 2 + (NG // 2 + j + 2))
                            a = half_row(acc, t, h)
                            v.scalar_tensor_tensor(out=a, in0=PU[j], scalar=1.0 / WSC, in1=a,
                                                   op0=ALU.mult, op1=ALU.add).then_inc(pu_free[j], 1)
                            dve_.wait_ge(pu_free[j], m * 5 + q + 2)
                        else:
                            dve_.wait_ge(unit_done, m * 10 + t + 1)
                            v.scalar_tensor_tensor(out=half_row(zx, t, h), in0=PU[j], scalar=1.0 / WSC,
                                                   in1=bgate[:, h * HALF:(h + 1) * HALF],
                                                   op0=ALU.mult, op1=ALU.add).then_inc(pu_free[j], 1)
                    def pair(q, qq, b):
                        for j in range(2):
                            if group:
                                for i in (2 * j, 2 * j + 1):
                                    group((m - m0) * 5 + q, i)
                                    tiles((m - m0) * 5 + q + 1, i)
                            unit(q, j)
                        if b is not None and not (isinstance(m, int) and m + 1 >= HALVES):
                            split(m + 1, (h + 1) % 2, q, b, None)
                    with dve_.Fori(0, 2) as qq:
                        for b in range(2):
                            pair(qq * 2 + b, qq, b)
                    pair(4, 2, None)

            def tail(group, tiles):
                for Q in (20, 21):
                    for i in range(4):
                        group(Q, i)
                        if Q == 20:
                            tiles(21, i)

            with dve_.Fori(0, COUNT_MAT) as mat:
                body(mat, "y")
            dve_.wait_ge(rec_in, 16)
            v.memset(cnt, 0.0)
            v.tensor_copy(dloc, rec[:, :, 1])
            link(v.tensor_copy(etf, rec[:, :, 2]))
            for r in range(R):
                last = v.tensor_scalar(is_type[:, :, r], etf, float(r), None, ALU.is_equal)
            link(last)
            for i in range(4):
                count_tiles(0, i)
            with dve_.Fori(COUNT_MAT, COUNT_MAT + 2) as mat:
                body(mat, "y", count_add, count_tiles, COUNT_MAT * 2)
            tail(count_add, count_tiles)
            dve_.wait_ge(pg_free[0], NG // 2 + 1)
            dve_.wait_ge(pg_free[1], NG // 2 + 1)
            link(v.tensor_scalar(cnt, cnt, 1.0, None, ALU.max))
            link(v.reciprocal(rinv, cnt))
            v.tensor_scalar(rinv, rinv, SSC, None, ALU.mult).then_inc(rinv_set, 1)
            with dve_.Fori(COUNT_MAT + 2, R) as mat:
                body(mat, "y")
            dve_.wait_ge(s_in, 16 * ST)
            link(v.tensor_copy(s_h16, s_all))
            link(v.tensor_tensor(s_lo, s_all, s_h16, ALU.subtract))
            v.memset(s_h16, 0.0).then_inc(tables_used, 1)
            dve_.wait_ge(bgate_in, 16)
            dve_.wait_ge(bias_in, 16 * NT)
            for i in range(4):
                sum_tiles(0, i)
            body(R, "root", sum_add, sum_tiles, 2 * R)
            body(R + 1, "gx", sum_add, sum_tiles, 2 * R)
            tail(sum_add, sum_tiles)
            for n in range(21 * CPH, 22 * CPH):
                split(21, 1, n % CPH, n % 2, None)
            dve_.wait_ge(pg_free[0], NG + 1)
            dve_.wait_ge(pg_free[1], NG + 1)
            dve_.wait_ge(w_lo, HALVES * CPH)
            dve_.sem_inc(acc_all, 1)

            GATE_LINKS = 3 + 3 + 9 + 1
            def step(s, j, half):
                if there(s - 2):
                    dve_.wait_ge(sc_done, s - 1)
                    c = cols(sc, (s - 2) * P, P)
                    v.tensor_scalar(c, PU[0][0:NX, 0:P], 1.0 / WSC, 17.0, ALU.mult, ALU.min).then_inc(sc_set, 1)
                if there(s):
                    gate = chain(dve_, dve_gate, s * GATE_LINKS)
                    dve_.wait_ge(mm_done, s + 1)
                    for h in range(2):
                        zh = half_row(zx, s, h)
                        ins = v.scalar_tensor_tensor(out=zh, in0=PG[j][h], scalar=1.0 / WSC, in1=zh,
                                                     op0=ALU.mult, op1=ALU.add)
                    ins.then_inc(z_set, 1)
                    dve_.wait_ge(z_set, s + 1)
                    dve_.wait_ge(d_set, s + 1)
                    gate(v.tensor_tensor(row(acc, s), row(zx, s), row(acc, s), ALU.mult))
                    dve_.wait_ge(xx_set, s + 1)
                    v.tensor_tensor(row(zx, s), row(acc, s), xt2[:, j], ALU.add).then_inc(x1_set, 1)
                    dve_.wait_ge(x1_set, s + 1)
                    for h in range(2):
                        ins = v.bn_stats(stats[:, j, h, :], half_row(zx, s, h))
                    gate(ins)
                    gate(v.bn_aggr(mv2, stats[:, j].rearrange("p a b -> p (a b)")))
                    newton(gate, ln2[:, j, 0:1], nr2[:, 0:1], nr2[:, 1:2], mv2[:, 1:2])
                    gate(v.scalar_tensor_tensor(out=ln2[:, j, 1:2], in0=mv2[:, 0:1], scalar=-1.0, in1=ln2[:, j, 0:1],
                                                op0=ALU.mult, op1=ALU.mult))
                    v.tensor_scalar(row(acc, s), row(zx, s), ln2[:, j, 0:1], ln2[:, j, 1:2],
                                    ALU.mult, ALU.add).then_inc(h_set, 1)
                    assert gate.count[0] == GATE_LINKS
            steps(dve_, step)

            dve_.wait_ge(sc_set, NT)
            link(v.tensor_scalar(sc, sc, -104.0, None, ALU.max))
            for i in range(TOP8):
                src_ = sc if i == 0 else sc_work
                eight = slice(i * 8, i * 8 + 8)
                link(v.max(top_v[:, eight], src_[:, 0:N]))
                link(v.max_index(top_i[:, eight], top_v[:, eight], src_[:, 0:N]))
                if i < TOP8 - 1:
                    link(v.match_replace(sc_work[:, 0:N], top_v[:, eight], src_[:, 0:N], MARK))
            v.memset(top_f[:, 0], 0.0)
            over = TOP8 * 8 - CAP
            v.memset(sc_work[:, N:N + over], -MARK)
            link(v.tensor_copy(top_f[:, 1, 0:8], top_v[:, (TOP8 - 1) * 8:TOP8 * 8]))
            link(v.memset(top_f[:, 1, 8 - over:8], -MARK))
            link(v.match_replace(sc_work[:, 0:N + over], top_f[:, 1, 0:8], sc_work[:, 0:N + over], MARK))
            v.tensor_copy(top_f[:, 0], top_i).then_inc(topf_i, 1)
            link(v.memset(sc_work[:, N:NP], 0.0))
            dve_.sem_inc(top_set, 1)
            dve_.wait_ge(sig_set, 1)
            link(v.tensor_scalar(sc[:, 0:N], sc[:, 0:N], 0.5, 0.5, ALU.mult, ALU.add))
            v.scalar_tensor_tensor(out=sc_work[:, 0:N], in0=sc_work[:, 0:N], scalar=MARK, in1=sc[:, 0:N],
                                   op0=ALU.is_equal, op1=ALU.mult).then_inc(mask_set, 1)
            dve_.wait_ge(topT_done, 1)
            for m, n in ((0, P), (1, REST)):
                v.tensor_copy(idx[0:n, m], PG[1][0][0:n, m * NX:(m + 1) * NX]).then_inc(idx_set, 1)
                v.tensor_scalar(sco[0:n, m], PG[1][0][0:n, 32 + m * NX:32 + (m + 1) * NX], 1.0, 0.5 / WSC,
                                ALU.add, ALU.mult).then_inc(idx_set, 1)
            dve_.wait_ge(mask_hi, 1)
            dve_.wait_ge(mask_set, 1)
            v.tensor_tensor(smask[:, 1], sc_work, smask[:, 0], ALU.subtract).then_inc(mask_lo, 1)
            dve_.wait_ge(sd_set, 2 * NT)
            for i in range(2 * NT):
                dve_.wait_ge(base_done, i + 1)
                a = half_row(zx, i // 2, i % 2)
                v.scalar_tensor_tensor(out=a, in0=PU[i % 2], scalar=1.0 / WSC, in1=a,
                                       op0=ALU.mult, op1=ALU.add).then_inc(base_set, 1)

            def evac_xg(e, par):
                dve_.wait_ge(xgT_done, e + 1)
                v.tensor_copy(xgT[:, par, 1, :, 0:P], PT[1].rearrange("p (k c) -> p k c", k=KD))
                v.tensor_copy(xgT[:, par, 1, :, P:CAP], PR[1][:, :, 0:REST]).then_inc(xgT_lo, 1)

            def expert(e, par, half, last):
                def product_of(j):
                    dve_.wait_ge(at_set, e * 4 + (j + 1))
                    t_ = a_t[:, j % 2]
                    v.scalar_tensor_tensor(out=t_[:, 0, 0:CAP], in0=t_[:, 0, 0:CAP], scalar=1.0, in1=t_[:, 1, 0:CAP],
                                           op0=ALU.add, op1=ALU.mult).then_inc(a_mid, 1)
                    dve_.wait_ge(a_mid, e * 4 + (j + 1))
                    v.tensor_tensor(t_[:, 3, 0:CAP], t_[:, 0, 0:CAP], t_[:, 2, 0:CAP], ALU.mult).then_inc(a_set, 1)
                def a_low(j):
                    dve_.wait_ge(a_hi, e * 4 + (j + 1))
                    v.tensor_tensor(a_pair[:, par, 1, j, 0:CAP], a_t[:, j % 2, 3, 0:CAP], a_pair[:, par, 0, j, 0:CAP],
                                    ALU.subtract).then_inc(a_lo, 1)
                def next_w(c):
                    if last:
                        return
                    dve_.wait_ge(est_hi, e * 6 + (10 + c))
                    w = ew[:, 1 - par, :, c * 2048:(c + 1) * 2048]
                    v.scalar_tensor_tensor(out=w[:, 1], in0=est[:, (3 + c) % 2], scalar=WSC, in1=w[:, 0],
                                           op0=ALU.mult, op1=ALU.subtract).then_inc(est_lo, 1)
                for j in range(4):
                    product_of(j)
                    next_w(j)
                    a_low(j)
                if not last:
                    evac_xg(e + 1, 1 - par)
                next_w(4)
                next_w(5)
                for h in range(2):
                    dve_.wait_ge(dn_done, e * 4 + (h + 3))
                    wait(dve_, eo_out, e * 32 - 32)
                    v.tensor_scalar(eo[0:REST, par, 1, h * HALF:(h + 1) * HALF], PG[1][h][0:REST],
                                    sco[0:REST, 1, e:e + 1] if isinstance(e, int) else sco[0:REST, 1, bass.ds(e, 1)],
                                    None, ALU.mult).then_inc(dn_d, 1)
            dve_.wait_ge(est_lo, 9)
            dve_.wait_ge(base_out, 16 * NT)
            evac_xg(0, 0)
            experts(dve_, expert)



def kernel(**inputs):
    import numpy as np
    import concourse.bacc as bacc
    from concourse.bass_utils import run_bass_kernel_spmd

    f = {k: np.asarray(v) for k, v in inputs.items()}

    def blocks(a, k):
        return np.ascontiguousarray(a.reshape(k, P, -1).transpose(1, 0, 2).reshape(P, -1))

    arrays = {
        "x": np.pad(f["x"], ((0, NP - N), (0, 0))),
        "src": f["src"].reshape(EPART, ECOL),
        "dst": f["dst"].reshape(EPART, ECOL),
        "etype": f["edge_type_8"].reshape(EPART, ECOL),
        "wall": np.concatenate([f["L0_gnn_weight"], f["L0_gnn_root"][None], f["L0_gnn_w_gate"][D:][None],
                                f["L0_gnn_w_gate"][:D][None]]),
        "bias": f["L0_gnn_bias"],
        "b_gate": f["L0_gnn_b_gate"],
        "gate_wT": blocks(f["L0_ffn_gate_w"].T, KD),
        "upT": np.stack([blocks(a.T, KD) for a in f["L0_ffn_up_w"]]),
        "up_b": np.ascontiguousarray(f["L0_ffn_up_b"].reshape(NX, KF, P).transpose(2, 0, 1).reshape(P, -1)),
        "gT": np.stack([blocks(a.T, KD) for a in f["L0_ffn_gw"]]),
        "gb": np.ascontiguousarray(f["L0_ffn_gb"].reshape(NX, KF, P).transpose(2, 0, 1).reshape(P, -1)),
        "downT": np.stack([blocks(a.T, KF) for a in f["L0_ffn_down_w"]]),
        "down_b": f["L0_ffn_down_b"],
        "sgT": blocks(f["L0_ffn_sh_gate_w"].T, KD),
        "suT": blocks(f["L0_ffn_sh_up_w"].T, KD),
        "sdT": blocks(f["L0_ffn_sh_down_w"].T, KS),
    }
    nc = bacc.Bacc("TRN2", target_bir_lowering=False, num_devices=1)
    aps = {n: nc.dram_tensor("in_" + n, a.shape, mybir.dt.from_np(a.dtype), kind="ExternalInput").ap()
           for n, a in arrays.items()}
    out = nc.dram_tensor("out", (N, D), FP32, kind="ExternalOutput").ap()
    build(nc, out=out, **aps)
    r = run_bass_kernel_spmd(nc, [{"in_" + n: a for n, a in arrays.items()}], core_ids=[0])
    return r.results[0]["out"]
```

```python
import concourse.bass as bass
from concourse import mybir
from contextlib import ExitStack

FP32 = mybir.dt.float32
FP16 = mybir.dt.float16
I32 = mybir.dt.int32
U32 = mybir.dt.uint32
ALU = mybir.AluOpType
ACT = mybir.ActivationFunctionType
AX_X = mybir.AxisListType.X

P = 128
N = 1250
D = 1024
NT = -(-N // P)
NP = NT * P
LAST = N - (NT - 1) * P
KD = D // P
HALF = D // 2
R = 8
E = 20000
EPART = 125
ECOL = E // EPART
GROUP = 2 * P
NG = (E + NT * (GROUP - 1)) // GROUP
ST = 2 * NG
NX = 16
F = 512
KF = F // P
SH = 256
KS = SH // P
CAP = -(-2 * N // NX)
REST = CAP - P
TOP8 = -(-CAP // 8)
EPS = 1e-5
WSC = 64.0
SSC = 1024.0
HALVES = 2 * (R + 3)
M_ROOT, M_GX, M_GU = 2 * R, 2 * R + 2, 2 * R + 4
CW = 2
CPH = KD // CW
COUNT_MAT = 3
TQ = NP // 5
SUNITS = KS * (NP // TQ)
MARK = -1.0e30


def build(nc, x, src, dst, etype, wall, bias, b_gate, gate_wT, upT, up_b, gT, gb, downT, down_b,
          sgT, suT, sdT, out):
    ctx = ExitStack()
    with ctx:
        FIXED = 196608
        MEM = ctx.enter_context(nc.sbuf_tensor("mem", [P, (FIXED + 16128) // 2], FP16))

        def at(off, shape, dt, parts=P):
            n = 1
            for s in shape:
                n *= s
            size = 2 if dt == FP16 else 4
            v = MEM[0:parts, off // 2:(off + n * size) // 2]
            if dt != FP16:
                v = v.bitcast(dt)
            if len(shape) == 2:
                v = v.rearrange("p (a b) -> p a b", a=shape[0])
            elif len(shape) == 3:
                v = v.rearrange("p (a b c) -> p a b c", a=shape[0], b=shape[1])
            elif len(shape) == 4:
                v = v.rearrange("p (a b c d) -> p a b c d", a=shape[0], b=shape[1], c=shape[2])
            return v

        XT, ZX, ACC, WB, WST, RING = 0, 40960, 81920, 122880, 155648, 163840
        xT = at(XT, [2, KD, NP], FP16)
        acc = at(ACC, [NT, D], FP32)
        zx = at(ZX, [NT, D], FP32)
        wb = at(WB, [2, 2, KD, HALF], FP16)
        wst = at(WST, [2, CW, HALF], FP32)
        ring = at(RING, [8, 2, D], FP16)
        xin = acc
        xn32 = at(ZX, [2, D], FP32)
        xnp = at(ZX + 8192, [2, 2, D], FP16)
        e_src = at(RING, [ECOL], I32, EPART)
        e_dst = at(RING + 640, [ECOL], I32, EPART)
        e_typ = at(RING + 1280, [ECOL], I32, EPART)
        e_key = at(RING + 1920, [ECOL], I32, EPART)
        e_ones = at(RING + 2560, [ECOL], FP32, EPART)
        e_rec = at(RING + 3200, [ECOL, 4], I32, EPART)
        e_posf = at(RING + 5760, [ECOL], FP32, EPART)
        e_pos = at(RING + 6400, [ECOL], I32, EPART)
        e_lane = at(RING + 7040, [ECOL], I32, EPART)
        e_tile = at(RING + 7680, [ECOL], I32, EPART)
        e_row = at(RING + 8320, [ECOL], I32, EPART)
        e_is = at(RING + 8960, [NT, ECOL], FP32, EPART)
        e_cum = at(RING + 15360, [NT, ECOL], FP32, EPART)
        rec0 = at(RING + 21760, [ST, 4], I32)
        tri = at(RING + 24576, [P], FP16)
        ones16 = at(RING + 24832, [P], FP16)
        tot16 = at(RING + 25088, [16], FP16)
        tot = at(RING + 25120, [4, NT], FP32)
        toti = at(RING + 25280, [NT], I32)
        iota_g = at(RING + 25344, [NG], FP32, 1)
        gmapf = at(RING + 25696, [NG], FP32, 1)
        ones10 = at(RING + 26048, [NT], FP32)
        is_type = at(RING + 26112, [ST, R], FP16)
        cnt = at(RING + 28928, [NT * R], FP32)
        rinv = at(RING + 29248, [NT * R], FP32)
        gw32 = at(RING + 29568, [KD, NX], FP32)
        s_h16 = at(RING + 30080, [ST], FP16)
        s_rec = at(RING + 30432, [ST], FP32)
        up_pair = at(WST, [2, 2, D], FP16)
        uT = at(WST + 8192, [2, 2, KD, P], FP16)
        xt2 = at(WST + 16384, [2, D], FP32)
        xn2 = at(WST + 24576, [2, D], FP32)
        h_pair = at(WST + 32768, [2, 2, D], FP16)
        off = FIXED
        def fixed(shape, dt, parts=P):
            nonlocal off
            v = at(off, shape, dt, parts)
            n = 1
            for s in shape:
                n *= s
            off += (n * (2 if dt == FP16 else 4) + 31) // 32 * 32
            assert off <= FIXED + 16128
            return v
        rec = fixed([ST, 4], I32)
        dloc = fixed([ST], FP32)
        etf = fixed([ST], FP32)
        s_rel = etf
        s_all = fixed([ST], FP32)
        gmap = fixed([NG], I32, 1)
        iota16 = fixed([P], FP16)
        ident = fixed([P], FP16)
        ident32 = fixed([16], FP32, 16)
        stats = fixed([2, 2, 6], FP32)
        mv = fixed([NT, 2], FP32)
        nr_y = fixed([NT], FP32)
        nr_t = fixed([NT], FP32)
        rstd = fixed([NT], FP32)
        nmr = fixed([NT], FP32)
        mv2 = fixed([2], FP32)
        nr2 = fixed([4], FP32)
        ln2 = fixed([2, 2], FP32)
        gw = fixed([2, KD, NX], FP16)
        ub_s = fixed([NX, KF], FP32)
        gb_s = fixed([NX, KF], FP32)
        gbh = fixed([NX, KF], FP32)
        sco_e = fixed([2], FP32)
        rel8 = fixed([2, 8], FP32)
        SLOTS = off
        stile = fixed([8, P], FP16)
        row_t = fixed([2, HALF], FP16)
        yst = fixed([2, 2, HALF], FP16)
        bgate = at(SLOTS + 4096, [D], FP32)
        sc = at(SLOTS, [NP], FP32, NX)
        top_v = at(SLOTS + 5120, [TOP8 * 8], FP32, NX)
        top_i = at(SLOTS + 5760, [TOP8 * 8], U32, NX)
        top_f = at(SLOTS + 6400, [2, TOP8 * 8], FP32, NX)
        idx = at(SLOTS + 7680, [2, NX], I32)
        sco = at(SLOTS + 7808, [2, NX], FP32)
        sc_work = at(FIXED, [NP], FP32, NX)
        EW1 = ACC + 2 * 3 * 4096 * 2
        EST = ACC + 2 * 2 * 3 * 4096 * 2
        ew = at(ACC, [2, 2, 3 * 4096], FP16)
        est = at(EST, [2, 2048], FP32)
        sh_stage = at(ACC, [3, 2048], FP32)
        stage = [est[:, 0], est[:, 1], at(ZX + 16384, [2048], FP32), at(ZX + 24576, [2048], FP32)]
        sw = at(EW1, [2, 3, 2048], FP16)
        sact = at(EW1 + 24576, [2, KS, NP], FP16)
        s_t = at(EW1 + 34816, [2, 3, TQ], FP32)
        sd_b = at(EW1 + 34816, [2, HALF], FP32)
        smask = at(EW1 + 34816, [2, NP], FP16, NX)
        db = at(EW1 + 40960, [2, D], FP16, NX)
        db32 = at(EW1 + 45056, [D], FP32, NX)
        xg = at(XT, [2, 2, 2, D], FP16)
        xgT = at(XT + 16384, [2, 2, KD, 160], FP16)
        a_pair = at(XT + 26624, [2, 2, KF, 160], FP16)
        a_t = at(XT + 31744, [2, 4, 160], FP32)
        eo = at(ZX, [2, 2, D], FP32)

        PT = [ctx.enter_context(nc.psum_tensor(f"pt{i}", [P, D], FP16))[:, :] for i in range(2)]
        PU = [ctx.enter_context(nc.psum_tensor(f"pu{i}", [P, 512], FP32))[:, :] for i in range(2)]
        PG = [[ctx.enter_context(nc.psum_tensor(f"pg{i}{j}", [P, 512], FP32))[:, :] for j in range(2)] for i in range(2)]

        y_tab = nc.dram_tensor("y_tab", [R * NP, 2 * D], FP16, kind="Internal").ap()
        rec_tab = nc.dram_tensor("rec_tab", [P * ST, 4], I32, kind="Internal").ap()
        rinv_tab = nc.dram_tensor("rinv_tab", [NP * R, 1], FP32, kind="Internal").ap()
        h_tab = nc.dram_tensor("h_tab", [NP, 2 * D], FP16, kind="Internal").ap()

        sem = lambda name: ctx.enter_context(nc.semaphore(name))
        x_in = [sem(f"x_in{t}") for t in range(NT)]
        edges_in = sem("edges_in"); small_in = sem("small_in"); bias_in = sem("bias_in"); bgate_in = sem("bgate_in")
        consts = sem("consts"); dve = sem("dve"); pool_own = sem("pool_own")
        mv_set = sem("mv_set"); ln1_set = sem("ln1_set"); xn_hi = sem("xn_hi"); xn_lo = sem("xn_lo")
        xt_done = sem("xt_done"); xT_hi = sem("xT_hi"); xT_lo = sem("xT_lo"); gw_hi = sem("gw_hi"); gw_lo = sem("gw_lo")
        wst_in = [sem("wst_in0"), sem("wst_in1")]; w_hi = sem("w_hi"); w_lo = sem("w_lo")
        unit_done = sem("unit_done"); y_hi = sem("y_hi"); pu_free = [sem("pu_free0"), sem("pu_free1")]
        y_out = [sem("y_out0"), sem("y_out1")]
        tot_set = sem("tot_set"); prefix_done = sem("prefix_done"); pos_set = sem("pos_set")
        rec0_set = sem("rec0_set"); rec0_out = sem("rec0_out"); rec_out = sem("rec_out"); rec_in = sem("rec_in")
        st_set = sem("st_set"); grp_done = sem("grp_done"); pg_free = [sem("pg_free0"), sem("pg_free1")]
        tables_used = sem("tables_used"); rinv_set = sem("rinv_set"); rinv_out = sem("rinv_out"); s_in = sem("s_in")
        rel8_set = sem("rel8_set"); row_scaled = sem("row_scaled"); row_set = sem("row_set")
        row_in = [sem(f"row_in{b}") for b in range(8)]
        acc_all = sem("acc_all")
        u_hi = sem("u_hi"); u_lo = sem("u_lo"); tu_done = sem("tu_done"); uT_set = sem("uT_set")
        x2_in = [sem("x2_in0"), sem("x2_in1")]; xn_set = sem("xn_set"); tanh_set = sem("tanh_set")
        xx_set = sem("xx_set"); d_set = sem("d_set"); mm_done = sem("mm_done"); z_set = sem("z_set")
        x1_set = sem("x1_set"); h_set = sem("h_set"); h_hi = sem("h_hi"); h_lo = sem("h_lo")
        th_done = sem("th_done"); hT_set = sem("hT_set"); h_out = [sem("h_out0"), sem("h_out1")]
        sc_done = sem("sc_done"); sc_set = sem("sc_set")
        est_in = [sem("est_in0"), sem("est_in1")]; sh_in = sem("sh_in"); stage_in = [sem(f"stage_in{b}") for b in range(4)]; est_hi = sem("est_hi"); est_lo = sem("est_lo")
        db_in = sem("db_in"); db_hi = sem("db_hi"); db_lo = sem("db_lo")
        su_done = sem("su_done"); su_t = sem("su_t"); su_a = sem("su_a"); su_p = sem("su_p"); est_sc = sem("est_sc"); db_sc = sem("db_sc"); sc_used = sem("sc_used"); tanh_sc = sem("tanh_sc"); sa_hi = sem("sa_hi"); sa_lo = sem("sa_lo")
        sd_done = sem("sd_done"); sd_t = sem("sd_t"); sd_set = sem("sd_set")
        top_set = sem("top_set"); topf_i = sem("topf_i"); topf_s = sem("topf_s"); topT_done = sem("topT_done"); idx_set = sem("idx_set")
        sig_set = sem("sig_set"); mask_set = sem("mask_set"); mask_hi = sem("mask_hi"); mask_lo = sem("mask_lo")
        base_done = sem("base_done"); base_set = sem("base_set"); base_out = sem("base_out")
        xg_in = [sem("xg_in0"), sem("xg_in1")]; xgT_done = sem("xgT_done"); xgT_hi = sem("xgT_hi"); xgT_lo = sem("xgT_lo")
        ug_done = sem("ug_done"); ug_free = [sem("ug_free0"), sem("ug_free1")]; at_set = sem("at_set")
        a_set = sem("a_set"); a_hi = sem("a_hi"); a_lo = sem("a_lo")
        dn_done = sem("dn_done"); sco_set = sem("sco_set"); dn_a = sem("dn_a"); dn_d = sem("dn_d"); dve_gate = sem("dve_gate"); a_mid = sem("a_mid"); eo_out = sem("eo_out")

        def wait(eng, s, value):
            if not isinstance(value, int) or value > 0:
                eng.wait_ge(s, value)

        def there(t):
            return not isinstance(t, int) or 0 <= t < NT

        def row(v, t):
            return v[:, t, :] if isinstance(t, int) else v[:, bass.ds(t, 1), :].rearrange("p a n -> p (a n)")

        def cols(v, first, n):
            return v[..., first:first + n] if isinstance(first, int) else v[..., bass.ds(first, n)]

        def chain(eng, s, base=0):
            count = [0]
            def link(ins):
                count[0] += 1
                ins.then_inc(s, 1)
                eng.wait_ge(s, base + count[0])
            link.count = count
            return link


        def steps(eng, body, first=-2, end=NT + 2):
            for st in range(first, end):
                body(st, st % 2, st // 2)

        def experts(eng, body):
            for e in range(2):
                body(e, e, 0, False)
            with eng.Fori(0, NX // 2 - 2) as i:
                for j in range(2):
                    body(i * 2 + (2 + j), j, i + 1, False)
            for e in range(NX - 2, NX):
                body(e, e % 2, e // 2, e == NX - 1)

        def col(v, i):
            return v[:, i:i + 1] if isinstance(i, int) else v[:, bass.ds(i, 1)]

        def of_expert(v, e, j):
            return v[:, e, j:j + 1] if isinstance(e, int) else \
                v[:, bass.ds(e, 1), j:j + 1].rearrange("p a b -> p (a b)")

        PR = [pu.bitcast(FP16)[:, 0:KD * 32].rearrange("p (k c) -> p k c", k=KD) for pu in PU]

        block = ctx.enter_context(nc.Block())

        @block.sync
        def _(sp):
            def load_x(t):
                sp.dma_start(xin[:, t, :], x[t * P:(t + 1) * P, :]).then_inc(x_in[t], 16)

            def load_w(mat, h, k0, b):
                rows = bass.ds(k0 * P, CW * P)
                s = wall[mat, rows, h * HALF:(h + 1) * HALF] if isinstance(mat, int) else \
                    wall[bass.ds(mat, 1), rows, h * HALF:(h + 1) * HALF].rearrange("a r n -> (a r) n")
                sp.dma_start(wst[:, b], s.rearrange("(c p) n -> p c n", p=P)).then_inc(wst_in[b], 16)

            def first_w(n):
                if n >= 2:
                    sp.wait_ge(w_hi, n - 1)
                    sp.wait_ge(w_lo, n - 1)
                load_w(n // (2 * CPH), n // CPH % 2, n % CPH * CW, n % 2)

            for t in range(3):
                load_x(t)
            for n in range(2):
                first_w(n)
            for t in range(3, 6):
                load_x(t)
            for n in range(2, CPH):
                first_w(n)
                load_x(n + 4)
            for t in range(CPH + 4, NT):
                load_x(t)
            for v, a in ((e_src, src), (e_dst, dst), (e_typ, etype)):
                sp.dma_start(v, a).then_inc(edges_in, 16)
            for n in range(CPH, CPH + 2):
                first_w(n)
            for v, a in ((ub_s, up_b), (gb_s, gb)):
                sp.dma_start(v.rearrange("p a b -> p (a b)"), a).then_inc(small_in, 16)
            sp.dma_start(gw32.rearrange("p a b -> p (a b)"), gate_wT).then_inc(small_in, 16)
            def store_unit(m, h, mat, q, t, j):
                sp.wait_ge(pu_free[j], m * 5 + (q + 2))
                dst_ = y_tab[bass.ds(mat * NP + t * P, P), :].rearrange(
                    "p (a f) -> p a f", a=2)[:, :, h * HALF:(h + 1) * HALF]
                sp.dma_start(dst_, yst[:, j]).then_inc(y_out[j], 16)

            def sp_body(mat, store):
                for h in range(2):
                    m = mat * 2 + h
                    for qq in range(2):
                        for b in range(2):
                            q = qq * 2 + b
                            if store:
                                for j in range(2):
                                    store_unit(m, h, mat, q, q * 2 + j, j)
                            n = (m + 1) * CPH + q
                            if isinstance(n, int) and n + 2 >= HALVES * CPH:
                                continue
                            sp.wait_ge(w_hi, n + 1)
                            sp.wait_ge(w_lo, n + 1)
                            mm, hh = divmod(h + (1 if q < 2 else 2), 2)
                            load_w(mat + mm, hh, (q + 2) % 4 * CW, b)
                    if store:
                        for j in range(2):
                            store_unit(m, h, mat, 4, 8 + j, j)

            sp_body(0, True)
            sp.wait_ge(xn_lo, NT)
            sp.wait_ge(xn_hi, NT)
            for t in range(NT):
                sp.dma_start(acc[:, t, :], bias.partition_broadcast(P)).then_inc(bias_in, 16)
            with sp.Fori(1, R) as mat:
                sp_body(mat, True)
            sp.wait_ge(y_out[0], 16 * R * 2 * 5)
            sp.wait_ge(y_out[1], 16 * R * 2 * 5)
            sp.dma_start(bgate, b_gate.partition_broadcast(P)).then_inc(bgate_in, 16)
            sp_body(R, False)
            sp_body(R + 1, False)
            for n in range(21 * CPH, HALVES * CPH - 2):
                sp.wait_ge(w_hi, n + 1)
                sp.wait_ge(w_lo, n + 1)
                load_w((n + 2) // (2 * CPH), (n + 2) // CPH % 2, (n + 2) % CPH * CW, n % 2)

            sp.wait_ge(acc_all, 1)
            def step(s, j, half):
                if there(s + 2):
                    t = s + 2
                    wait(sp, x1_set, s + 1)
                    sp.dma_start(xt2[:, j], x[t * P:(t + 1) * P, :] if isinstance(t, int) else x[bass.ds(t * P, P), :]
                                 ).then_inc(x2_in[j], 16)
                if there(s - 1):
                    t = s - 1
                    sp.wait_ge(h_hi, s)
                    sp.wait_ge(h_lo, s)
                    d_ = h_tab[t * P:(t + 1) * P, :] if isinstance(t, int) else h_tab[bass.ds(t * P, P), :]
                    sp.dma_start(d_, h_pair[:, 1 - j].rearrange("p a n -> p (a n)")).then_inc(h_out[1 - j], 16)
            steps(sp, step, -2, NT - 1)
            for c, w in enumerate((sgT, suT, sdT)):
                sp.dma_start(sh_stage[:, c], w).then_inc(sh_in, 16)
            steps(sp, step, NT - 1)

            sp.wait_ge(h_set, NT)
            sp.wait_ge(h_lo, NT)
            sp.wait_ge(h_hi, NT)
            sp.wait_ge(th_done, NT)
            sp.wait_ge(mm_done, NT)
            sp.wait_ge(h_out[0], 16 * NT // 2)
            sp.wait_ge(h_out[1], 16 * NT // 2)
            sp.dma_start(db32, down_b).then_inc(db_in, 16)

            for c in range(6):
                if c >= 2:
                    sp.wait_ge(est_hi, c + 2)
                    sp.wait_ge(est_lo, c + 2)
                w = (upT, gT, downT)[c // 2]
                sp.dma_start(est[:, c % 2], w[0, :, c % 2 * 2048:(c % 2 + 1) * 2048]).then_inc(est_in[c % 2], 16)
            for t in range(NT):
                rows = min(P, N - t * P)
                sp.wait_ge(base_set, 2 * t + 2)
                sp.dma_start(out[t * P:t * P + rows, :], zx[0:rows, t, :]).then_inc(base_out, 16)
            def expert_chunks(e, par):
                for c in range(6):
                    if not (isinstance(e, int) and c < 4):
                        sp.wait_ge(est_hi, e * 6 + c)
                        sp.wait_ge(est_lo, e * 6 + c)
                    w = (upT, gT, downT)[c // 2]
                    w = w[e] if isinstance(e, int) else w[bass.ds(e, 1)].rearrange("a p n -> (a p) n")
                    b = (c + 2 * (1 - par)) % 4
                    sp.dma_start(stage[b], w[:, c % 2 * 2048:(c % 2 + 1) * 2048]).then_inc(stage_in[b], 16)
            sp.wait_ge(est_hi, 9)
            sp.wait_ge(est_lo, 9)
            sp.wait_ge(base_out, 16 * NT)
            expert_chunks(1, 1)
            with sp.Fori(1, NX // 2) as i:
                for j in range(2):
                    expert_chunks(i * 2 + j, j)

        @block.gpsimd
        def _(pool):
            g = nc.gpsimd
            own = chain(pool, pool_own)
            own(g.memset(ident, 0.0))
            own(g.memset(ident32, 0.0))
            own(g.memset(tri, 1.0))
            own(g.affine_select(out=ident, in_=ident, compare_op=ALU.not_equal, fill=1.0, base=0,
                                pattern=[[-1, P]], channel_multiplier=1))
            g.affine_select(out=ident32, in_=ident32, compare_op=ALU.not_equal, fill=1.0, base=0,
                            pattern=[[-1, 16]], channel_multiplier=1).then_inc(consts, 1)
            g.affine_select(out=tri, in_=tri, compare_op=ALU.is_gt, fill=0.0, base=0,
                            pattern=[[1, P]], channel_multiplier=-1).then_inc(consts, 1)
            g.memset(ones16, 1.0).then_inc(consts, 1)
            g.memset(e_ones, 1.0).then_inc(consts, 1)
            g.memset(ones10, 1.0).then_inc(consts, 1)
            g.iota(iota16, pattern=[[1, P]], base=0, channel_multiplier=0,
                   allow_small_or_imprecise_dtypes=True).then_inc(consts, 1)
            g.iota(iota_g, pattern=[[1, NG]], base=0, channel_multiplier=0,
                   allow_small_or_imprecise_dtypes=True).then_inc(consts, 1)
            own(g.memset(rec0, 0))
            g.memset(rec0[:, :, 1:2], -1).then_inc(rec0_set, 1)
            pool.wait_ge(rec0_set, 1)
            pool.dma_start(rec_tab.rearrange("(p t) f -> p (t f)", p=P),
                           rec0.rearrange("p t f -> p (t f)")).then_inc(rec0_out, 16)
            pool.wait_ge(rec0_out, 16)
            pool.wait_ge(pos_set, 1)
            for c in range(ECOL):
                pool.indirect_dma_start(rec_tab, bass.IndirectOffsetOnAxis(e_row[:, c:c + 1], 0),
                                        e_rec[:, c, :], None).then_inc(rec_out, 16)
            pool.wait_ge(rec_out, 16 * ECOL)
            pool.dma_start(rec.rearrange("p t f -> p (t f)"),
                           rec_tab.rearrange("(p t) f -> p (t f)", p=P)).then_inc(rec_in, 16)
            pool.wait_ge(rinv_set, 1)
            pool.dma_start(rinv_tab.rearrange("(d p r) f -> p d (r f)", d=NT, p=P),
                           rinv.rearrange("p (d r) -> p d r", r=R)).then_inc(rinv_out, 16)
            pool.wait_ge(rinv_out, 16)
            for T in range(ST):
                pool.indirect_dma_start(s_all[:, T:T + 1], None, rinv_tab,
                                        bass.IndirectOffsetOnAxis(rec[:, T, 3:4], 0)).then_inc(s_in, 16)
            pool.wait_ge(y_out[0], 16 * R * 2 * 5)
            pool.wait_ge(y_out[1], 16 * R * 2 * 5)
            pool.wait_ge(tables_used, 1)
            for T in range(ST):
                if T >= 8:
                    pool.wait_ge(grp_done, NG + (T - 8) // 2 + 1)
                pool.indirect_dma_start(ring[:, T % 8].rearrange("p a n -> p (a n)"), None, y_tab,
                                        bass.IndirectOffsetOnAxis(rec[:, T, 0:1], 0)).then_inc(row_in[T % 8], 16)

            pool.wait_ge(acc_all, 1)
            def step(s, j, half):
                if there(s + 2):
                    t = s + 2
                    pool.wait_ge(u_hi, s + 3)
                    g.tensor_tensor(out=up_pair[:, j, 1], in0=row(acc, t), in1=up_pair[:, j, 0],
                                    op=ALU.subtract).then_inc(u_lo, 1)
                if there(s + 1):
                    t = s + 1
                    pool.wait_ge(xn_set, s + (NT + 2))
                    g.tensor_tensor(out=xt2[:, 1 - j], in0=xt2[:, 1 - j], in1=xn2[:, 1 - j],
                                    op=ALU.add).then_inc(xx_set, 1)
                    pool.wait_ge(tanh_set, s + 2)
                    g.tensor_tensor(out=row(acc, t), in0=row(acc, t), in1=xn2[:, 1 - j],
                                    op=ALU.subtract).then_inc(d_set, 1)
                if there(s - 1):
                    t = s - 1
                    pool.wait_ge(h_hi, s)
                    g.tensor_tensor(out=h_pair[:, 1 - j, 1], in0=row(acc, t), in1=h_pair[:, 1 - j, 0],
                                    op=ALU.subtract).then_inc(h_lo, 1)
            steps(pool, step)

            def low(c):
                pool.wait_ge(est_hi, c + 4)
                w = ew[:, 0, :, c * 2048:(c + 1) * 2048]
                g.tensor_tensor(out=w[:, 1], in0=est[:, c % 2], in1=w[:, 0], op=ALU.subtract).then_inc(est_lo, 1)
            pool.wait_ge(db_hi, 1)
            g.tensor_tensor(out=db[:, 1], in0=db32, in1=db[:, 0], op=ALU.subtract).then_inc(db_lo, 1)

            def shared_unit(i):
                pool.wait_ge(su_t, 3 * i + 3)
                pool.wait_ge(su_p, i + 1)
                t_ = s_t[:, i % 2]
                own(g.tensor_tensor(out=t_[:, 1], in0=t_[:, 0], in1=t_[:, 1], op=ALU.mult))
                g.tensor_tensor(out=t_[:, 1], in0=t_[:, 1], in1=t_[:, 2], op=ALU.mult).then_inc(su_a, 1)
                pool.wait_ge(sa_hi, i + 1)
                c, n = divmod(i, NP // TQ)
                g.tensor_tensor(out=sact[:, 1, c, n * TQ:(n + 1) * TQ], in0=t_[:, 1],
                                in1=sact[:, 0, c, n * TQ:(n + 1) * TQ], op=ALU.subtract).then_inc(sa_lo, 1)
            for i in range(SUNITS):
                shared_unit(i)
                if i < 6:
                    low(i)
            for i in range(2 * NT):
                t, h = divmod(i, 2)
                pool.wait_ge(sd_t, i + 1)
                a = zx[:, t, h * HALF:(h + 1) * HALF]
                g.tensor_tensor(out=a, in0=a, in1=sd_b[:, i % 2], op=ALU.add).then_inc(sd_set, 1)

            pool.wait_ge(h_out[0], 16 * NT // 2)
            pool.wait_ge(h_out[1], 16 * NT // 2)
            pool.wait_ge(su_done, SUNITS)
            pool.wait_ge(sc_done, NT)
            pool.wait_ge(idx_set, 4)

            def gather(e):
                if e >= 2:
                    pool.wait_ge(xgT_done, e - 1)
                for m, n in ((0, P), (1, REST)):
                    pool.indirect_dma_start(xg[0:n, e % 2, m].rearrange("p a n -> p (a n)"), None, h_tab,
                                            bass.IndirectOffsetOnAxis(idx[0:n, m, e:e + 1], 0)).then_inc(xg_in[e % 2], 16)
            gather(0)
            for e in range(NX):
                if e + 1 < NX:
                    gather(e + 1)
                if e == 0:
                    pool.wait_ge(base_out, 16 * NT)
                else:
                    pool.wait_ge(eo_out, 32 * e)
                pool.wait_ge(dn_a, 2 * e + 2)
                pool.wait_ge(dn_d, 2 * e + 2)
                for m, n in ((0, P), (1, REST)):
                    pool.indirect_dma_start(out, bass.IndirectOffsetOnAxis(idx[0:n, m, e:e + 1], 0),
                                            eo[0:n, e % 2, m], None, compute_op=ALU.add).then_inc(eo_out, 16)
            pool.wait_ge(eo_out, 32 * NX)

        @block.scalar
        def _(act):
            s = nc.scalar
            def split_n(n, ordinal, buf, q, b):
                act.wait_ge(wst_in[b], 16 * (ordinal + 1))
                ks = slice(q * CW, q * CW + CW) if isinstance(q, int) else bass.ds(q * CW, CW)
                s.activation(wb[:, buf, 0, ks, :], wst[:, b], ACT.Copy, scale=WSC).then_inc(w_hi, 1)

            def norm(t):
                if t % 2 == 0:
                    act.wait_ge(ln1_set, t // 2 + 1)
                wait(act, xn_lo, t - 1)
                wait(act, xt_done, t - 1)
                s.activation(xn32[:, t % 2], xin[:, t, :], ACT.Identity, scale=rstd[:, t:t + 1],
                             bias=nmr[:, t:t + 1]).then_inc(xn_set, 1)
                act.wait_ge(xn_set, t + 1)
                s.activation(xnp[:, t % 2, 0], xn32[:, t % 2], ACT.Copy).then_inc(xn_hi, 1)

            def evac_xT(t):
                act.wait_ge(xt_done, t + 1)
                s.activation(xT[:, 0, :, t * P:(t + 1) * P], PT[0].rearrange("p (k c) -> p k c", k=KD),
                             ACT.Copy).then_inc(xT_hi, 1)

            def evac_y(m, q, j):
                u = m * 10 + q * 2 + j
                act.wait_ge(unit_done, u + 1)
                wait(act, y_out[j], 16 * (m * 5 + q))
                s.activation(yst[:, j, 0], PU[j], ACT.Copy, scale=1.0 / WSC).then_inc(y_hi, 1)

            norm(0)
            for n in range(2):
                split_n(n, n // 2, 0, n, n % 2)
            norm(1)
            evac_xT(0)
            for n in range(2, CPH):
                split_n(n, n // 2, 0, n, n % 2)
            evac_xT(1)
            norm(2)
            for t in range(2, NT + 2):
                u = t - 2
                evac_y(0, u // 2, u % 2)
                if t < NT:
                    evac_xT(t)
                if t + 1 < NT:
                    norm(t + 1)
                if t % 2 and u // 2 < CPH:
                    split_n(None, 2 + u // 4, 1, u // 2, u // 2 % 2)

            def rel_columns(Q, par):
                v_ = s_rel[:, Q * 8:Q * 8 + 8] if isinstance(Q, int) else s_rel[:, bass.ds(Q * 8, 8)]
                s.activation(rel8[:, par], v_, ACT.Copy).then_inc(rel8_set, 1)

            def scale_rows(Q, par, i):
                act.wait_ge(rel8_set, Q + 1)
                for st in range(2):
                    b = i * 2 + st
                    act.wait_ge(row_in[b], Q * 16 + 16)
                    for h in range(2):
                        act.wait_ge(row_set, Q * 16 + (b * 2 + h + 1))
                        s.activation(row_t[:, h], ring[:, b, 0, h * HALF:(h + 1) * HALF], ACT.Copy,
                                     scale=rel8[:, par, b:b + 1]).then_inc(row_scaled, 1)

            def body(mat, evac, halves=(0, 1)):
                for h in halves:
                    m = mat * 2 + h
                    def pair(q, qq, b):
                        if evac:
                            evac_y(m, q, 0)
                            evac_y(m, q, 1)
                        else:
                            Q = (m - 2 * R) * 5 + q
                            par = (h + (b or 0)) % 2
                            scale_rows(Q, par, 2)
                            scale_rows(Q, par, 3)
                            rel_columns(Q + 1, 1 - par)
                            act.wait_ge(unit_done, m * 10 + q * 2 + 1)
                        if b is not None and not (isinstance(m, int) and m + 1 >= HALVES):
                            split_n(None, (m + 1) * 2 + qq, (h + 1) % 2, q, b)
                        if not evac:
                            scale_rows(Q + 1, 1 - par, 0)
                            scale_rows(Q + 1, 1 - par, 1)
                    with act.Fori(0, 2) as qq:
                        for b in range(2):
                            pair(qq * 2 + b, qq, b)
                    pair(4, 2, None)
            body(0, True, (1,))
            with act.Fori(1, R) as mat:
                body(mat, True)
            act.wait_ge(tables_used, 1)
            rel_columns(0, 0)
            scale_rows(0, 0, 0)
            scale_rows(0, 0, 1)
            body(R, False)
            body(R + 1, False)
            for i in range(6):
                if i == 2:
                    rel_columns(21, 1)
                scale_rows(20 + (i + 2) // 4, (i + 2) // 4, (i + 2) % 4)
                if i == 0:
                    act.wait_ge(unit_done, M_GU * 10)
                if i % 2 == 0:
                    n = (HALVES - 1) * CPH + i // 2
                    split_n(n, n // 2, 1, i // 2, n % 2)
            split_n(n + 1, (n + 1) // 2, 1, CPH - 1, (n + 1) % 2)

            act.wait_ge(acc_all, 1)
            def step(s_, j, half):
                if there(s_ + 1):
                    act.wait_ge(tu_done, s_ + 2)
                    wait(act, mm_done, s_)
                    for a in range(2):
                        ins = s.activation(uT[:, 1 - j, a], PT[a].rearrange("p (k c) -> p k c", k=KD), ACT.Copy)
                    ins.then_inc(uT_set, 1)
                if there(s_ + 2):
                    wait(act, tu_done, s_ + 1)
                    s.activation(up_pair[:, j, 0], row(acc, s_ + 2), ACT.Copy).then_inc(u_hi, 1)
                if there(s_ + 1):
                    t = s_ + 1
                    act.wait_ge(x2_in[1 - j], (half + (j + 1)) * 16)
                    wait(act, xx_set, s_)
                    wait(act, d_set, s_)
                    s.activation(xn2[:, 1 - j], xt2[:, 1 - j], ACT.Identity, scale=col(rstd, t),
                                 bias=col(nmr, t)).then_inc(xn_set, 1)
                    act.wait_ge(u_lo, s_ + 2)
                    s.activation(row(acc, t), row(acc, t), ACT.Tanh).then_inc(tanh_set, 1)
                if there(s_ - 2):
                    act.wait_ge(th_done, s_ - 1)
                    for a in range(2):
                        ins = s.activation(cols(xT[:, a], (s_ - 2) * P, P), PT[a].rearrange("p (k c) -> p k c", k=KD),
                                           ACT.Copy)
                    ins.then_inc(hT_set, 1)
                if there(s_ - 1):
                    act.wait_ge(h_set, s_)
                    wait(act, th_done, s_ - 2)
                    wait(act, h_out[1 - j], (half + (j - 1)) * 16)
                    s.activation(h_pair[:, 1 - j, 0], row(acc, s_ - 1), ACT.Copy).then_inc(h_hi, 1)
            steps(act, step, -2, NT)
            act.wait_ge(mm_done, NT)
            act.wait_ge(sh_in, 48)
            for c in range(3):
                s.activation(sw[:, 0, c, :], sh_stage[:, c], ACT.Copy, scale=WSC).then_inc(est_hi, 1)
            steps(act, step, NT)

            def high(c):
                if c == 0:
                    act.wait_ge(est_lo, 3)
                act.wait_ge(est_in[c % 2], (c // 2 + 1) * 16)
                s.activation(est[:, c % 2], est[:, c % 2], ACT.Copy, scale=WSC).then_inc(est_sc, 1)
                act.wait_ge(est_sc, c + 1)
                s.activation(ew[:, 0, 0, c * 2048:(c + 1) * 2048], est[:, c % 2], ACT.Copy).then_inc(est_hi, 1)
            act.wait_ge(db_in, 16)
            s.activation(db32, db32, ACT.Copy, scale=WSC).then_inc(db_sc, 1)
            act.wait_ge(db_sc, 1)
            s.activation(db[:, 0], db32, ACT.Copy).then_inc(db_hi, 1)
            act.wait_ge(sc_used, 1)
            s.activation(sc[:, 0:N], sc[:, 0:N], ACT.Tanh, scale=0.5).then_inc(tanh_sc, 1)
            act.wait_ge(tanh_sc, 1)
            s.activation(sc[:, 0:N], sc[:, 0:N], ACT.Identity, bias=1.0).then_inc(sig_set, 1)
            for i in range(SUNITS):
                act.wait_ge(su_done, i + 1)
                wait(act, sa_lo, i - 1)
                g_, u_ = PG[i % 2]
                t_ = s_t[:, i % 2]
                s.activation(t_[:, 0], g_[:, 0:TQ], ACT.Tanh, scale=0.5 / WSC).then_inc(su_t, 1)
                s.activation(t_[:, 1], g_[:, 0:TQ], ACT.Copy, scale=0.5 / WSC).then_inc(su_t, 1)
                s.activation(t_[:, 2], u_[:, 0:TQ], ACT.Copy, scale=1.0 / WSC).then_inc(su_t, 1)
                act.wait_ge(su_t, 3 * i + 1)
                s.activation(t_[:, 0], t_[:, 0], ACT.Identity, bias=1.0).then_inc(su_p, 1)
                if i < 6:
                    high(i)
                act.wait_ge(su_a, i + 1)
                c, n = divmod(i, NP // TQ)
                s.activation(sact[:, 0, c, n * TQ:(n + 1) * TQ], t_[:, 1], ACT.Copy).then_inc(sa_hi, 1)
            act.wait_ge(sa_lo, SUNITS)
            for i in range(2 * NT):
                act.wait_ge(sd_done, i + 1)
                wait(act, sd_set, i - 1)
                s.activation(sd_b[:, i % 2], PU[i % 2], ACT.Copy, scale=1.0 / WSC).then_inc(sd_t, 1)
            act.wait_ge(top_set, 1)
            s.activation(top_f[:, 1], top_v, ACT.Tanh, scale=0.5).then_inc(topf_s, 1)
            act.wait_ge(mask_set, 1)
            act.wait_ge(sd_t, 2 * NT)
            act.wait_ge(sd_set, 2 * NT)
            s.activation(smask[:, 0], sc_work, ACT.Copy).then_inc(mask_hi, 1)

            def evac_xg(e, par):
                act.wait_ge(xgT_done, e + 1)
                s.activation(xgT[:, par, 0, :, 0:P], PT[0].rearrange("p (k c) -> p k c", k=KD), ACT.Copy)
                s.activation(xgT[:, par, 0, :, P:CAP], PR[0][:, :, 0:REST], ACT.Copy).then_inc(xgT_hi, 1)

            def expert(e, par, half, last):
                def gate_up(j):
                    act.wait_ge(ug_done, e * 4 + (j + 1))
                    wait(act, a_lo, e * 4 + (j - 1))
                    ps = PG[0][j % 2]
                    b_g, b_u = of_expert(gbh, e, j), of_expert(ub_s, e, j)
                    s.activation(a_t[:, j % 2, 0, 0:CAP], ps[:, 160:160 + CAP], ACT.Tanh, scale=0.5 / WSC, bias=b_g)
                    s.activation(a_t[:, j % 2, 1, 0:CAP], ps[:, 160:160 + CAP], ACT.Identity, scale=0.5 / WSC, bias=b_g)
                    s.activation(a_t[:, j % 2, 2, 0:CAP], ps[:, 0:CAP], ACT.Identity, scale=1.0 / WSC,
                                 bias=b_u).then_inc(at_set, 1)
                def a_high(j):
                    act.wait_ge(a_set, e * 4 + (j + 1))
                    s.activation(a_pair[:, par, 0, j, 0:CAP], a_t[:, j % 2, 3, 0:CAP], ACT.Copy).then_inc(a_hi, 1)
                def next_w(c):
                    if last:
                        return
                    if c == 0:
                        wait(act, dn_done, e * 4)
                    act.wait_ge(stage_in[(c + 2 * par) % 4], (half * 3 + ((c + 6 * par) // 4 + 1)) * 16)
                    s.activation(ew[:, 1 - par, 0, c * 2048:(c + 1) * 2048], stage[(c + 2 * par) % 4], ACT.Copy,
                                 scale=WSC).then_inc(est_hi, 1)
                s.activation(sco_e[:, par:par + 1], col(sco[:, 0], e), ACT.Copy).then_inc(sco_set, 1)
                for j in range(4):
                    gate_up(j)
                    if j < 3:
                        next_w(j)
                    a_high(j)
                if not last:
                    evac_xg(e + 1, 1 - par)
                act.wait_ge(sco_set, e + 1)
                for h in range(2):
                    next_w(3 + h)
                    act.wait_ge(dn_done, e * 4 + (h + 1))
                    wait(act, eo_out, e * 32 - 32)
                    s.activation(eo[:, par, 0, h * HALF:(h + 1) * HALF], PG[1][h], ACT.Copy,
                                 scale=sco_e[:, par:par + 1]).then_inc(dn_a, 1)
                next_w(5)
            act.wait_ge(idx_set, 4)
            act.wait_ge(base_out, 16 * NT)
            evac_xg(0, 0)
            experts(act, expert)

        @block.tensor
        def _(pe):
            mm = nc.tensor.matmul

            def product(ps, lhs, rhs, ks, first=True, last=True):
                ks = range(ks) if isinstance(ks, int) else ks
                for i, k in enumerate(ks):
                    for a, b in ((0, 0), (0, 1), (1, 0)):
                        ins = mm(ps, lhs(a, k), rhs(b, k), start=first and i == 0 and (a, b) == (0, 0),
                                 stop=last and i == len(ks) - 1 and (a, b) == (1, 0))
                return ins

            def unit(m, h, q, j, between=None):
                pe.wait_ge(w_hi, m * CPH + CPH)
                pe.wait_ge(w_lo, m * CPH + CPH)
                pe.wait_ge(pu_free[j], m * 5 + q + 1)
                first = (q * 2 + j) * P
                def part(ks, **ends):
                    return product(PU[j], lambda a, k: cols(xT[:, a, k, :], first, P),
                                   lambda b, k: wb[:, h, b, k, :], ks, **ends)
                if between:
                    part(range(KD // 2), last=False)
                    between()
                    part(range(KD // 2, KD), first=False).then_inc(unit_done, 1)
                else:
                    part(KD).then_inc(unit_done, 1)

            def count_group(Q, i, base):
                pe.wait_ge(st_set, Q * 4 + i + 1)
                pe.wait_ge(pg_free[i % 2], Q * 2 + (i // 2 + 1))
                for s in range(2):
                    ins = mm(PG[i % 2][0][:, 0:R], stile[:, i * 2 + s], cols_t(is_type, Q * 8 + i * 2 + s),
                             start=s == 0, stop=s == 1)
                ins.then_inc(grp_done, 1)

            def cols_t(v, T):
                return v[:, T, :] if isinstance(T, int) else v[:, bass.ds(T, 1), :].rearrange("p a n -> p (a n)")

            def sum_group(Q, i, base):
                pe.wait_ge(st_set, Q * 4 + (NG + i + 1))
                pe.wait_ge(pg_free[i % 2], Q * 2 + (NG // 2 + i // 2 + 1))
                pe.wait_ge(row_set, Q * 16 + (i * 4 + 6))
                for h in range(2):
                    for s in range(2):
                        b = i * 2 + s
                        for c in range(2):
                            ins = mm(PG[i % 2][h], stile[:, b], ring[:, b, c, h * HALF:(h + 1) * HALF],
                                     start=s == 0 and c == 0, stop=s == 1 and c == 1)
                ins.then_inc(grp_done, 1)

            def body(mat, group=None, m0=0, halves=(0, 1)):
                for h in halves:
                    m = mat * 2 + h
                    def pair(q):
                        for j in range(2):
                            if group:
                                unit(m, h, q, j, lambda: group((m - m0) * 5 + q, 2 * j, None))
                                group((m - m0) * 5 + q, 2 * j + 1, None)
                            else:
                                unit(m, h, q, j)
                    with pe.Fori(0, 2) as qq:
                        for b in range(2):
                            pair(qq * 2 + b)
                    pair(4)

            def tail(group):
                for Q in (20, 21):
                    for i in range(4):
                        group(Q, i, None)

            pe.wait_ge(consts, 7)
            def transpose_x(t):
                pe.wait_ge(xn_hi, t + 1)
                pe.wait_ge(xn_lo, t + 1)
                wait(pe, xT_hi, t)
                wait(pe, xT_lo, t)
                for a in range(2):
                    for k in range(KD):
                        ins = nc.tensor.transpose(PT[a][:, k * P:(k + 1) * P],
                                                  xnp[:, t % 2, a, k * P:(k + 1) * P], ident)
                ins.then_inc(xt_done, 1)
            def first_unit(t):
                pe.wait_ge(xT_hi, t + 1)
                pe.wait_ge(xT_lo, t + 1)
                unit(0, 0, t // 2, t % 2)
            transpose_x(0)
            for t in range(1, NT):
                transpose_x(t)
                first_unit(t - 1)
            first_unit(NT - 1)
            pe.wait_ge(tot_set, 1)
            mm(PG[0][0][:, 0:NT], tri[0:EPART], tot16[0:EPART, 0:NT], start=True, stop=True)
            mm(PG[0][0][:, 16:16 + NT], ones16[0:EPART], tot16[0:EPART, 0:NT],
               start=True, stop=True).then_inc(prefix_done, 1)
            body(0, halves=(1,))
            with pe.Fori(1, COUNT_MAT) as mat:
                body(mat)
            with pe.Fori(COUNT_MAT, COUNT_MAT + 2) as mat:
                body(mat, count_group, COUNT_MAT * 2)
            tail(count_group)
            with pe.Fori(COUNT_MAT + 2, R) as mat:
                body(mat)
            body(R, sum_group, 2 * R)
            body(R + 1, sum_group, 2 * R)
            tail(sum_group)

            pe.wait_ge(acc_all, 1)
            pe.wait_ge(w_hi, HALVES * CPH)
            pe.wait_ge(w_lo, HALVES * CPH)
            pe.wait_ge(gw_lo, 2)
            def transpose_pair(pair):
                for a in range(2):
                    for k in range(KD):
                        ins = nc.tensor.transpose(PT[a][:, k * P:(k + 1) * P], pair[:, a, k * P:(k + 1) * P], ident)
                return ins
            def step(s, j, half):
                if there(s + 1):
                    pe.wait_ge(u_hi, s + 2)
                    pe.wait_ge(u_lo, s + 2)
                    wait(pe, hT_set, s - 2)
                    transpose_pair(up_pair[:, 1 - j]).then_inc(tu_done, 1)
                def gate_half(h):
                    if h == 0:
                        pe.wait_ge(uT_set, s + 1)
                        wait(pe, z_set, s - 1)
                    return product(PG[j][h], lambda a, k: uT[:, j, a, k, :], lambda b, k: wb[:, h, b, k, :], KD)
                if there(s):
                    gate_half(0)
                if there(s - 2):
                    pe.wait_ge(h_hi, s - 1)
                    pe.wait_ge(h_lo, s - 1)
                    if there(s + 1):
                        pe.wait_ge(uT_set, s + 2)
                    wait(pe, hT_set, s - 2)
                    transpose_pair(h_pair[:, j]).then_inc(th_done, 1)
                if there(s):
                    gate_half(1).then_inc(mm_done, 1)
                if there(s - 2):
                    pe.wait_ge(hT_set, s - 1)
                    wait(pe, sc_set, s - 2)
                    product(PU[0][0:NX, 0:P], lambda a, k: gw[:, a, k, :],
                            lambda b, k: cols(xT[:, b, k, :], (s - 2) * P, P), KD).then_inc(sc_done, 1)
            steps(pe, step)

            pe.wait_ge(est_hi, 2)
            pe.wait_ge(est_lo, 2)
            pe.wait_ge(sc_set, NT)
            for i in range(SUNITS):
                c, n = divmod(i, NP // TQ)
                wait(pe, su_t, 3 * (i - 1))
                for w in range(2):
                    ins = product(PG[i % 2][w][:, 0:TQ], lambda a, k: sw[:, a, w, k * SH + c * P:k * SH + (c + 1) * P],
                                  lambda b, k: xT[:, b, k, n * TQ:(n + 1) * TQ], KD)
                ins.then_inc(su_done, 1)
            pe.wait_ge(est_hi, 3)
            pe.wait_ge(est_lo, 3)
            pe.wait_ge(sa_hi, SUNITS)
            pe.wait_ge(sa_lo, SUNITS)
            for i in range(2 * NT):
                t, h = divmod(i, 2)
                wait(pe, sd_t, i - 1)
                product(PU[i % 2], lambda a, k: sact[:, a, k, t * P:(t + 1) * P],
                        lambda b, k: sw[:, b, 2, k * D + h * HALF:k * D + (h + 1) * HALF], KS).then_inc(sd_done, 1)
            pe.wait_ge(topf_i, 1)
            pe.wait_ge(topf_s, 1)
            for w in range(2):
                nc.tensor.transpose(PG[1][0][:, w * 32:w * 32 + NX], top_f[:, w, 0:P], ident32)
                ins = nc.tensor.transpose(PG[1][0][0:REST, w * 32 + NX:w * 32 + 2 * NX], top_f[:, w, P:CAP], ident32)
            ins.then_inc(topT_done, 1)
            pe.wait_ge(db_hi, 1)
            pe.wait_ge(db_lo, 1)
            pe.wait_ge(mask_hi, 1)
            pe.wait_ge(mask_lo, 1)
            pe.wait_ge(sd_t, 2 * NT)
            for i in range(2 * NT):
                t, h = divmod(i, 2)
                wait(pe, base_set, i - 1)
                product(PU[i % 2], lambda a, k: smask[:, a, t * P:(t + 1) * P],
                        lambda b, k: db[:, b, h * HALF:(h + 1) * HALF], 1).then_inc(base_done, 1)

            def transpose_rows(e, par, half):
                pe.wait_ge(xg_in[par], half * 32 + 32)
                wait(pe, xgT_hi, e)
                wait(pe, xgT_lo, e)
                for a in range(2):
                    for k in range(KD):
                        nc.tensor.transpose(PT[a][:, k * P:(k + 1) * P], xg[:, par, 0, a, k * P:(k + 1) * P], ident)
                        ins = nc.tensor.transpose(PR[a][:, k, 0:REST], xg[0:REST, par, 1, a, k * P:(k + 1) * P],
                                                  ident[0:REST, 0:REST])
                ins.then_inc(xgT_done, 1)

            def expert(e, par, half, last):
                pe.wait_ge(xgT_hi, e + 1)
                pe.wait_ge(xgT_lo, e + 1)
                pe.wait_ge(est_hi, e * 6 + 7)
                pe.wait_ge(est_lo, e * 6 + 7)
                for j in range(4):
                    wait(pe, at_set, e * 4 + (j - 1))
                    for w in range(2):
                        ins = product(PG[0][j % 2][:, w * 160:w * 160 + CAP],
                                      lambda a, k: ew[:, par, a, w * 4096 + k * F + j * P:w * 4096 + k * F + (j + 1) * P],
                                      lambda b, k: xgT[:, par, b, k, 0:CAP], KD)
                    ins.then_inc(ug_done, 1)
                if not last:
                    transpose_rows(e + 1, 1 - par, half + par)
                pe.wait_ge(est_hi, e * 6 + 9)
                pe.wait_ge(est_lo, e * 6 + 9)
                def down(m, n, h, ks, **ends):
                    return product(PG[1][h][0:n], lambda a, k: a_pair[:, par, a, k, m * P:m * P + n],
                                   lambda b, k: ew[:, par, b, 8192 + k * D + h * HALF:8192 + k * D + (h + 1) * HALF],
                                   ks, **ends)
                pe.wait_ge(a_hi, e * 4 + 3)
                pe.wait_ge(a_lo, e * 4 + 3)
                for h in range(2):
                    wait(pe, dn_d, e * 2 + (h - 1))
                    down(0, P, h, range(KF - 1), last=False)
                pe.wait_ge(a_hi, e * 4 + 4)
                pe.wait_ge(a_lo, e * 4 + 4)
                for h in range(2):
                    down(0, P, h, range(KF - 1, KF), first=False).then_inc(dn_done, 1)
                for h in range(2):
                    pe.wait_ge(dn_a, e * 2 + (h + 1))
                    down(1, REST, h, KF).then_inc(dn_done, 1)
            pe.wait_ge(base_set, 2 * NT)
            pe.wait_ge(idx_set, 4)
            transpose_rows(0, 0, 0)
            experts(pe, expert)

        @block.vector
        def _(dve_):
            v = nc.vector
            link = chain(dve_, dve)
            for bank in (*pu_free, *pg_free):
                dve_.sem_inc(bank, 1)
            dve_.sem_inc(row_set, 2)
            def newton(link, y, t, ve, var):
                link(v.tensor_scalar(ve, var, EPS, None, ALU.add))
                link(v.tensor_single_scalar(t.bitcast(I32), ve.bitcast(I32), 1, op=ALU.arith_shift_right))
                link(v.tensor_scalar(y.bitcast(I32), t.bitcast(I32), -1.0, float(0x5F3759DF), ALU.mult, ALU.add))
                for _ in range(3):
                    link(v.tensor_tensor(t, y, y, ALU.mult))
                    link(v.scalar_tensor_tensor(out=t, in0=t, scalar=-0.5, in1=ve, op0=ALU.mult, op1=ALU.mult))
                    link(v.scalar_tensor_tensor(out=y, in0=t, scalar=1.5, in1=y, op0=ALU.add, op1=ALU.mult))

            def split(m1, buf, q, b, ordinal):
                dve_.wait_ge(w_hi, m1 * CPH + q + 1)
                ks = slice(q * CW, q * CW + CW) if isinstance(q, int) else bass.ds(q * CW, CW)
                v.scalar_tensor_tensor(out=wb[:, buf, 1, ks, :], in0=wst[:, b], scalar=WSC, in1=wb[:, buf, 0, ks, :],
                                       op0=ALU.mult, op1=ALU.subtract).then_inc(w_lo, 1)

            def x_stats(t):
                dve_.wait_ge(x_in[t], 16)
                v.bn_stats(stats[:, t % 2, 0, :], xin[:, t, 0:HALF])
                link(v.bn_stats(stats[:, t % 2, 1, :], xin[:, t, HALF:D]))
                link(v.bn_aggr(mv[:, t, :], stats[:, t % 2].rearrange("p a b -> p (a b)")))

            def x_rstd(c):
                two = slice(2 * c, 2 * c + 2)
                newton(link, rstd[:, two], nr_t[:, two], nr_y[:, two], mv[:, two, 1])
                v.scalar_tensor_tensor(out=nmr[:, two], in0=mv[:, two, 0], scalar=-1.0, in1=rstd[:, two],
                                       op0=ALU.mult, op1=ALU.mult).then_inc(ln1_set, 1)

            def norm_low(t):
                dve_.wait_ge(xn_hi, t + 1)
                wait(dve_, xt_done, t - 1)
                v.tensor_tensor(xnp[:, t % 2, 1], xn32[:, t % 2], xnp[:, t % 2, 0], ALU.subtract).then_inc(xn_lo, 1)

            def evac_xT(t):
                dve_.wait_ge(xt_done, t + 1)
                v.tensor_copy(xT[:, 1, :, t * P:(t + 1) * P],
                              PT[1].rearrange("p (k c) -> p k c", k=KD)).then_inc(xT_lo, 1)

            def evac_y(m, t, j):
                dve_.wait_ge(y_hi, m * 10 + t + 1)
                v.scalar_tensor_tensor(out=yst[:, j, 1], in0=PU[j], scalar=1.0 / WSC, in1=yst[:, j, 0],
                                       op0=ALU.mult, op1=ALU.subtract).then_inc(pu_free[j], 1)

            def edge_keys():
                dve_.wait_ge(edges_in, 48)
                dve_.wait_ge(consts, 7)
                v.tensor_single_scalar(e_key, e_dst, 7, op=ALU.arith_shift_right)
                v.tensor_single_scalar(e_lane, e_dst, P - 1, op=ALU.bitwise_and)
                v.scalar_tensor_tensor(out=e_rec[:, :, 0], in0=e_typ, scalar=float(NP), in1=e_src,
                                       op0=ALU.mult, op1=ALU.add)
                v.scalar_tensor_tensor(out=e_rec[:, :, 3], in0=e_dst, scalar=float(R), in1=e_typ,
                                       op0=ALU.mult, op1=ALU.add)
                link(v.tensor_copy(e_rec[:, :, 2], e_typ))
                v.tensor_copy(e_rec[:, :, 1], e_lane)
                for k in range(NT):
                    v.tensor_scalar(e_is[:, k, :], e_key, float(k), None, ALU.is_equal)
                link(v.memset(tot16[:, :], 0.0))

            def edge_counts():
                for k in range(NT):
                    last = v.tensor_tensor_scan(e_cum[:, k, :], e_ones, e_is[:, k, :], 0.0, ALU.mult, ALU.add)
                link(last)
                v.tensor_copy(tot16[0:EPART, 0:NT], e_cum[:, :, ECOL - 1]).then_inc(tot_set, 1)

            def edge_offsets():
                dve_.wait_ge(prefix_done, 1)
                link(v.tensor_scalar(toti, PG[0][0][:, 16:16 + NT], float(GROUP - 1), None, ALU.add))
                link(v.tensor_single_scalar(toti, toti, 8, op=ALU.arith_shift_right))
                link(v.tensor_copy(tot[:, 0, :], toti))
                link(v.tensor_tensor_scan(tot[:, 1, :], ones10, tot[:, 0, :], 0.0, ALU.mult, ALU.add))
                link(v.tensor_tensor(tot[:, 2, :], tot[:, 1, :], tot[:, 0, :], ALU.subtract))
                link(v.scalar_tensor_tensor(out=tot[:, 3, :], in0=tot[:, 2, :], scalar=float(GROUP),
                                            in1=PG[0][0][:, 0:NT], op0=ALU.mult, op1=ALU.add))
                link(v.tensor_scalar(tot[:, 2, :], tot[:, 3, :], -1.0, None, ALU.add))

            def edge_places():
                for k in range(NT):
                    last = v.scalar_tensor_tensor(out=e_cum[:, k, :], in0=e_cum[:, k, :],
                                                  scalar=tot[0:EPART, 2, k:k + 1], in1=e_is[:, k, :],
                                                  op0=ALU.add, op1=ALU.mult)
                link(last)

            def edge_rows():
                link(v.tensor_reduce(out=e_posf, in_=e_cum.rearrange("p k t -> p t k"), op=ALU.add, axis=AX_X))
                link(v.tensor_copy(e_pos, e_posf))
                v.tensor_single_scalar(e_lane, e_pos, P - 1, op=ALU.bitwise_and)
                link(v.tensor_single_scalar(e_tile, e_pos, 7, op=ALU.arith_shift_right))
                v.scalar_tensor_tensor(out=e_row, in0=e_lane, scalar=float(ST), in1=e_tile,
                                       op0=ALU.mult, op1=ALU.add).then_inc(pos_set, 1)

            def edge_groups():
                link(v.tensor_scalar(gmapf, iota_g, tot[0:1, 1, 0:1], None, ALU.is_ge))
                for k in range(1, NT):
                    link(v.scalar_tensor_tensor(out=gmapf, in0=iota_g, scalar=tot[0:1, 1, k:k + 1], in1=gmapf,
                                                op0=ALU.is_ge, op1=ALU.add))
                link(v.tensor_scalar(gmap, gmapf, float(NT - 1), None, ALU.min))

            def count_tiles(Q, i):
                wait(dve_, grp_done, (Q - 1) * 4 + i + 1)
                for s in range(2):
                    ins = v.tensor_scalar(stile[:, i * 2 + s], iota16, col(dloc, Q * 8 + i * 2 + s), None, ALU.is_equal)
                ins.then_inc(st_set, 1)

            def sum_tiles(Q, i):
                if not (isinstance(Q, int) and Q == 0):
                    dve_.wait_ge(grp_done, (Q - 1) * 4 + (NG + i + 1))
                for s in range(2):
                    T = Q * 8 + i * 2 + s
                    ins = v.tensor_scalar(stile[:, i * 2 + s], iota16, col(dloc, T), col(s_all, T), ALU.is_equal, ALU.mult)
                ins.then_inc(st_set, 1)

            def add_rows(Q, i, tiles=(0, 1)):
                for s in tiles:
                    b = i * 2 + s
                    for h in range(2):
                        dve_.wait_ge(row_scaled, Q * 16 + (b * 2 + h + 1))
                        low = ring[:, b, 1, h * HALF:(h + 1) * HALF]
                        v.tensor_tensor(low, low, row_t[:, h], ALU.add).then_inc(row_set, 1)

            def next_rows(Q, i, s):
                if i < 2:
                    add_rows(Q, i + 2, (s,))
                else:
                    add_rows(Q + 1, i - 2, (s,))

            def tile_of(Q, i):
                g_ = Q * 4 + i
                return v.value_load(gmap[0:1, g_:g_ + 1] if isinstance(g_, int) else gmap[0:1, bass.ds(g_, 1)],
                                    min_val=0, max_val=NT - 1)

            def count_add(Q, i):
                dve_.wait_ge(grp_done, Q * 4 + i + 1)
                dve_.wait_ge(pg_free[(i - 1) % 2], Q * 2 + ((i + 1) // 2 + 1))
                d = tile_of(Q, i)
                c = cnt[:, bass.ds(d * R, R)]
                v.tensor_tensor(c, PG[i % 2][0][:, 0:R], c, ALU.add).then_inc(pg_free[i % 2], 1)

            def sum_add(Q, i):
                dve_.wait_ge(grp_done, Q * 4 + (NG + i + 1))
                dve_.wait_ge(pg_free[(i - 1) % 2], Q * 2 + (NG // 2 + (i + 1) // 2 + 1))
                d = tile_of(Q, i)
                for h in range(2):
                    a = acc[:, bass.ds(d, 1), h * HALF:(h + 1) * HALF].rearrange("p a n -> p (a n)")
                    ins = v.scalar_tensor_tensor(out=a, in0=PG[i % 2][h], scalar=1.0 / SSC, in1=a, op0=ALU.mult, op1=ALU.add)
                ins.then_inc(pg_free[i % 2], 1)

            def half_row(x_, t, h):
                return row(x_, t)[:, h * HALF:(h + 1) * HALF]

            x_stats(0)
            x_stats(1)
            x_rstd(0)
            x_stats(2)
            norm_low(0)
            for n in range(2):
                split(0, 0, n, n % 2, n // 2)
            norm_low(1)
            x_stats(3)
            evac_xT(0)
            for n in range(2, CPH):
                split(0, 0, n, n % 2, n // 2)
            evac_xT(1)
            x_rstd(1)
            norm_low(2)
            x_stats(4)
            x_stats(5)
            for t in range(2, NT + 2):
                u = t - 2
                evac_y(0, u, u % 2)
                if t < NT:
                    evac_xT(t)
                if t + 1 < NT:
                    norm_low(t + 1)
                if t % 2 == 0 and t + 2 < NT:
                    x_rstd(t // 2 + 1)
                if t % 2 == 1 and t + 4 < NT:
                    x_stats(t + 3)
                    x_stats(t + 4)
                if t % 2 and u // 2 < CPH:
                    split(1, 1, u // 2, u // 2 % 2, None)
                if t == NT - 3:
                    edge_keys()
                if t == NT - 2:
                    edge_counts()
            for t in range(NT):
                evac_y(1, t, t % 2)
                if t == 0:
                    edge_offsets()
                elif t == 1:
                    edge_places()
                elif t == 2:
                    edge_rows()
                elif t == 4:
                    edge_groups()
                if t % 2 and t // 2 < CPH:
                    split(2, 0, t // 2, t // 2 % 2, None)
            dve_.wait_ge(small_in, 48)
            link(v.tensor_scalar(gw[:, 0], gw32, WSC, None, ALU.mult))
            v.scalar_tensor_tensor(out=gw[:, 1], in0=gw32, scalar=WSC, in1=gw[:, 0], op0=ALU.mult, op1=ALU.subtract).then_inc(gw_lo, 1)
            v.tensor_scalar(gbh, gb_s, 0.5, None, ALU.mult).then_inc(gw_lo, 1)


            def body(mat, kind, group=None, tiles=None, m0=0):
                for h in range(2):
                    m = mat * 2 + h
                    def unit(q, j):
                        t = q * 2 + j
                        if kind == "y":
                            evac_y(m, t, j)
                        elif kind == "root":
                            dve_.wait_ge(unit_done, m * 10 + t + 1)
                            dve_.wait_ge(pg_free[0], ((m - m0) * 5 + q) * 2 + (NG // 2 + j + 2))
                            a = half_row(acc, t, h)
                            v.scalar_tensor_tensor(out=a, in0=PU[j], scalar=1.0 / WSC, in1=a,
                                                   op0=ALU.mult, op1=ALU.add).then_inc(pu_free[j], 1)
                            dve_.wait_ge(pu_free[j], m * 5 + q + 2)
                        else:
                            dve_.wait_ge(unit_done, m * 10 + t + 1)
                            v.scalar_tensor_tensor(out=half_row(zx, t, h), in0=PU[j], scalar=1.0 / WSC,
                                                   in1=bgate[:, h * HALF:(h + 1) * HALF],
                                                   op0=ALU.mult, op1=ALU.add).then_inc(pu_free[j], 1)
                    def pair(q, qq, b):
                        for j in range(2):
                            def of_group(i):
                                Q = (m - m0) * 5 + q
                                if kind != "y":
                                    next_rows(Q, i, 0)
                                group(Q, i)
                                if kind != "y":
                                    next_rows(Q, i, 1)
                                tiles(Q + 1, i)
                            if group:
                                of_group(2 * j)
                            unit(q, j)
                            if group:
                                of_group(2 * j + 1)
                        if b is not None and not (isinstance(m, int) and m + 1 >= HALVES):
                            split(m + 1, (h + 1) % 2, q, b, None)
                    with dve_.Fori(0, 2) as qq:
                        for b in range(2):
                            pair(qq * 2 + b, qq, b)
                    pair(4, 2, None)

            def tail(group, tiles, beside=None):
                for Q in (20, 21):
                    for i in range(4):
                        rows = beside and (Q == 20 or i < 2)
                        if rows:
                            next_rows(Q, i, 0)
                        group(Q, i)
                        if rows:
                            next_rows(Q, i, 1)
                        if Q == 20:
                            tiles(21, i)
                        if beside and i % 2 == 0:
                            beside((Q - 20) * 2 + i // 2)

            with dve_.Fori(1, COUNT_MAT) as mat:
                body(mat, "y")
            dve_.wait_ge(rec_in, 16)
            v.memset(cnt, 0.0)
            v.tensor_copy(dloc, rec[:, :, 1])
            link(v.tensor_copy(etf, rec[:, :, 2]))
            for r in range(R):
                last = v.tensor_scalar(is_type[:, :, r], etf, float(r), None, ALU.is_equal)
            link(last)
            for i in range(4):
                count_tiles(0, i)
            with dve_.Fori(COUNT_MAT, COUNT_MAT + 2) as mat:
                body(mat, "y", count_add, count_tiles, COUNT_MAT * 2)
            tail(count_add, count_tiles)
            dve_.wait_ge(pg_free[0], NG // 2 + 1)
            dve_.wait_ge(pg_free[1], NG // 2 + 1)
            link(v.tensor_scalar(cnt, cnt, 1.0, None, ALU.max))
            link(v.reciprocal(rinv, cnt))
            v.tensor_scalar(rinv, rinv, SSC, None, ALU.mult).then_inc(rinv_set, 1)
            with dve_.Fori(COUNT_MAT + 2, R) as mat:
                body(mat, "y")
            dve_.wait_ge(s_in, 16 * ST)
            link(v.tensor_copy(s_h16, s_all))
            link(v.reciprocal(s_rec, s_h16))
            link(v.tensor_tensor(s_rel, s_all, s_h16, ALU.subtract))
            link(v.tensor_tensor(s_rel, s_rel, s_rec, ALU.mult))
            v.memset(s_h16, 0.0).then_inc(tables_used, 1)
            dve_.wait_ge(bgate_in, 16)
            dve_.wait_ge(bias_in, 16 * NT)
            for i in range(4):
                sum_tiles(0, i)
            add_rows(0, 0)
            add_rows(0, 1)
            body(R, "root", sum_add, sum_tiles, 2 * R)
            body(R + 1, "gx", sum_add, sum_tiles, 2 * R)
            tail(sum_add, sum_tiles, lambda i: split(HALVES - 1, 1, i, i % 2, None))
            dve_.wait_ge(pg_free[0], NG + 1)
            dve_.wait_ge(pg_free[1], NG + 1)
            dve_.wait_ge(w_lo, HALVES * CPH)
            dve_.sem_inc(acc_all, 1)

            GATE_LINKS = 3 + 3 + 9 + 1
            def step(s, j, half):
                if there(s - 2):
                    dve_.wait_ge(sc_done, s - 1)
                    c = cols(sc, (s - 2) * P, P)
                    v.tensor_scalar(c, PU[0][0:NX, 0:P], 1.0 / WSC, 17.0, ALU.mult, ALU.min).then_inc(sc_set, 1)
                if there(s):
                    gate = chain(dve_, dve_gate, s * GATE_LINKS)
                    dve_.wait_ge(mm_done, s + 1)
                    for h in range(2):
                        zh = half_row(zx, s, h)
                        ins = v.scalar_tensor_tensor(out=zh, in0=PG[j][h], scalar=1.0 / WSC, in1=zh,
                                                     op0=ALU.mult, op1=ALU.add)
                    ins.then_inc(z_set, 1)
                    dve_.wait_ge(z_set, s + 1)
                    dve_.wait_ge(d_set, s + 1)
                    gate(v.tensor_tensor(row(acc, s), row(zx, s), row(acc, s), ALU.mult))
                    dve_.wait_ge(xx_set, s + 1)
                    v.tensor_tensor(row(zx, s), row(acc, s), xt2[:, j], ALU.add).then_inc(x1_set, 1)
                    dve_.wait_ge(x1_set, s + 1)
                    for h in range(2):
                        ins = v.bn_stats(stats[:, j, h, :], half_row(zx, s, h))
                    gate(ins)
                    gate(v.bn_aggr(mv2, stats[:, j].rearrange("p a b -> p (a b)")))
                    newton(gate, ln2[:, j, 0:1], nr2[:, 0:1], nr2[:, 1:2], mv2[:, 1:2])
                    gate(v.scalar_tensor_tensor(out=ln2[:, j, 1:2], in0=mv2[:, 0:1], scalar=-1.0, in1=ln2[:, j, 0:1],
                                                op0=ALU.mult, op1=ALU.mult))
                    v.tensor_scalar(row(acc, s), row(zx, s), ln2[:, j, 0:1], ln2[:, j, 1:2],
                                    ALU.mult, ALU.add).then_inc(h_set, 1)
                    assert gate.count[0] == GATE_LINKS
            steps(dve_, step, -2, NT + 1)
            for c in range(3):
                dve_.wait_ge(est_hi, c + 1)
                v.scalar_tensor_tensor(out=sw[:, 1, c, :], in0=sh_stage[:, c], scalar=WSC, in1=sw[:, 0, c, :],
                                       op0=ALU.mult, op1=ALU.subtract).then_inc(est_lo, 1)
            steps(dve_, step, NT + 1)

            dve_.wait_ge(sc_set, NT)
            link(v.tensor_scalar(sc, sc, -104.0, None, ALU.max))
            for i in range(TOP8):
                src_ = sc if i == 0 else sc_work
                eight = slice(i * 8, i * 8 + 8)
                link(v.max(top_v[:, eight], src_[:, 0:N]))
                link(v.max_index(top_i[:, eight], top_v[:, eight], src_[:, 0:N]))
                if i < TOP8 - 1:
                    link(v.match_replace(sc_work[:, 0:N], top_v[:, eight], src_[:, 0:N], MARK))
                if i == 0:
                    dve_.sem_inc(sc_used, 1)
            v.memset(top_f[:, 0], 0.0)
            over = TOP8 * 8 - CAP
            v.memset(sc_work[:, N:N + over], -MARK)
            link(v.tensor_copy(top_f[:, 1, 0:8], top_v[:, (TOP8 - 1) * 8:TOP8 * 8]))
            link(v.memset(top_f[:, 1, 8 - over:8], -MARK))
            link(v.match_replace(sc_work[:, 0:N + over], top_f[:, 1, 0:8], sc_work[:, 0:N + over], MARK))
            v.tensor_copy(top_f[:, 0], top_i).then_inc(topf_i, 1)
            link(v.memset(sc_work[:, N:NP], 0.0))
            dve_.sem_inc(top_set, 1)
            dve_.wait_ge(sig_set, 1)
            v.scalar_tensor_tensor(out=sc_work[:, 0:N], in0=sc_work[:, 0:N], scalar=MARK, in1=sc[:, 0:N],
                                   op0=ALU.is_equal, op1=ALU.mult).then_inc(mask_set, 1)
            dve_.wait_ge(topT_done, 1)
            for m, n in ((0, P), (1, REST)):
                v.tensor_copy(idx[0:n, m], PG[1][0][0:n, m * NX:(m + 1) * NX]).then_inc(idx_set, 1)
                v.tensor_scalar(sco[0:n, m], PG[1][0][0:n, 32 + m * NX:32 + (m + 1) * NX], 1.0, 0.5 / WSC,
                                ALU.add, ALU.mult).then_inc(idx_set, 1)
            dve_.wait_ge(mask_hi, 1)
            dve_.wait_ge(mask_set, 1)
            v.tensor_tensor(smask[:, 1], sc_work, smask[:, 0], ALU.subtract).then_inc(mask_lo, 1)
            dve_.wait_ge(sd_set, 2 * NT)
            for i in range(2 * NT):
                dve_.wait_ge(base_done, i + 1)
                a = half_row(zx, i // 2, i % 2)
                v.scalar_tensor_tensor(out=a, in0=PU[i % 2], scalar=0.5 / WSC, in1=a,
                                       op0=ALU.mult, op1=ALU.add).then_inc(base_set, 1)

            def evac_xg(e, par):
                dve_.wait_ge(xgT_done, e + 1)
                v.tensor_copy(xgT[:, par, 1, :, 0:P], PT[1].rearrange("p (k c) -> p k c", k=KD))
                v.tensor_copy(xgT[:, par, 1, :, P:CAP], PR[1][:, :, 0:REST]).then_inc(xgT_lo, 1)

            def expert(e, par, half, last):
                def product_of(j):
                    dve_.wait_ge(at_set, e * 4 + (j + 1))
                    t_ = a_t[:, j % 2]
                    v.scalar_tensor_tensor(out=t_[:, 0, 0:CAP], in0=t_[:, 0, 0:CAP], scalar=1.0, in1=t_[:, 1, 0:CAP],
                                           op0=ALU.add, op1=ALU.mult).then_inc(a_mid, 1)
                    dve_.wait_ge(a_mid, e * 4 + (j + 1))
                    v.tensor_tensor(t_[:, 3, 0:CAP], t_[:, 0, 0:CAP], t_[:, 2, 0:CAP], ALU.mult).then_inc(a_set, 1)
                def a_low(j):
                    dve_.wait_ge(a_hi, e * 4 + (j + 1))
                    v.tensor_tensor(a_pair[:, par, 1, j, 0:CAP], a_t[:, j % 2, 3, 0:CAP], a_pair[:, par, 0, j, 0:CAP],
                                    ALU.subtract).then_inc(a_lo, 1)
                def next_w(c):
                    if last:
                        return
                    dve_.wait_ge(est_hi, e * 6 + (10 + c))
                    w = ew[:, 1 - par, :, c * 2048:(c + 1) * 2048]
                    v.scalar_tensor_tensor(out=w[:, 1], in0=stage[(c + 2 * par) % 4], scalar=WSC, in1=w[:, 0],
                                           op0=ALU.mult, op1=ALU.subtract).then_inc(est_lo, 1)
                for j in range(4):
                    product_of(j)
                    if j < 2:
                        next_w(j)
                    a_low(j)
                if not last:
                    evac_xg(e + 1, 1 - par)
                next_w(2)
                next_w(3)
                next_w(4)
                next_w(5)
                for h in range(2):
                    dve_.wait_ge(dn_done, e * 4 + (h + 3))
                    wait(dve_, eo_out, e * 32 - 32)
                    v.tensor_scalar(eo[0:REST, par, 1, h * HALF:(h + 1) * HALF], PG[1][h][0:REST],
                                    sco[0:REST, 1, e:e + 1] if isinstance(e, int) else sco[0:REST, 1, bass.ds(e, 1)],
                                    None, ALU.mult).then_inc(dn_d, 1)
            dve_.wait_ge(est_lo, 9)
            dve_.wait_ge(base_out, 16 * NT)
            evac_xg(0, 0)
            experts(dve_, expert)



def kernel(**inputs):
    import numpy as np
    import concourse.bacc as bacc
    from concourse.bass_utils import run_bass_kernel_spmd

    f = {k: np.asarray(v) for k, v in inputs.items()}

    def blocks(a, k):
        return np.ascontiguousarray(a.reshape(k, P, -1).transpose(1, 0, 2).reshape(P, -1))

    arrays = {
        "x": np.pad(f["x"], ((0, NP - N), (0, 0))),
        "src": f["src"].reshape(EPART, ECOL),
        "dst": f["dst"].reshape(EPART, ECOL),
        "etype": f["edge_type_8"].reshape(EPART, ECOL),
        "wall": np.concatenate([f["L0_gnn_weight"], f["L0_gnn_root"][None], f["L0_gnn_w_gate"][D:][None],
                                f["L0_gnn_w_gate"][:D][None]]),
        "bias": f["L0_gnn_bias"],
        "b_gate": f["L0_gnn_b_gate"],
        "gate_wT": blocks(f["L0_ffn_gate_w"].T, KD),
        "upT": np.stack([blocks(a.T, KD) for a in f["L0_ffn_up_w"]]),
        "up_b": np.ascontiguousarray(f["L0_ffn_up_b"].reshape(NX, KF, P).transpose(2, 0, 1).reshape(P, -1)),
        "gT": np.stack([blocks(a.T, KD) for a in f["L0_ffn_gw"]]),
        "gb": np.ascontiguousarray(f["L0_ffn_gb"].reshape(NX, KF, P).transpose(2, 0, 1).reshape(P, -1)),
        "downT": np.stack([blocks(a.T, KF) for a in f["L0_ffn_down_w"]]),
        "down_b": f["L0_ffn_down_b"],
        "sgT": blocks(f["L0_ffn_sh_gate_w"].T, KD),
        "suT": blocks(f["L0_ffn_sh_up_w"].T, KD),
        "sdT": blocks(f["L0_ffn_sh_down_w"].T, KS),
    }
    nc = bacc.Bacc("TRN2", target_bir_lowering=False, num_devices=1)
    aps = {n: nc.dram_tensor("in_" + n, a.shape, mybir.dt.from_np(a.dtype), kind="ExternalInput").ap()
           for n, a in arrays.items()}
    out = nc.dram_tensor("out", (N, D), FP32, kind="ExternalOutput").ap()
    build(nc, out=out, **aps)
    r = run_bass_kernel_spmd(nc, [{"in_" + n: a for n, a in arrays.items()}], core_ids=[0])
    return r.results[0]["out"]
```

```python
import concourse.bass as bass
from concourse import mybir
from contextlib import ExitStack

FP32 = mybir.dt.float32
FP16 = mybir.dt.float16
I32 = mybir.dt.int32
U32 = mybir.dt.uint32
ALU = mybir.AluOpType
ACT = mybir.ActivationFunctionType
AX_X = mybir.AxisListType.X

P = 128
N = 1250
D = 1024
NT = -(-N // P)
NP = NT * P
KD = D // P
HALF = D // 2
R = 8
E = 20000
EPART = 125
ECOL = E // EPART
GROUP = 2 * P
NG = (E + NT * (GROUP - 1)) // GROUP
ST = 2 * NG
NX = 16
F = 512
KF = F // P
SH = 256
KS = SH // P
CAP = -(-2 * N // NX)
REST = CAP - P
REST2 = 2 * REST
TOP8 = -(-CAP // 8)
EPS = 1e-5
WSC = 64.0
SSC = 1024.0
HALVES = 2 * (R + 3)
M_GU = 2 * R + 4
CW = 2
CPH = KD // CW
QUADS = NG // 4
COUNT_MAT = 3
TQ = NP // 5
TRIO = 80
SUNITS = KS * (NP // TQ)
MARK = -1.0e30


def build(nc, x, src, dst, etype, wall, bias, b_gate, gate_wT, upT, up_b, gT, gb, downT, down_b,
          sgT, suT, sdT, out):
    ctx = ExitStack()
    with ctx:
        FIXED = 196608
        MEM = ctx.enter_context(nc.sbuf_tensor("mem", [P, (FIXED + 16128) // 2], FP16))

        def at(off, shape, dt, parts=P):
            n = 1
            for s in shape:
                n *= s
            size = 2 if dt == FP16 else 4
            v = MEM[0:parts, off // 2:(off + n * size) // 2]
            if dt != FP16:
                v = v.bitcast(dt)
            if len(shape) == 2:
                v = v.rearrange("p (a b) -> p a b", a=shape[0])
            elif len(shape) == 3:
                v = v.rearrange("p (a b c) -> p a b c", a=shape[0], b=shape[1])
            elif len(shape) == 4:
                v = v.rearrange("p (a b c d) -> p a b c d", a=shape[0], b=shape[1], c=shape[2])
            return v

        XT, ZX, ACC, WB, WST, RING = 0, 40960, 81920, 122880, 155648, 163840
        xT = at(XT, [2, KD, NP], FP16)
        acc = at(ACC, [NT, D], FP32)
        zx = at(ZX, [NT, D], FP32)
        wb = at(WB, [2, 2, KD, HALF], FP16)
        wst = at(WST, [2, CW, HALF], FP32)
        ring = at(RING, [8, 2, D], FP16)
        xin = acc
        xn32 = at(ZX, [2, D], FP32)
        xnp = at(ZX + 8192, [2, 2, D], FP16)
        e_src = at(RING, [ECOL], I32, EPART)
        e_dst = at(RING + 640, [ECOL], I32, EPART)
        e_typ = at(RING + 1280, [ECOL], I32, EPART)
        e_key = at(RING + 1920, [ECOL], I32, EPART)
        lane_ones = at(RING + 2560, [ECOL], FP32, EPART)
        e_rec = at(RING + 3200, [ECOL, 4], I32, EPART)
        e_posf = at(RING + 5760, [ECOL], FP32, EPART)
        e_pos = at(RING + 6400, [ECOL], I32, EPART)
        e_lane = at(RING + 7040, [ECOL], I32, EPART)
        e_tile = at(RING + 7680, [ECOL], I32, EPART)
        e_row = at(RING + 8320, [ECOL], I32, EPART)
        e_is = at(RING + 8960, [NT, ECOL], FP32, EPART)
        e_cum = at(RING + 15360, [NT, ECOL], FP32, EPART)
        rec0 = at(RING + 21760, [ST, 4], I32)
        tri = at(RING + 24576, [P], FP16)
        ones16 = at(RING + 24832, [P], FP16)
        tot16 = at(RING + 25088, [16], FP16)
        tot = at(RING + 25120, [4, NT], FP32)
        toti = at(RING + 25280, [NT], I32)
        iota_g = at(RING + 25344, [NG], FP32, 1)
        gmapf = at(RING + 25696, [NG], FP32, 1)
        key_ones = at(RING + 26048, [NT], FP32)
        is_type = at(RING + 26112, [ST, R], FP16)
        cnt = at(RING + 28928, [NT * R], FP32)
        rinv = at(RING + 29248, [NT * R], FP32)
        s_h16 = at(RING + 30080, [ST], FP16)
        s_rec = at(RING + 30432, [ST], FP32)
        h_pair = at(WST, [2, 2, D], FP16)
        uT = at(WST + 8192, [2, 2, KD, P], FP16)
        xt2 = at(WST + 16384, [2, D], FP32)
        xn2 = at(WST + 24576, [2, D], FP32)
        up_pair = at(WST + 32768, [2, 2, D], FP16)
        off = FIXED
        def fixed(shape, dt, parts=P):
            nonlocal off
            v = at(off, shape, dt, parts)
            n = 1
            for s in shape:
                n *= s
            off += (n * (2 if dt == FP16 else 4) + 31) // 32 * 32
            assert off <= FIXED + 16128
            return v
        rec = fixed([ST, 4], I32)
        dloc = fixed([ST], FP32)
        etf = fixed([ST], FP32)
        s_rel = etf
        s_all = fixed([ST], FP32)
        gmap = fixed([NG], I32, 1)
        iota16 = fixed([P], FP16)
        ident = fixed([P], FP16)
        ident32 = fixed([16], FP32, 16)
        stats = fixed([2, 2, 6], FP32)
        mv = fixed([NT, 2], FP32)
        nr_y = fixed([NT], FP32)
        nr_t = fixed([NT], FP32)
        rstd = fixed([NT], FP32)
        nmr = fixed([NT], FP32)
        mv2 = fixed([2], FP32)
        nr2 = fixed([4], FP32)
        ln2 = fixed([2, 2], FP32)
        ub_s = fixed([NX, KF], FP32)
        gb_s = fixed([NX, KF], FP32)
        gbh = fixed([NX, KF], FP32)
        sco_e = fixed([2], FP32)
        rel8 = fixed([2, 8], FP32)
        SLOTS = off
        stile = fixed([8, P], FP16)
        row_t = fixed([2, HALF], FP16)
        yst = fixed([2, 2, HALF], FP16)
        bgate = at(SLOTS + 4096, [D], FP32)
        gw = at(FIXED, [2, KD, TRIO], FP16)
        gw32 = at(SLOTS + 5120, [KD, TRIO], FP32)
        sc = at(SLOTS, [NP], FP32, TRIO)
        top_v = at(SLOTS + 5120, [TOP8 * 8], FP32, TRIO)
        top_i = at(SLOTS + 5760, [TOP8 * 8], U32, NX)
        top_f = at(SLOTS + 6400, [2, P + REST2], FP32, NX)
        top_8 = at(SLOTS + 8160, [8], FP32, TRIO)
        idx = at(SLOTS + 7904, [2, NX], I32)
        sco = at(SLOTS + 8032, [2, NX], FP32)
        sc_work = at(FIXED, [NP], FP32, TRIO)
        EW1 = ACC + 2 * 3 * 4096 * 2
        EST = ACC + 2 * 2 * 3 * 4096 * 2
        ew = at(ACC, [2, 2, 3 * 4096], FP16)
        est = at(EST, [2, 2048], FP32)
        sh_stage = at(ACC, [3, 2048], FP32)
        stage = [est[:, 0], est[:, 1], at(ZX + 16384, [2048], FP32), at(ZX + 24576, [2048], FP32)]
        sw = at(EW1, [2, 3, 2048], FP16)
        sact = at(EW1 + 24576, [2, KS, NP], FP16)
        s_t = at(EW1 + 34816, [2, 3, TQ], FP32)
        sd_b = at(EW1 + 34816, [2, HALF], FP32)
        smask = at(EW1 + 34816, [NP], FP16, TRIO)
        db = at(EW1 + 40960, [D], FP16, TRIO)
        db32 = at(EW1 + 45056, [D], FP32, TRIO)
        xg = at(XT, [2, 2, 2, D], FP16)
        xgT = at(XT + 16384, [2, 2, KD, 160], FP16)
        a_pair = at(XT + 26624, [2, KF, 320], FP16)
        A_LOW = CAP + REST
        a_t = at(XT + 31744, [2, 4, 160], FP32)
        eo = at(ZX, [2, 2, D], FP32)

        PT = [ctx.enter_context(nc.psum_tensor(f"pt{i}", [P, D], FP16))[:, :] for i in range(2)]
        PU = [ctx.enter_context(nc.psum_tensor(f"pu{i}", [P, 512], FP32))[:, :] for i in range(2)]
        PG = [[ctx.enter_context(nc.psum_tensor(f"pg{i}{j}", [P, 512], FP32))[:, :] for j in range(2)] for i in range(2)]

        y_tab = nc.dram_tensor("y_tab", [R * NP, 2 * D], FP16, kind="Internal").ap()
        rec_tab = nc.dram_tensor("rec_tab", [P * ST, 4], I32, kind="Internal").ap()
        rinv_tab = nc.dram_tensor("rinv_tab", [NP * R, 1], FP32, kind="Internal").ap()
        h_tab = nc.dram_tensor("h_tab", [NP, 2 * D], FP16, kind="Internal").ap()

        sem = lambda name: ctx.enter_context(nc.semaphore(name))
        x_in = [sem(f"x_in{t}") for t in range(NT)]
        edges_in = sem("edges_in"); small_in = sem("small_in"); bias_in = sem("bias_in"); bgate_in = sem("bgate_in")
        consts = sem("consts"); dve = sem("dve"); pool_own = sem("pool_own")
        ln1_set = sem("ln1_set"); xn_hi = sem("xn_hi"); xn_lo = sem("xn_lo")
        xt_done = sem("xt_done"); xT_hi = sem("xT_hi"); xT_lo = sem("xT_lo"); gw_in = sem("gw_in"); gw_lo = sem("gw_lo")
        wst_in = [sem("wst_in0"), sem("wst_in1")]; w_hi = sem("w_hi"); w_lo = sem("w_lo")
        unit_done = sem("unit_done"); y_hi = sem("y_hi"); pu_free = [sem("pu_free0"), sem("pu_free1")]
        y_out = [sem("y_out0"), sem("y_out1")]
        tot_set = sem("tot_set"); prefix_done = sem("prefix_done"); pos_set = sem("pos_set")
        rec0_set = sem("rec0_set"); rec0_out = sem("rec0_out"); rec_out = sem("rec_out"); rec_in = sem("rec_in")
        st_set = sem("st_set"); grp_done = sem("grp_done"); pg_free = [sem("pg_free0"), sem("pg_free1")]
        tables_used = sem("tables_used"); rinv_set = sem("rinv_set"); rinv_out = sem("rinv_out"); s_in = sem("s_in")
        rel8_set = sem("rel8_set"); row_scaled = sem("row_scaled"); row_set = sem("row_set")
        row_in = [sem(f"row_in{b}") for b in range(8)]
        acc_all = sem("acc_all")
        u_hi = sem("u_hi"); u_lo = sem("u_lo"); tu_done = sem("tu_done"); uT_set = sem("uT_set")
        x2_in = [sem("x2_in0"), sem("x2_in1")]; xn_set = sem("xn_set"); tanh_set = sem("tanh_set")
        xx_set = sem("xx_set"); d_set = sem("d_set"); mm_done = sem("mm_done"); z_set = sem("z_set")
        x1_set = sem("x1_set"); h_set = sem("h_set"); h_hi = sem("h_hi"); h_lo = sem("h_lo")
        th_done = sem("th_done"); hT_set = sem("hT_set"); h_out = [sem("h_out0"), sem("h_out1")]
        sc_done = sem("sc_done"); sc_set = sem("sc_set")
        est_in = [sem("est_in0"), sem("est_in1")]; est_sc = sem("est_sc"); est_hi = sem("est_hi"); est_lo = sem("est_lo")
        sh_in = sem("sh_in"); stage_in = [sem(f"stage_in{b}") for b in range(4)]
        db_in = sem("db_in"); db_hi = sem("db_hi"); db_lo = sem("db_lo")
        db_sc = sem("db_sc"); sc_used = sem("sc_used"); tanh_sc = sem("tanh_sc")
        su_done = sem("su_done"); su_t = sem("su_t"); su_p = sem("su_p"); su_a = sem("su_a"); sa_hi = sem("sa_hi"); sa_lo = sem("sa_lo")
        sd_done = sem("sd_done"); sd_t = sem("sd_t"); sd_set = sem("sd_set")
        top_set = sem("top_set"); topf_i = sem("topf_i"); topf_s = sem("topf_s"); topT_done = sem("topT_done"); idx_set = sem("idx_set")
        sig_set = sem("sig_set"); mask_set = sem("mask_set"); mask_hi = sem("mask_hi"); mask_lo = sem("mask_lo")
        base_done = sem("base_done"); base_set = sem("base_set"); base_out = sem("base_out")
        xg_in = [sem("xg_in0"), sem("xg_in1")]; xgT_done = sem("xgT_done"); xgT_hi = sem("xgT_hi"); xgT_lo = sem("xgT_lo")
        ug_done = sem("ug_done"); at_set = sem("at_set")
        a_set = sem("a_set"); a_hi = sem("a_hi"); a_lo = sem("a_lo")
        a_mid = sem("a_mid"); dve_gate = sem("dve_gate"); sco_set = sem("sco_set")
        dn_done = sem("dn_done"); dn_a = sem("dn_a"); dn_d = sem("dn_d"); eo_out = sem("eo_out")

        def wait(eng, s, value):
            if not isinstance(value, int) or value > 0:
                eng.wait_ge(s, value)

        def there(t):
            return not isinstance(t, int) or 0 <= t < NT

        def row(v, t):
            return v[:, t, :] if isinstance(t, int) else v[:, bass.ds(t, 1), :].rearrange("p a n -> p (a n)")

        def cols(v, first, n):
            return v[..., first:first + n] if isinstance(first, int) else v[..., bass.ds(first, n)]

        def chain(eng, s, base=0):
            count = [0]
            def link(ins):
                count[0] += 1
                ins.then_inc(s, 1)
                eng.wait_ge(s, base + count[0])
            link.count = count
            return link


        M_LAST = 2 * R + 3
        REST_Q = (M_LAST - 2 * R) * 5
        REST_G = NG - 4 * REST_Q
        half_unit_at = {k * REST_G // (2 * NT): k for k in range(2 * NT)}

        def steps(eng, body, first=-2, end=NT + 2):
            for st in range(first, end):
                body(st, st % 2, st // 2)

        def experts(eng, body):
            for e in range(2):
                body(e, e, 0, False)
            with eng.Fori(0, NX // 2 - 2) as i:
                for j in range(2):
                    body(i * 2 + (2 + j), j, i + 1, False)
            for e in range(NX - 2, NX):
                body(e, e % 2, e // 2, e == NX - 1)

        def col(v, i):
            return v[:, i:i + 1] if isinstance(i, int) else v[:, bass.ds(i, 1)]

        def of_expert(v, e, j):
            return v[:, e, j:j + 1] if isinstance(e, int) else \
                v[:, bass.ds(e, 1), j:j + 1].rearrange("p a b -> p (a b)")

        def rest_rows(bank):
            return bank.bitcast(FP16)[:, 0:KD * 32].rearrange("p (k c) -> p k c", k=KD)
        PR = [rest_rows(bank) for bank in PU]
        PR0 = [rest_rows(bank) for bank in PG[0]]

        block = ctx.enter_context(nc.Block())

        @block.sync
        def _(sp):
            def load_x(t):
                sp.dma_start(xin[:, t, :], x[t * P:(t + 1) * P, :]).then_inc(x_in[t], 16)

            def load_w(mat, h, k0, b):
                rows = bass.ds(k0 * P, CW * P)
                s = wall[mat, rows, h * HALF:(h + 1) * HALF] if isinstance(mat, int) else \
                    wall[bass.ds(mat, 1), rows, h * HALF:(h + 1) * HALF].rearrange("a r n -> (a r) n")
                sp.dma_start(wst[:, b], s.rearrange("(c p) n -> p c n", p=P)).then_inc(wst_in[b], 16)

            def first_w(n):
                if n >= 2:
                    sp.wait_ge(w_hi, n - 1)
                    sp.wait_ge(w_lo, n - 1)
                load_w(n // (2 * CPH), n // CPH % 2, n % CPH * CW, n % 2)

            for t in range(2):
                load_x(t)
            for n in range(2):
                first_w(n)
            for t in range(2, 4):
                load_x(t)
            for n in range(2, CPH):
                first_w(n)
            for t in range(4, NT):
                load_x(t)
            for v, a in ((e_src, src), (e_dst, dst), (e_typ, etype)):
                sp.dma_start(v, a).then_inc(edges_in, 16)
            for n in range(CPH, CPH + 2):
                first_w(n)
            for v, a in ((ub_s, up_b), (gb_s, gb)):
                sp.dma_start(v.rearrange("p a b -> p (a b)"), a).then_inc(small_in, 16)
            def store_unit(m, h, mat, q, t, j):
                sp.wait_ge(pu_free[j], m * 5 + (q + 2))
                dst_ = y_tab[bass.ds(mat * NP + t * P, P), :].rearrange(
                    "p (a f) -> p a f", a=2)[:, :, h * HALF:(h + 1) * HALF]
                sp.dma_start(dst_, yst[:, j]).then_inc(y_out[j], 16)

            def sp_body(mat, store):
                for h in range(2):
                    m = mat * 2 + h
                    for qq in range(2):
                        for b in range(2):
                            q = qq * 2 + b
                            if store:
                                for j in range(2):
                                    store_unit(m, h, mat, q, q * 2 + j, j)
                            n = (m + 1) * CPH + q
                            if isinstance(n, int) and n + 2 >= HALVES * CPH:
                                continue
                            sp.wait_ge(w_hi, n + 1)
                            sp.wait_ge(w_lo, n + 1)
                            mm, hh = divmod(h + (1 if q < 2 else 2), 2)
                            load_w(mat + mm, hh, (q + 2) % 4 * CW, b)
                    if store:
                        for j in range(2):
                            store_unit(m, h, mat, 4, 8 + j, j)

            sp_body(0, True)
            sp.wait_ge(xn_lo, NT)
            sp.wait_ge(xn_hi, NT)
            for t in range(NT):
                sp.dma_start(acc[:, t, :], bias.partition_broadcast(P)).then_inc(bias_in, 16)
            with sp.Fori(1, R) as mat:
                sp_body(mat, True)
            sp.wait_ge(y_out[0], 16 * R * 2 * 5)
            sp.wait_ge(y_out[1], 16 * R * 2 * 5)
            sp.dma_start(bgate, b_gate.partition_broadcast(P)).then_inc(bgate_in, 16)
            sp_body(R, False)
            sp_body(R + 1, False)

            def last_w(n):
                sp.wait_ge(w_hi, n - 1)
                sp.wait_ge(w_lo, n - 1)
                load_w(HALVES // 2 - 1, 1, n % CPH * CW, n % 2)
            last_w(HALVES * CPH - 2)

            sp.wait_ge(acc_all, 1)
            def step(s, j, half):
                if there(s + 2):
                    t = s + 2
                    wait(sp, x1_set, s + 1)
                    sp.dma_start(xt2[:, j], x[t * P:(t + 1) * P, :] if isinstance(t, int) else x[bass.ds(t * P, P), :]
                                 ).then_inc(x2_in[j], 16)
                if there(s - 1):
                    t = s - 1
                    sp.wait_ge(h_hi, s)
                    sp.wait_ge(h_lo, s)
                    d_ = h_tab[t * P:(t + 1) * P, :] if isinstance(t, int) else h_tab[bass.ds(t * P, P), :]
                    sp.dma_start(d_, h_pair[:, 1 - j].rearrange("p a n -> p (a n)")).then_inc(h_out[1 - j], 16)
            steps(sp, step, -2, 0)
            last_w(HALVES * CPH - 1)
            sp.dma_start(gw32.rearrange("p a b -> p (a b)"), gate_wT).then_inc(gw_in, 16)
            steps(sp, step, 0, NT - 1)
            for c, w in enumerate((sgT, suT, sdT)):
                sp.dma_start(sh_stage[:, c], w).then_inc(sh_in, 16)
            steps(sp, step, NT - 1)

            sp.wait_ge(h_set, NT)
            sp.wait_ge(h_lo, NT)
            sp.wait_ge(h_hi, NT)
            sp.wait_ge(th_done, NT)
            sp.wait_ge(mm_done, NT)
            sp.wait_ge(h_out[0], 16 * NT // 2)
            sp.wait_ge(h_out[1], 16 * NT // 2)
            sp.dma_start(db32, down_b).then_inc(db_in, 16)

            for c in range(6):
                if c >= 2:
                    sp.wait_ge(est_hi, c + 2)
                    sp.wait_ge(est_lo, c + 2)
                w = (upT, gT, downT)[c // 2]
                sp.dma_start(est[:, c % 2], w[0, :, c % 2 * 2048:(c % 2 + 1) * 2048]).then_inc(est_in[c % 2], 16)
            for t in range(NT):
                rows = min(P, N - t * P)
                sp.wait_ge(base_set, 2 * t + 2)
                sp.dma_start(out[t * P:t * P + rows, :], zx[0:rows, t, :]).then_inc(base_out, 16)
            def expert_chunks(e, par):
                for c in range(6):
                    if not (isinstance(e, int) and c < 4):
                        sp.wait_ge(est_hi, e * 6 + c)
                        sp.wait_ge(est_lo, e * 6 + c)
                    w = (upT, gT, downT)[c // 2]
                    w = w[e] if isinstance(e, int) else w[bass.ds(e, 1)].rearrange("a p n -> (a p) n")
                    b = (c + 2 * (1 - par)) % 4
                    sp.dma_start(stage[b], w[:, c % 2 * 2048:(c % 2 + 1) * 2048]).then_inc(stage_in[b], 16)
            sp.wait_ge(est_hi, 9)
            sp.wait_ge(est_lo, 9)
            sp.wait_ge(base_out, 16 * NT)
            expert_chunks(1, 1)
            with sp.Fori(1, NX // 2) as i:
                for j in range(2):
                    expert_chunks(i * 2 + j, j)

        @block.gpsimd
        def _(pool):
            g = nc.gpsimd
            own = chain(pool, pool_own)
            own(g.memset(ident, 0.0))
            own(g.memset(ident32, 0.0))
            own(g.memset(tri, 1.0))
            own(g.affine_select(out=ident, in_=ident, compare_op=ALU.not_equal, fill=1.0, base=0,
                                pattern=[[-1, P]], channel_multiplier=1))
            g.affine_select(out=ident32, in_=ident32, compare_op=ALU.not_equal, fill=1.0, base=0,
                            pattern=[[-1, 16]], channel_multiplier=1).then_inc(consts, 1)
            g.affine_select(out=tri, in_=tri, compare_op=ALU.is_gt, fill=0.0, base=0,
                            pattern=[[1, P]], channel_multiplier=-1).then_inc(consts, 1)
            g.memset(ones16, 1.0).then_inc(consts, 1)
            g.memset(lane_ones, 1.0).then_inc(consts, 1)
            g.memset(key_ones, 1.0).then_inc(consts, 1)
            g.iota(iota16, pattern=[[1, P]], base=0, channel_multiplier=0,
                   allow_small_or_imprecise_dtypes=True).then_inc(consts, 1)
            g.iota(iota_g, pattern=[[1, NG]], base=0, channel_multiplier=0,
                   allow_small_or_imprecise_dtypes=True).then_inc(consts, 1)
            own(g.memset(rec0, 0))
            g.memset(rec0[:, :, 1:2], -1).then_inc(rec0_set, 1)
            pool.wait_ge(rec0_set, 1)
            pool.dma_start(rec_tab.rearrange("(p t) f -> p (t f)", p=P),
                           rec0.rearrange("p t f -> p (t f)")).then_inc(rec0_out, 16)
            pool.wait_ge(rec0_out, 16)
            pool.wait_ge(pos_set, 1)
            for c in range(ECOL):
                pool.indirect_dma_start(rec_tab, bass.IndirectOffsetOnAxis(e_row[:, c:c + 1], 0),
                                        e_rec[:, c, :], None).then_inc(rec_out, 16)
            pool.wait_ge(rec_out, 16 * ECOL)
            pool.dma_start(rec.rearrange("p t f -> p (t f)"),
                           rec_tab.rearrange("(p t) f -> p (t f)", p=P)).then_inc(rec_in, 16)
            pool.wait_ge(rinv_set, 1)
            pool.dma_start(rinv_tab.rearrange("(d p r) f -> p d (r f)", d=NT, p=P),
                           rinv.rearrange("p (d r) -> p d r", r=R)).then_inc(rinv_out, 16)
            pool.wait_ge(rinv_out, 16)
            for T in range(ST):
                pool.indirect_dma_start(s_all[:, T:T + 1], None, rinv_tab,
                                        bass.IndirectOffsetOnAxis(rec[:, T, 3:4], 0)).then_inc(s_in, 16)
            pool.wait_ge(y_out[0], 16 * R * 2 * 5)
            pool.wait_ge(y_out[1], 16 * R * 2 * 5)
            pool.wait_ge(tables_used, 1)
            for T in range(ST):
                if T >= 8:
                    pool.wait_ge(grp_done, NG + (T - 8) // 2 + 1)
                pool.indirect_dma_start(ring[:, T % 8].rearrange("p a n -> p (a n)"), None, y_tab,
                                        bass.IndirectOffsetOnAxis(rec[:, T, 0:1], 0)).then_inc(row_in[T % 8], 16)

            pool.wait_ge(acc_all, 1)
            def step(s, j, half):
                if there(s + 2) and s > -2:
                    t = s + 2
                    pool.wait_ge(u_hi, s + 3)
                    if s == -1:
                        pool.wait_ge(u_lo, 1)
                    g.tensor_tensor(out=up_pair[:, j, 1], in0=row(acc, t), in1=up_pair[:, j, 0],
                                    op=ALU.subtract).then_inc(u_lo, 1)
                if there(s + 1):
                    t = s + 1
                    pool.wait_ge(xn_set, s + (NT + 2))
                    g.tensor_tensor(out=xt2[:, 1 - j], in0=xt2[:, 1 - j], in1=xn2[:, 1 - j],
                                    op=ALU.add).then_inc(xx_set, 1)
                    pool.wait_ge(tanh_set, s + 2)
                    g.tensor_tensor(out=row(acc, t), in0=row(acc, t), in1=xn2[:, 1 - j],
                                    op=ALU.subtract).then_inc(d_set, 1)
                if there(s - 1):
                    t = s - 1
                    pool.wait_ge(h_hi, s)
                    g.tensor_tensor(out=h_pair[:, 1 - j, 1], in0=row(acc, t), in1=h_pair[:, 1 - j, 0],
                                    op=ALU.subtract).then_inc(h_lo, 1)
            steps(pool, step)

            def low(c):
                pool.wait_ge(est_hi, c + 4)
                w = ew[:, 0, :, c * 2048:(c + 1) * 2048]
                g.tensor_tensor(out=w[:, 1], in0=est[:, c % 2], in1=w[:, 0], op=ALU.subtract).then_inc(est_lo, 1)
            pool.wait_ge(db_hi, 1)
            g.tensor_tensor(out=db[32:32 + NX], in0=db32[32:32 + NX], in1=db[32:32 + NX], op=ALU.subtract).then_inc(db_lo, 1)
            pool.wait_ge(db_lo, 1)

            def shared_unit(i):
                pool.wait_ge(su_t, 3 * i + 3)
                pool.wait_ge(su_p, i + 1)
                t_ = s_t[:, i % 2]
                own(g.tensor_tensor(out=t_[:, 1], in0=t_[:, 0], in1=t_[:, 1], op=ALU.mult))
                g.tensor_tensor(out=t_[:, 1], in0=t_[:, 1], in1=t_[:, 2], op=ALU.mult).then_inc(su_a, 1)
                pool.wait_ge(sa_hi, i + 1)
                c, n = divmod(i, NP // TQ)
                g.tensor_tensor(out=sact[:, 1, c, n * TQ:(n + 1) * TQ], in0=t_[:, 1],
                                in1=sact[:, 0, c, n * TQ:(n + 1) * TQ], op=ALU.subtract).then_inc(sa_lo, 1)
            for i in range(SUNITS):
                shared_unit(i)
                if i < 6:
                    low(i)
            for i in range(2 * NT):
                t, h = divmod(i, 2)
                pool.wait_ge(sd_t, i + 1)
                a = zx[:, t, h * HALF:(h + 1) * HALF]
                g.tensor_tensor(out=a, in0=a, in1=sd_b[:, i % 2], op=ALU.add).then_inc(sd_set, 1)

            pool.wait_ge(h_out[0], 16 * NT // 2)
            pool.wait_ge(h_out[1], 16 * NT // 2)
            pool.wait_ge(su_done, SUNITS)
            pool.wait_ge(sc_done, NT)
            pool.wait_ge(idx_set, 4)

            def gather(e):
                if e >= 2:
                    pool.wait_ge(xgT_done, e - 1)
                for m, n in ((0, P), (1, REST)):
                    pool.indirect_dma_start(xg[0:n, e % 2, m].rearrange("p a n -> p (a n)"), None, h_tab,
                                            bass.IndirectOffsetOnAxis(idx[0:n, m, e:e + 1], 0)).then_inc(xg_in[e % 2], 16)
            gather(0)
            gather(1)
            for e in range(NX):
                if e == 0:
                    pool.wait_ge(base_out, 16 * NT)
                else:
                    pool.wait_ge(eo_out, 48 * e)
                for m, a, b in ((0, 0, P), (1, 0, REST), (1, REST, REST2)):
                    if a == 0:
                        pool.wait_ge((dn_a, dn_d)[m], 2 * e + 2)
                    else:
                        if e + 2 < NX:
                            gather(e + 2)
                        pool.wait_ge(eo_out, 48 * e + 32)
                    pool.indirect_dma_start(out, bass.IndirectOffsetOnAxis(idx[0:b - a, m, e:e + 1], 0),
                                            eo[a:b, e % 2, m], None, compute_op=ALU.add).then_inc(eo_out, 16)
            pool.wait_ge(eo_out, 48 * NX)

        @block.scalar
        def _(act):
            s = nc.scalar
            def split_high(ordinal, buf, q, b):
                act.wait_ge(wst_in[b], 16 * (ordinal + 1))
                ks = slice(q * CW, q * CW + CW) if isinstance(q, int) else bass.ds(q * CW, CW)
                s.activation(wb[:, buf, 0, ks, :], wst[:, b], ACT.Copy, scale=WSC).then_inc(w_hi, 1)

            def norm(t):
                if t % 2 == 0:
                    act.wait_ge(ln1_set, t // 2 + 1)
                wait(act, xn_lo, t - 1)
                wait(act, xt_done, t - 1)
                s.activation(xn32[:, t % 2], xin[:, t, :], ACT.Identity, scale=rstd[:, t:t + 1],
                             bias=nmr[:, t:t + 1]).then_inc(xn_set, 1)
                act.wait_ge(xn_set, t + 1)
                s.activation(xnp[:, t % 2, 0], xn32[:, t % 2], ACT.Copy).then_inc(xn_hi, 1)

            def evac_xT(t):
                act.wait_ge(xt_done, t + 1)
                s.activation(xT[:, 0, :, t * P:(t + 1) * P], PT[0].rearrange("p (k c) -> p k c", k=KD),
                             ACT.Copy).then_inc(xT_hi, 1)

            def evac_y(m, q, j):
                u = m * 10 + q * 2 + j
                act.wait_ge(unit_done, u + 1)
                wait(act, y_out[j], 16 * (m * 5 + q))
                s.activation(yst[:, j, 0], PU[j], ACT.Copy, scale=1.0 / WSC).then_inc(y_hi, 1)

            for n in range(2):
                split_high(n // 2, 0, n, n % 2)
            norm(0)
            norm(1)
            evac_xT(0)
            for n in range(2, CPH):
                split_high(n // 2, 0, n, n % 2)
            evac_xT(1)
            norm(2)
            for t in range(2, NT + 2):
                u = t - 2
                evac_y(0, u // 2, u % 2)
                if t < NT:
                    evac_xT(t)
                if t + 1 < NT:
                    norm(t + 1)
                if t % 2 and u // 2 < CPH:
                    split_high(2 + u // 4, 1, u // 2, u // 2 % 2)

            def rel_columns(Q, par):
                v_ = s_rel[:, Q * 8:Q * 8 + 8] if isinstance(Q, int) else s_rel[:, bass.ds(Q * 8, 8)]
                s.activation(rel8[:, par], v_, ACT.Copy).then_inc(rel8_set, 1)

            def scale_rows(Q, par, i):
                act.wait_ge(rel8_set, Q + 1)
                for st in range(2):
                    b = i * 2 + st
                    act.wait_ge(row_in[b], Q * 16 + 16)
                    for h in range(2):
                        act.wait_ge(row_set, Q * 16 + (b * 2 + h + 1))
                        s.activation(row_t[:, h], ring[:, b, 0, h * HALF:(h + 1) * HALF], ACT.Copy,
                                     scale=rel8[:, par, b:b + 1]).then_inc(row_scaled, 1)

            def body(mat, evac, halves=(0, 1)):
                for h in halves:
                    m = mat * 2 + h
                    def pair(q, qq, b):
                        if evac:
                            evac_y(m, q, 0)
                            evac_y(m, q, 1)
                        else:
                            Q = (m - 2 * R) * 5 + q
                            par = (h + (b or 0)) % 2
                            scale_rows(Q, par, 2)
                            scale_rows(Q, par, 3)
                            rel_columns(Q + 1, 1 - par)
                            act.wait_ge(unit_done, m * 10 + q * 2 + 1)
                        if b is not None and not (isinstance(m, int) and m + 1 >= HALVES):
                            split_high((m + 1) * 2 + qq, (h + 1) % 2, q, b)
                        if not evac:
                            scale_rows(Q + 1, 1 - par, 0)
                            scale_rows(Q + 1, 1 - par, 1)
                    with act.Fori(0, 2) as qq:
                        for b in range(2):
                            pair(qq * 2 + b, qq, b)
                    pair(4, 2, None)
            body(0, True, (1,))
            with act.Fori(1, R) as mat:
                body(mat, True)
            act.wait_ge(tables_used, 1)
            rel_columns(0, 0)
            scale_rows(0, 0, 0)
            scale_rows(0, 0, 1)
            body(R, False)
            body(R + 1, False, (0,))
            for n in range(REST_G):
                g_ = 4 * REST_Q + n + 2
                if g_ < NG:
                    if g_ % 4 == 0:
                        rel_columns(g_ // 4, g_ // 4 % 2)
                    scale_rows(g_ // 4, g_ // 4 % 2, g_ % 4)
                k = half_unit_at.get(n, 0)
                if k % 4 == 3 and k // 4 < CPH:
                    q = k // 4
                    act.wait_ge(unit_done, M_LAST * 10 + k // 2)
                    split_high((M_LAST + 1) * 2 + q // 2, 0, q, q % 2)
            def last_high(c):
                split_high((HALVES - 1) * 2 + c // 2, 1, c, c % 2)
            act.wait_ge(unit_done, M_GU * 10)
            last_high(0)
            last_high(1)

            act.wait_ge(acc_all, 1)
            def step(s_, j, half):
                def u_high():
                    wait(act, tu_done, s_ + 1)
                    s.activation(up_pair[:, j, 0], row(acc, s_ + 2), ACT.Copy).then_inc(u_hi, 1)
                if s_ == -1:
                    u_high()
                    last_high(2)
                if there(s_ + 1):
                    act.wait_ge(tu_done, s_ + 2)
                    wait(act, mm_done, s_)
                    for a in range(2):
                        ins = s.activation(uT[:, 1 - j, a], PT[a].rearrange("p (k c) -> p k c", k=KD), ACT.Copy)
                    ins.then_inc(uT_set, 1)
                if there(s_ + 2) and s_ != -1:
                    u_high()
                if there(s_ + 1):
                    t = s_ + 1
                    act.wait_ge(x2_in[1 - j], (half + (j + 1)) * 16)
                    wait(act, xx_set, s_)
                    wait(act, d_set, s_)
                    s.activation(xn2[:, 1 - j], xt2[:, 1 - j], ACT.Identity, scale=col(rstd, t),
                                 bias=col(nmr, t)).then_inc(xn_set, 1)
                    act.wait_ge(u_lo, s_ + 2)
                    s.activation(row(acc, t), row(acc, t), ACT.Tanh).then_inc(tanh_set, 1)
                if s_ == -1:
                    last_high(3)
                if there(s_ - 2):
                    act.wait_ge(th_done, s_ - 1)
                    for a in range(2):
                        ins = s.activation(cols(xT[:, a], (s_ - 2) * P, P), PT[a].rearrange("p (k c) -> p k c", k=KD),
                                           ACT.Copy)
                    ins.then_inc(hT_set, 1)
                if there(s_ - 1):
                    act.wait_ge(h_set, s_)
                    wait(act, th_done, s_ - 2)
                    wait(act, h_out[1 - j], (half + (j - 1)) * 16)
                    s.activation(h_pair[:, 1 - j, 0], row(acc, s_ - 1), ACT.Copy).then_inc(h_hi, 1)
            steps(act, step, -2, NT)
            act.wait_ge(mm_done, NT)
            act.wait_ge(sh_in, 48)
            for c in range(3):
                s.activation(sw[:, 0, c, :], sh_stage[:, c], ACT.Copy, scale=WSC).then_inc(est_hi, 1)
            steps(act, step, NT)

            def high(c):
                if c == 0:
                    act.wait_ge(est_lo, 3)
                act.wait_ge(est_in[c % 2], (c // 2 + 1) * 16)
                s.activation(est[:, c % 2], est[:, c % 2], ACT.Copy, scale=WSC).then_inc(est_sc, 1)
                act.wait_ge(est_sc, c + 1)
                s.activation(ew[:, 0, 0, c * 2048:(c + 1) * 2048], est[:, c % 2], ACT.Copy).then_inc(est_hi, 1)
            act.wait_ge(db_in, 16)
            s.activation(db32, db32, ACT.Copy, scale=WSC).then_inc(db_sc, 1)
            act.wait_ge(db_sc, 1)
            s.activation(db, db32, ACT.Copy).then_inc(db_hi, 1)
            act.wait_ge(sc_used, 1)
            s.activation(sc[:, 0:N], sc[:, 0:N], ACT.Tanh, scale=0.5).then_inc(tanh_sc, 1)
            act.wait_ge(tanh_sc, 1)
            s.activation(sc[:, 0:N], sc[:, 0:N], ACT.Identity, bias=1.0).then_inc(sig_set, 1)
            act.wait_ge(h_out[0], 16 * NT // 2)
            act.wait_ge(h_out[1], 16 * NT // 2)
            for i in range(SUNITS):
                act.wait_ge(su_done, i + 1)
                wait(act, sa_lo, i - 1)
                g_, u_ = PG[i % 2]
                t_ = s_t[:, i % 2]
                s.activation(t_[:, 0], g_[:, 0:TQ], ACT.Tanh, scale=0.5 / WSC).then_inc(su_t, 1)
                s.activation(t_[:, 1], g_[:, 0:TQ], ACT.Copy, scale=0.5 / WSC).then_inc(su_t, 1)
                s.activation(t_[:, 2], u_[:, 0:TQ], ACT.Copy, scale=1.0 / WSC).then_inc(su_t, 1)
                act.wait_ge(su_t, 3 * i + 1)
                s.activation(t_[:, 0], t_[:, 0], ACT.Identity, bias=1.0).then_inc(su_p, 1)
                if i < 6:
                    high(i)
                act.wait_ge(su_a, i + 1)
                c, n = divmod(i, NP // TQ)
                s.activation(sact[:, 0, c, n * TQ:(n + 1) * TQ], t_[:, 1], ACT.Copy).then_inc(sa_hi, 1)
            act.wait_ge(sa_lo, SUNITS)
            for i in range(2 * NT):
                act.wait_ge(sd_done, i + 1)
                wait(act, sd_set, i - 1)
                s.activation(sd_b[:, i % 2], PU[i % 2], ACT.Copy, scale=1.0 / WSC).then_inc(sd_t, 1)
            act.wait_ge(top_set, 1)
            s.activation(top_f[:, 1, 0:CAP], top_v[0:NX, 0:CAP], ACT.Tanh, scale=0.5)
            s.activation(top_f[:, 1, CAP:CAP + REST], top_v[0:NX, P:CAP], ACT.Tanh, scale=0.5).then_inc(topf_s, 1)
            act.wait_ge(mask_set, 1)
            act.wait_ge(sd_t, 2 * NT)
            act.wait_ge(sd_set, 2 * NT)
            s.activation(smask, sc_work, ACT.Copy).then_inc(mask_hi, 1)

            def evac_xg(e, par, pr=PR):
                act.wait_ge(xgT_done, e + 1)
                s.activation(xgT[:, par, 0, :, 0:P], PT[0].rearrange("p (k c) -> p k c", k=KD), ACT.Copy)
                s.activation(xgT[:, par, 0, :, P:CAP], pr[0][:, :, 0:REST], ACT.Copy).then_inc(xgT_hi, 1)

            def expert(e, par, half, last):
                def gate_up(j):
                    act.wait_ge(ug_done, e * 4 + (j + 1))
                    wait(act, a_lo, e * 4 + (j - 1))
                    ps = PG[0][j % 2]
                    b_g, b_u = of_expert(gbh, e, j), of_expert(ub_s, e, j)
                    s.activation(a_t[:, j % 2, 0, 0:CAP], ps[:, 160:160 + CAP], ACT.Tanh, scale=0.5 / WSC, bias=b_g)
                    s.activation(a_t[:, j % 2, 1, 0:CAP], ps[:, 160:160 + CAP], ACT.Identity, scale=0.5 / WSC, bias=b_g)
                    s.activation(a_t[:, j % 2, 2, 0:CAP], ps[:, 0:CAP], ACT.Identity, scale=1.0 / WSC,
                                 bias=b_u).then_inc(at_set, 1)
                def a_high(j):
                    act.wait_ge(a_set, e * 4 + (j + 1))
                    s.activation(a_pair[:, par, j, 0:CAP], a_t[:, j % 2, 3, 0:CAP], ACT.Copy).then_inc(a_hi, 1)
                def next_w(c):
                    if last:
                        return
                    if c == 0:
                        wait(act, dn_done, e * 4)
                    act.wait_ge(stage_in[(c + 2 * par) % 4], (half * 3 + ((c + 6 * par) // 4 + 1)) * 16)
                    s.activation(ew[:, 1 - par, 0, c * 2048:(c + 1) * 2048], stage[(c + 2 * par) % 4], ACT.Copy,
                                 scale=WSC).then_inc(est_hi, 1)
                s.activation(sco_e[:, par:par + 1], col(sco[:, 0], e), ACT.Copy).then_inc(sco_set, 1)
                for j in range(4):
                    gate_up(j)
                    if j < 3:
                        next_w(j)
                    a_high(j)
                if not last:
                    evac_xg(e + 1, 1 - par)
                act.wait_ge(sco_set, e + 1)
                next_w(3)
                for h in range(2):
                    act.wait_ge(dn_done, e * 4 + (h + 1))
                    wait(act, eo_out, e * 48 - 48)
                    s.activation(eo[:, par, 0, h * HALF:(h + 1) * HALF], PG[1][h], ACT.Copy,
                                 scale=sco_e[:, par:par + 1]).then_inc(dn_a, 1)
                next_w(4)
                next_w(5)
            act.wait_ge(idx_set, 4)
            evac_xg(0, 0, PR0)
            act.wait_ge(base_out, 16 * NT)
            experts(act, expert)

        @block.tensor
        def _(pe):
            mm = nc.tensor.matmul

            def product(ps, lhs, rhs, ks, first=True, last=True):
                ks = range(ks) if isinstance(ks, int) else ks
                for i, k in enumerate(ks):
                    for a, b in ((0, 0), (0, 1), (1, 0)):
                        ins = mm(ps, lhs(a, k), rhs(b, k), start=first and i == 0 and (a, b) == (0, 0),
                                 stop=last and i == len(ks) - 1 and (a, b) == (1, 0))
                return ins

            def half_unit(m, h, q, j, part):
                if part == 0:
                    pe.wait_ge(w_hi, m * CPH + CPH)
                    pe.wait_ge(w_lo, m * CPH + CPH)
                    pe.wait_ge(pu_free[j], m * 5 + q + 1)
                first = (q * 2 + j) * P
                ins = product(PU[j], lambda a, k: cols(xT[:, a, k, :], first, P), lambda b, k: wb[:, h, b, k, :],
                              range(part * KD // 2, (part + 1) * KD // 2), first=part == 0, last=part == 1)
                if part == 1:
                    ins.then_inc(unit_done, 1)

            def unit(m, h, q, j, between=None):
                half_unit(m, h, q, j, 0)
                if between:
                    between()
                half_unit(m, h, q, j, 1)

            def count_group(Q, i):
                pe.wait_ge(st_set, Q * 4 + i + 1)
                pe.wait_ge(pg_free[i % 2], Q * 2 + (i // 2 + 1))
                for s in range(2):
                    ins = mm(PG[i % 2][0][:, 0:R], stile[:, i * 2 + s], cols_t(is_type, Q * 8 + i * 2 + s),
                             start=s == 0, stop=s == 1)
                ins.then_inc(grp_done, 1)

            def cols_t(v, T):
                return v[:, T, :] if isinstance(T, int) else v[:, bass.ds(T, 1), :].rearrange("p a n -> p (a n)")

            def sum_group(Q, i):
                pe.wait_ge(st_set, Q * 4 + (NG + i + 1))
                pe.wait_ge(pg_free[i % 2], Q * 2 + (NG // 2 + i // 2 + 1))
                pe.wait_ge(row_set, Q * 16 + (i * 4 + 6))
                for h in range(2):
                    for s in range(2):
                        b = i * 2 + s
                        for c in range(2):
                            ins = mm(PG[i % 2][h], stile[:, b], ring[:, b, c, h * HALF:(h + 1) * HALF],
                                     start=s == 0 and c == 0, stop=s == 1 and c == 1)
                ins.then_inc(grp_done, 1)

            def body(mat, group=None, m0=0, halves=(0, 1), last_quads=False):
                for h in halves:
                    m = mat * 2 + h
                    def pair(q, group=group):
                        for j in range(2):
                            if group:
                                unit(m, h, q, j, lambda: group((m - m0) * 5 + q, 2 * j))
                                group((m - m0) * 5 + q, 2 * j + 1)
                            else:
                                unit(m, h, q, j)
                    if last_quads:
                        for q in range(5):
                            pair(q, group if (m - m0) * 5 + q < QUADS else None)
                        continue
                    with pe.Fori(0, 2) as qq:
                        for b in range(2):
                            pair(qq * 2 + b)
                    pair(4)

            pe.wait_ge(consts, 7)
            def transpose_x(t):
                pe.wait_ge(xn_hi, t + 1)
                pe.wait_ge(xn_lo, t + 1)
                wait(pe, xT_hi, t)
                wait(pe, xT_lo, t)
                for a in range(2):
                    for k in range(KD):
                        ins = nc.tensor.transpose(PT[a][:, k * P:(k + 1) * P],
                                                  xnp[:, t % 2, a, k * P:(k + 1) * P], ident)
                ins.then_inc(xt_done, 1)
            def first_unit(t):
                pe.wait_ge(xT_hi, t + 1)
                pe.wait_ge(xT_lo, t + 1)
                unit(0, 0, t // 2, t % 2)
            transpose_x(0)
            for t in range(1, NT):
                transpose_x(t)
                first_unit(t - 1)
            first_unit(NT - 1)
            pe.wait_ge(tot_set, 1)
            mm(PG[0][0][:, 0:NT], tri[0:EPART], tot16[0:EPART, 0:NT], start=True, stop=True)
            mm(PG[0][0][:, 16:16 + NT], ones16[0:EPART], tot16[0:EPART, 0:NT],
               start=True, stop=True).then_inc(prefix_done, 1)
            body(0, halves=(1,))
            with pe.Fori(1, COUNT_MAT) as mat:
                body(mat)
            with pe.Fori(COUNT_MAT, COUNT_MAT + 2) as mat:
                body(mat, count_group, COUNT_MAT * 2)
            body(COUNT_MAT + 2, count_group, COUNT_MAT * 2, halves=(0,), last_quads=True)
            body(COUNT_MAT + 2, halves=(1,))
            with pe.Fori(COUNT_MAT + 3, R) as mat:
                body(mat)
            body(R, sum_group, 2 * R)
            body(R + 1, sum_group, 2 * R, halves=(0,))
            for n in range(REST_G):
                if n in half_unit_at:
                    t, part = divmod(half_unit_at[n], 2)
                    half_unit(M_LAST, 1, t // 2, t % 2, part)
                sum_group(REST_Q + n // 4, n % 4)

            pe.wait_ge(acc_all, 1)
            pe.wait_ge(w_hi, (HALVES - 1) * CPH)
            pe.wait_ge(w_lo, (HALVES - 1) * CPH)
            def transpose_pair(pair):
                for a in range(2):
                    for k in range(KD):
                        ins = nc.tensor.transpose(PT[a][:, k * P:(k + 1) * P], pair[:, a, k * P:(k + 1) * P], ident)
                return ins
            def step(s, j, half):
                def transpose_u():
                    pe.wait_ge(u_hi, s + 2)
                    pe.wait_ge(u_lo, s + 2)
                    wait(pe, hT_set, s - 2)
                    transpose_pair(up_pair[:, 1 - j]).then_inc(tu_done, 1)
                if there(s + 1) and s:
                    transpose_u()
                def gate_half(h):
                    if h == 0:
                        pe.wait_ge(uT_set, s + 1)
                        wait(pe, z_set, s - 1)
                    elif s == 0:
                        pe.wait_ge(w_hi, HALVES * CPH)
                        pe.wait_ge(w_lo, HALVES * CPH)
                    return product(PG[j][h], lambda a, k: uT[:, j, a, k, :], lambda b, k: wb[:, h, b, k, :], KD)
                if there(s):
                    gate_half(0)
                if s == 0:
                    transpose_u()
                if there(s - 2):
                    pe.wait_ge(h_hi, s - 1)
                    pe.wait_ge(h_lo, s - 1)
                    if there(s + 1):
                        pe.wait_ge(uT_set, s + 2)
                    wait(pe, hT_set, s - 2)
                    transpose_pair(h_pair[:, j]).then_inc(th_done, 1)
                if there(s):
                    gate_half(1).then_inc(mm_done, 1)
                if there(s - 2):
                    pe.wait_ge(hT_set, s - 1)
                    wait(pe, sc_set, s - 2)
                    pe.wait_ge(gw_lo, 2)
                    product(PU[0][0:TRIO, 0:P], lambda a, k: gw[:, a, k, :],
                            lambda b, k: cols(xT[:, b, k, :], (s - 2) * P, P), KD).then_inc(sc_done, 1)
            steps(pe, step)

            pe.wait_ge(est_hi, 2)
            pe.wait_ge(est_lo, 2)
            pe.wait_ge(sc_set, NT)
            for i in range(SUNITS):
                c, n = divmod(i, NP // TQ)
                wait(pe, su_t, 3 * (i - 1))
                for w in range(2):
                    ins = product(PG[i % 2][w][:, 0:TQ], lambda a, k: sw[:, a, w, k * SH + c * P:k * SH + (c + 1) * P],
                                  lambda b, k: xT[:, b, k, n * TQ:(n + 1) * TQ], KD)
                ins.then_inc(su_done, 1)
            pe.wait_ge(est_hi, 3)
            pe.wait_ge(est_lo, 3)
            for i in range(2 * NT):
                t, h = divmod(i, 2)
                pe.wait_ge(sa_hi, SUNITS - NP // TQ + (t * P // TQ + 1))
                pe.wait_ge(sa_lo, SUNITS - NP // TQ + (t * P // TQ + 1))
                wait(pe, sd_t, i - 1)
                product(PU[i % 2], lambda a, k: sact[:, a, k, t * P:(t + 1) * P],
                        lambda b, k: sw[:, b, 2, k * D + h * HALF:k * D + (h + 1) * HALF], KS).then_inc(sd_done, 1)
            pe.wait_ge(topf_i, 1)
            pe.wait_ge(topf_s, 1)
            for w in range(2):
                nc.tensor.transpose(PG[1][0][:, w * 32:w * 32 + NX], top_f[:, w, 0:P], ident32)
                ins = nc.tensor.transpose(PG[1][0][0:REST2, w * 32 + NX:w * 32 + 2 * NX], top_f[:, w, P:P + REST2], ident32)
            ins.then_inc(topT_done, 1)
            pe.wait_ge(db_hi, 1)
            pe.wait_ge(db_lo, 1)
            pe.wait_ge(mask_hi, 1)
            pe.wait_ge(mask_lo, 1)
            def transpose_rows(e, par, half, pr=PR):
                pe.wait_ge(xg_in[par], half * 32 + 32)
                wait(pe, xgT_hi, e)
                wait(pe, xgT_lo, e)
                wait(pe, dn_d, 2 * e - 2)
                for a in range(2):
                    for k in range(KD):
                        nc.tensor.transpose(PT[a][:, k * P:(k + 1) * P], xg[:, par, 0, a, k * P:(k + 1) * P], ident)
                        ins = nc.tensor.transpose(pr[a][:, k, 0:REST], xg[0:REST, par, 1, a, k * P:(k + 1) * P],
                                                  ident[0:REST, 0:REST])
                ins.then_inc(xgT_done, 1)

            def expert(e, par, half, last):
                pe.wait_ge(xgT_hi, e + 1)
                pe.wait_ge(xgT_lo, e + 1)
                pe.wait_ge(est_hi, e * 6 + 7)
                pe.wait_ge(est_lo, e * 6 + 7)
                for j in range(4):
                    wait(pe, at_set, e * 4 + (j - 1))
                    for w in range(2):
                        ins = product(PG[0][j % 2][:, w * 160:w * 160 + CAP],
                                      lambda a, k: ew[:, par, a, w * 4096 + k * F + j * P:w * 4096 + k * F + (j + 1) * P],
                                      lambda b, k: xgT[:, par, b, k, 0:CAP], KD)
                    ins.then_inc(ug_done, 1)
                if not last:
                    transpose_rows(e + 1, 1 - par, half + par)
                pe.wait_ge(est_hi, e * 6 + 9)
                pe.wait_ge(est_lo, e * 6 + 9)
                def down(h, ks, **ends):
                    return product(PG[1][h], lambda a, k: a_pair[:, par, k, a * A_LOW:a * A_LOW + P],
                                   lambda b, k: ew[:, par, b, 8192 + k * D + h * HALF:8192 + k * D + (h + 1) * HALF],
                                   ks, **ends)
                pe.wait_ge(a_hi, e * 4 + 3)
                pe.wait_ge(a_lo, e * 4 + 3)
                for h in range(2):
                    wait(pe, dn_a, e * 2 + (h - 1))
                    down(h, range(KF - 1), last=False)
                pe.wait_ge(a_hi, e * 4 + 4)
                pe.wait_ge(a_lo, e * 4 + 4)
                for h in range(2):
                    down(h, range(KF - 1, KF), first=False).then_inc(dn_done, 1)
                if not last:
                    pe.wait_ge(xgT_hi, e + 2)
                    pe.wait_ge(xgT_lo, e + 2)
                for h in range(2):
                    def rest(k, w, rows):
                        first = 8192 + k * D + h * HALF
                        return mm(PU[h][0:rows], a_pair[:, par, k, P:P + rows], ew[:, par, w, first:first + HALF],
                                  start=(k, w) == (0, 0), stop=(k, w) == (KF - 1, 0))
                    for k in range(KF - 1):
                        rest(k, 0, REST2)
                        rest(k, 1, REST)
                    rest(KF - 1, 1, REST)
                    rest(KF - 1, 0, REST2).then_inc(dn_done, 1)
            pe.wait_ge(sd_t, 2 * NT)
            for i in range(2 * NT):
                t, h = divmod(i, 2)
                wait(pe, base_set, i - 1)
                mm(PU[i % 2], smask[:, t * P:(t + 1) * P], db[:, h * HALF:(h + 1) * HALF],
                   start=True, stop=True).then_inc(base_done, 1)
                if i == 5:
                    transpose_rows(0, 0, 0, PR0)
            pe.wait_ge(base_set, 2 * NT)
            experts(pe, expert)

        @block.vector
        def _(dve_):
            v = nc.vector
            link = chain(dve_, dve)
            for bank in (*pu_free, *pg_free):
                dve_.sem_inc(bank, 1)
            dve_.sem_inc(row_set, 2)
            def newton(link, y, t, ve, var):
                link(v.tensor_scalar(ve, var, EPS, None, ALU.add))
                link(v.tensor_single_scalar(t.bitcast(I32), ve.bitcast(I32), 1, op=ALU.arith_shift_right))
                link(v.tensor_scalar(y.bitcast(I32), t.bitcast(I32), -1.0, float(0x5F3759DF), ALU.mult, ALU.add))
                for _ in range(3):
                    link(v.tensor_tensor(t, y, y, ALU.mult))
                    link(v.scalar_tensor_tensor(out=t, in0=t, scalar=-0.5, in1=ve, op0=ALU.mult, op1=ALU.mult))
                    link(v.scalar_tensor_tensor(out=y, in0=t, scalar=1.5, in1=y, op0=ALU.add, op1=ALU.mult))

            def split(m1, buf, q, b):
                dve_.wait_ge(w_hi, m1 * CPH + q + 1)
                ks = slice(q * CW, q * CW + CW) if isinstance(q, int) else bass.ds(q * CW, CW)
                v.scalar_tensor_tensor(out=wb[:, buf, 1, ks, :], in0=wst[:, b], scalar=WSC, in1=wb[:, buf, 0, ks, :],
                                       op0=ALU.mult, op1=ALU.subtract).then_inc(w_lo, 1)

            def x_stats(t):
                dve_.wait_ge(x_in[t], 16)
                v.bn_stats(stats[:, t % 2, 0, :], xin[:, t, 0:HALF])
                link(v.bn_stats(stats[:, t % 2, 1, :], xin[:, t, HALF:D]))
                link(v.bn_aggr(mv[:, t, :], stats[:, t % 2].rearrange("p a b -> p (a b)")))

            def x_rstd(c):
                two = slice(2 * c, 2 * c + 2)
                newton(link, rstd[:, two], nr_t[:, two], nr_y[:, two], mv[:, two, 1])
                v.scalar_tensor_tensor(out=nmr[:, two], in0=mv[:, two, 0], scalar=-1.0, in1=rstd[:, two],
                                       op0=ALU.mult, op1=ALU.mult).then_inc(ln1_set, 1)

            def norm_low(t):
                dve_.wait_ge(xn_hi, t + 1)
                wait(dve_, xt_done, t - 1)
                v.tensor_tensor(xnp[:, t % 2, 1], xn32[:, t % 2], xnp[:, t % 2, 0], ALU.subtract).then_inc(xn_lo, 1)

            def evac_xT(t):
                dve_.wait_ge(xt_done, t + 1)
                v.tensor_copy(xT[:, 1, :, t * P:(t + 1) * P],
                              PT[1].rearrange("p (k c) -> p k c", k=KD)).then_inc(xT_lo, 1)

            def evac_y(m, t, j):
                dve_.wait_ge(y_hi, m * 10 + t + 1)
                v.scalar_tensor_tensor(out=yst[:, j, 1], in0=PU[j], scalar=1.0 / WSC, in1=yst[:, j, 0],
                                       op0=ALU.mult, op1=ALU.subtract).then_inc(pu_free[j], 1)

            def edge_keys():
                dve_.wait_ge(edges_in, 48)
                dve_.wait_ge(consts, 7)
                v.tensor_single_scalar(e_key, e_dst, 7, op=ALU.arith_shift_right)
                v.tensor_single_scalar(e_lane, e_dst, P - 1, op=ALU.bitwise_and)
                v.scalar_tensor_tensor(out=e_rec[:, :, 0], in0=e_typ, scalar=float(NP), in1=e_src,
                                       op0=ALU.mult, op1=ALU.add)
                v.scalar_tensor_tensor(out=e_rec[:, :, 3], in0=e_dst, scalar=float(R), in1=e_typ,
                                       op0=ALU.mult, op1=ALU.add)
                link(v.tensor_copy(e_rec[:, :, 2], e_typ))
                v.tensor_copy(e_rec[:, :, 1], e_lane)
                for k in range(NT):
                    v.tensor_scalar(e_is[:, k, :], e_key, float(k), None, ALU.is_equal)
                link(v.memset(tot16[:, :], 0.0))

            def edge_counts():
                for k in range(NT):
                    last = v.tensor_tensor_scan(e_cum[:, k, :], lane_ones, e_is[:, k, :], 0.0, ALU.mult, ALU.add)
                link(last)
                v.tensor_copy(tot16[0:EPART, 0:NT], e_cum[:, :, ECOL - 1]).then_inc(tot_set, 1)

            def edge_offsets():
                dve_.wait_ge(prefix_done, 1)
                link(v.tensor_scalar(toti, PG[0][0][:, 16:16 + NT], float(GROUP - 1), None, ALU.add))
                link(v.tensor_single_scalar(toti, toti, 8, op=ALU.arith_shift_right))
                link(v.tensor_copy(tot[:, 0, :], toti))
                link(v.tensor_tensor_scan(tot[:, 1, :], key_ones, tot[:, 0, :], 0.0, ALU.mult, ALU.add))
                link(v.tensor_tensor(tot[:, 2, :], tot[:, 1, :], tot[:, 0, :], ALU.subtract))
                link(v.scalar_tensor_tensor(out=tot[:, 3, :], in0=tot[:, 2, :], scalar=float(GROUP),
                                            in1=PG[0][0][:, 0:NT], op0=ALU.mult, op1=ALU.add))
                link(v.tensor_scalar(tot[:, 2, :], tot[:, 3, :], -1.0, None, ALU.add))

            def edge_places():
                for k in range(NT):
                    last = v.scalar_tensor_tensor(out=e_cum[:, k, :], in0=e_cum[:, k, :],
                                                  scalar=tot[0:EPART, 2, k:k + 1], in1=e_is[:, k, :],
                                                  op0=ALU.add, op1=ALU.mult)
                link(last)

            def edge_rows():
                link(v.tensor_reduce(out=e_posf, in_=e_cum.rearrange("p k t -> p t k"), op=ALU.add, axis=AX_X))
                link(v.tensor_copy(e_pos, e_posf))
                v.tensor_single_scalar(e_lane, e_pos, P - 1, op=ALU.bitwise_and)
                link(v.tensor_single_scalar(e_tile, e_pos, 7, op=ALU.arith_shift_right))
                v.scalar_tensor_tensor(out=e_row, in0=e_lane, scalar=float(ST), in1=e_tile,
                                       op0=ALU.mult, op1=ALU.add).then_inc(pos_set, 1)

            def edge_groups():
                link(v.tensor_scalar(gmapf, iota_g, tot[0:1, 1, 0:1], None, ALU.is_ge))
                for k in range(1, NT):
                    link(v.scalar_tensor_tensor(out=gmapf, in0=iota_g, scalar=tot[0:1, 1, k:k + 1], in1=gmapf,
                                                op0=ALU.is_ge, op1=ALU.add))
                link(v.tensor_scalar(gmap, gmapf, float(NT - 1), None, ALU.min))

            def count_tiles(Q, i):
                wait(dve_, grp_done, (Q - 1) * 4 + i + 1)
                for s in range(2):
                    ins = v.tensor_scalar(stile[:, i * 2 + s], iota16, col(dloc, Q * 8 + i * 2 + s), None, ALU.is_equal)
                ins.then_inc(st_set, 1)

            def sum_tiles(Q, i):
                if not (isinstance(Q, int) and Q == 0):
                    dve_.wait_ge(grp_done, (Q - 1) * 4 + (NG + i + 1))
                for s in range(2):
                    T = Q * 8 + i * 2 + s
                    ins = v.tensor_scalar(stile[:, i * 2 + s], iota16, col(dloc, T), col(s_all, T), ALU.is_equal, ALU.mult)
                ins.then_inc(st_set, 1)

            def add_rows(Q, i, tiles=(0, 1)):
                for s in tiles:
                    b = i * 2 + s
                    for h in range(2):
                        dve_.wait_ge(row_scaled, Q * 16 + (b * 2 + h + 1))
                        low = ring[:, b, 1, h * HALF:(h + 1) * HALF]
                        v.tensor_tensor(low, low, row_t[:, h], ALU.add).then_inc(row_set, 1)

            def next_rows(Q, i, s):
                if i < 2:
                    add_rows(Q, i + 2, (s,))
                else:
                    add_rows(Q + 1, i - 2, (s,))

            def tile_of(Q, i):
                g_ = Q * 4 + i
                return v.value_load(gmap[0:1, g_:g_ + 1] if isinstance(g_, int) else gmap[0:1, bass.ds(g_, 1)],
                                    min_val=0, max_val=NT - 1)

            def count_add(Q, i):
                dve_.wait_ge(grp_done, Q * 4 + i + 1)
                dve_.wait_ge(pg_free[(i - 1) % 2], Q * 2 + ((i + 1) // 2 + 1))
                d = tile_of(Q, i)
                c = cnt[:, bass.ds(d * R, R)]
                v.tensor_tensor(c, PG[i % 2][0][:, 0:R], c, ALU.add).then_inc(pg_free[i % 2], 1)

            def sum_add(Q, i):
                dve_.wait_ge(grp_done, Q * 4 + (NG + i + 1))
                dve_.wait_ge(pg_free[(i - 1) % 2], Q * 2 + (NG // 2 + (i + 1) // 2 + 1))
                d = tile_of(Q, i)
                for h in range(2):
                    a = acc[:, bass.ds(d, 1), h * HALF:(h + 1) * HALF].rearrange("p a n -> p (a n)")
                    ins = v.scalar_tensor_tensor(out=a, in0=PG[i % 2][h], scalar=1.0 / SSC, in1=a, op0=ALU.mult, op1=ALU.add)
                ins.then_inc(pg_free[i % 2], 1)

            def half_row(x_, t, h):
                return row(x_, t)[:, h * HALF:(h + 1) * HALF]

            x_stats(0)
            x_stats(1)
            x_rstd(0)
            for n in range(2):
                split(0, 0, n, n % 2)
            norm_low(0)
            norm_low(1)
            evac_xT(0)
            x_stats(2)
            for n in range(2, CPH):
                split(0, 0, n, n % 2)
            evac_xT(1)
            x_stats(3)
            x_rstd(1)
            norm_low(2)
            x_stats(4)
            x_stats(5)
            for t in range(2, NT + 2):
                u = t - 2
                evac_y(0, u, u % 2)
                if t < NT:
                    evac_xT(t)
                if t + 1 < NT:
                    norm_low(t + 1)
                if t % 2 == 0 and t + 2 < NT:
                    x_rstd(t // 2 + 1)
                if t % 2 == 1 and t + 4 < NT:
                    x_stats(t + 3)
                    x_stats(t + 4)
                if t % 2 and u // 2 < CPH:
                    split(1, 1, u // 2, u // 2 % 2)
                if t == NT - 3:
                    edge_keys()
                if t == NT - 2:
                    edge_counts()
            for t in range(NT):
                evac_y(1, t, t % 2)
                if t == 0:
                    edge_offsets()
                elif t == 1:
                    edge_places()
                elif t == 2:
                    edge_rows()
                elif t == 4:
                    edge_groups()
                if t % 2 and t // 2 < CPH:
                    split(2, 0, t // 2, t // 2 % 2)
            dve_.wait_ge(small_in, 32)
            v.tensor_scalar(gbh, gb_s, 0.5, None, ALU.mult).then_inc(gw_lo, 1)


            def body(mat, kind, group=None, tiles=None, m0=0, halves=(0, 1), last_quads=False):
                for h in halves:
                    m = mat * 2 + h
                    def unit(q, j):
                        t = q * 2 + j
                        if kind == "y":
                            evac_y(m, t, j)
                        elif kind == "root":
                            dve_.wait_ge(unit_done, m * 10 + t + 1)
                            dve_.wait_ge(pg_free[0], ((m - m0) * 5 + q) * 2 + (NG // 2 + j + 2))
                            a = half_row(acc, t, h)
                            v.scalar_tensor_tensor(out=a, in0=PU[j], scalar=1.0 / WSC, in1=a,
                                                   op0=ALU.mult, op1=ALU.add).then_inc(pu_free[j], 1)
                            dve_.wait_ge(pu_free[j], m * 5 + q + 2)
                        else:
                            dve_.wait_ge(unit_done, m * 10 + t + 1)
                            v.scalar_tensor_tensor(out=half_row(zx, t, h), in0=PU[j], scalar=1.0 / WSC,
                                                   in1=bgate[:, h * HALF:(h + 1) * HALF],
                                                   op0=ALU.mult, op1=ALU.add).then_inc(pu_free[j], 1)
                    def pair(q, b, group=group):
                        for j in range(2):
                            def of_group(i):
                                Q = (m - m0) * 5 + q
                                if kind != "y":
                                    next_rows(Q, i, 0)
                                group(Q, i)
                                if kind != "y":
                                    next_rows(Q, i, 1)
                                if not isinstance(Q, int) or Q + 1 < QUADS:
                                    tiles(Q + 1, i)
                            if group:
                                of_group(2 * j)
                            unit(q, j)
                            if group:
                                of_group(2 * j + 1)
                        if b is not None and not (isinstance(m, int) and m + 1 >= HALVES):
                            split(m + 1, (h + 1) % 2, q, b)
                    if last_quads:
                        for q in range(5):
                            pair(q, q % 2 if q < 4 else None, group if (m - m0) * 5 + q < QUADS else None)
                        continue
                    with dve_.Fori(0, 2) as qq:
                        for b in range(2):
                            pair(qq * 2 + b, b)
                    pair(4, None)


            with dve_.Fori(1, COUNT_MAT) as mat:
                body(mat, "y")
            dve_.wait_ge(rec_in, 16)
            v.memset(cnt, 0.0)
            v.tensor_copy(dloc, rec[:, :, 1])
            link(v.tensor_copy(etf, rec[:, :, 2]))
            for r in range(R):
                last = v.tensor_scalar(is_type[:, :, r], etf, float(r), None, ALU.is_equal)
            link(last)
            for i in range(4):
                count_tiles(0, i)
            with dve_.Fori(COUNT_MAT, COUNT_MAT + 2) as mat:
                body(mat, "y", count_add, count_tiles, COUNT_MAT * 2)
            body(COUNT_MAT + 2, "y", count_add, count_tiles, COUNT_MAT * 2, halves=(0,), last_quads=True)
            dve_.wait_ge(pg_free[0], NG // 2 + 1)
            dve_.wait_ge(pg_free[1], NG // 2 + 1)
            link(v.tensor_scalar(cnt, cnt, 1.0, None, ALU.max))
            link(v.reciprocal(rinv, cnt))
            v.tensor_scalar(rinv, rinv, SSC, None, ALU.mult).then_inc(rinv_set, 1)
            body(COUNT_MAT + 2, "y", halves=(1,))
            with dve_.Fori(COUNT_MAT + 3, R) as mat:
                body(mat, "y")
            dve_.wait_ge(s_in, 16 * ST)
            link(v.tensor_copy(s_h16, s_all))
            link(v.reciprocal(s_rec, s_h16))
            link(v.tensor_tensor(s_rel, s_all, s_h16, ALU.subtract))
            link(v.tensor_tensor(s_rel, s_rel, s_rec, ALU.mult))
            dve_.sem_inc(tables_used, 1)
            dve_.wait_ge(bgate_in, 16)
            dve_.wait_ge(bias_in, 16 * NT)
            for i in range(4):
                sum_tiles(0, i)
            add_rows(0, 0)
            add_rows(0, 1)
            body(R, "root", sum_add, sum_tiles, 2 * R)
            body(R + 1, "gx", sum_add, sum_tiles, 2 * R, halves=(0,))
            for n in range(REST_G):
                Q, i = REST_Q + n // 4, n % 4
                k = half_unit_at.get(n, 0)
                if k % 2:
                    t = k // 2
                    dve_.wait_ge(unit_done, M_LAST * 10 + t + 1)
                    v.scalar_tensor_tensor(out=half_row(zx, t, 1), in0=PU[t % 2], scalar=1.0 / WSC,
                                           in1=bgate[:, HALF:D], op0=ALU.mult, op1=ALU.add).then_inc(pu_free[t % 2], 1)
                rows = n + 2 < REST_G
                if rows:
                    next_rows(Q, i, 0)
                if n == REST_G - 1:
                    split(HALVES - 1, 1, 0, 0)
                sum_add(Q, i)
                if rows:
                    next_rows(Q, i, 1)
                if Q + 1 < QUADS:
                    sum_tiles(Q + 1, i)
                if k % 4 == 3 and k // 4 < CPH:
                    split(M_LAST + 1, 0, k // 4, k // 4 % 2)
            dve_.wait_ge(pg_free[0], NG + 1)
            dve_.wait_ge(pg_free[1], NG + 1)
            dve_.sem_inc(acc_all, 1)
            dve_.wait_ge(u_hi, 1)
            v.tensor_tensor(up_pair[:, 0, 1], acc[:, 0, :], up_pair[:, 0, 0], ALU.subtract).then_inc(u_lo, 1)
            for c in range(1, CPH):
                split(HALVES - 1, 1, c, c % 2)
            dve_.wait_ge(gw_in, 16)
            link(v.tensor_scalar(gw[:, 0], gw32, WSC, None, ALU.mult))
            v.scalar_tensor_tensor(out=gw[:, 1], in0=gw32, scalar=WSC, in1=gw[:, 0], op0=ALU.mult, op1=ALU.subtract).then_inc(gw_lo, 1)
            GATE_LINKS = 3 + 3 + 9 + 1
            def step(s, j, half):
                if there(s - 2):
                    dve_.wait_ge(sc_done, s - 1)
                    c = cols(sc, (s - 2) * P, P)
                    v.tensor_scalar(c, PU[0][0:TRIO, 0:P], 1.0 / WSC, 17.0, ALU.mult, ALU.min).then_inc(sc_set, 1)
                if there(s):
                    gate = chain(dve_, dve_gate, s * GATE_LINKS)
                    dve_.wait_ge(mm_done, s + 1)
                    for h in range(2):
                        zh = half_row(zx, s, h)
                        ins = v.scalar_tensor_tensor(out=zh, in0=PG[j][h], scalar=1.0 / WSC, in1=zh,
                                                     op0=ALU.mult, op1=ALU.add)
                    ins.then_inc(z_set, 1)
                    dve_.wait_ge(z_set, s + 1)
                    dve_.wait_ge(d_set, s + 1)
                    gate(v.tensor_tensor(row(acc, s), row(zx, s), row(acc, s), ALU.mult))
                    dve_.wait_ge(xx_set, s + 1)
                    v.tensor_tensor(row(zx, s), row(acc, s), xt2[:, j], ALU.add).then_inc(x1_set, 1)
                    dve_.wait_ge(x1_set, s + 1)
                    for h in range(2):
                        ins = v.bn_stats(stats[:, j, h, :], half_row(zx, s, h))
                    gate(ins)
                    gate(v.bn_aggr(mv2, stats[:, j].rearrange("p a b -> p (a b)")))
                    newton(gate, ln2[:, j, 0:1], nr2[:, 0:1], nr2[:, 1:2], mv2[:, 1:2])
                    gate(v.scalar_tensor_tensor(out=ln2[:, j, 1:2], in0=mv2[:, 0:1], scalar=-1.0, in1=ln2[:, j, 0:1],
                                                op0=ALU.mult, op1=ALU.mult))
                    v.tensor_scalar(row(acc, s), row(zx, s), ln2[:, j, 0:1], ln2[:, j, 1:2],
                                    ALU.mult, ALU.add).then_inc(h_set, 1)
                    assert gate.count[0] == GATE_LINKS
            steps(dve_, step, -2, NT + 1)
            for c in range(3):
                dve_.wait_ge(est_hi, c + 1)
                v.scalar_tensor_tensor(out=sw[:, 1, c, :], in0=sh_stage[:, c], scalar=WSC, in1=sw[:, 0, c, :],
                                       op0=ALU.mult, op1=ALU.subtract).then_inc(est_lo, 1)
            steps(dve_, step, NT + 1)

            dve_.wait_ge(sc_set, NT)
            link(v.tensor_scalar(sc, sc, -104.0, None, ALU.max))
            for i in range(TOP8):
                src_ = sc if i == 0 else sc_work
                eight = slice(i * 8, i * 8 + 8)
                link(v.max(top_v[:, eight], src_[:, 0:N]))
                link(v.max_index(top_i[:, eight], top_v[0:NX, eight], src_[0:NX, 0:N]))
                if i < TOP8 - 1:
                    link(v.match_replace(sc_work[:, 0:N], top_v[:, eight], src_[:, 0:N], MARK))
                if i == 0:
                    dve_.sem_inc(sc_used, 1)
            v.memset(top_f[:, 0], 0.0)
            over = TOP8 * 8 - CAP
            v.memset(sc_work[:, N:N + over], -MARK)
            link(v.tensor_copy(top_8, top_v[:, (TOP8 - 1) * 8:TOP8 * 8]))
            link(v.memset(top_8[:, 8 - over:8], -MARK))
            link(v.match_replace(sc_work[:, 0:N + over], top_8, sc_work[:, 0:N + over], MARK))
            v.tensor_copy(top_f[:, 0, 0:CAP], top_i[:, 0:CAP])
            v.tensor_copy(top_f[:, 0, CAP:CAP + REST], top_i[:, P:CAP]).then_inc(topf_i, 1)
            link(v.memset(sc_work[:, N:NP], 0.0))
            dve_.sem_inc(top_set, 1)
            dve_.wait_ge(sig_set, 1)
            v.scalar_tensor_tensor(out=sc_work[:, 0:N], in0=sc_work[:, 0:N], scalar=MARK, in1=sc[:, 0:N],
                                   op0=ALU.is_equal, op1=ALU.mult).then_inc(mask_set, 1)
            dve_.wait_ge(topT_done, 1)
            for m, n in ((0, P), (1, REST2)):
                v.tensor_copy(idx[0:n, m], PG[1][0][0:n, m * NX:(m + 1) * NX]).then_inc(idx_set, 1)
                v.tensor_scalar(sco[0:n, m], PG[1][0][0:n, 32 + m * NX:32 + (m + 1) * NX], 1.0, 0.5 / WSC,
                                ALU.add, ALU.mult).then_inc(idx_set, 1)
            dve_.wait_ge(mask_hi, 1)
            dve_.wait_ge(mask_set, 1)
            low = slice(64, 64 + NX)
            v.tensor_tensor(smask[low], sc_work[low], smask[low], ALU.subtract).then_inc(mask_lo, 1)
            dve_.wait_ge(sd_set, 2 * NT)
            def evac_xg(e, par, pr=PR):
                dve_.wait_ge(xgT_done, e + 1)
                v.tensor_copy(xgT[:, par, 1, :, 0:P], PT[1].rearrange("p (k c) -> p k c", k=KD))
                v.tensor_copy(xgT[:, par, 1, :, P:CAP], pr[1][:, :, 0:REST]).then_inc(xgT_lo, 1)
            for i in range(2 * NT):
                if i == 8:
                    evac_xg(0, 0, PR0)
                dve_.wait_ge(base_done, i + 1)
                a = half_row(zx, i // 2, i % 2)
                v.scalar_tensor_tensor(out=a, in0=PU[i % 2], scalar=0.5 / WSC, in1=a,
                                       op0=ALU.mult, op1=ALU.add).then_inc(base_set, 1)

            def expert(e, par, half, last):
                def product_of(j):
                    dve_.wait_ge(at_set, e * 4 + (j + 1))
                    t_ = a_t[:, j % 2]
                    v.scalar_tensor_tensor(out=t_[:, 0, 0:CAP], in0=t_[:, 0, 0:CAP], scalar=1.0, in1=t_[:, 1, 0:CAP],
                                           op0=ALU.add, op1=ALU.mult).then_inc(a_mid, 1)
                    dve_.wait_ge(a_mid, e * 4 + (j + 1))
                    v.tensor_tensor(t_[:, 3, 0:CAP], t_[:, 0, 0:CAP], t_[:, 2, 0:CAP], ALU.mult).then_inc(a_set, 1)
                def a_low(j):
                    dve_.wait_ge(a_hi, e * 4 + (j + 1))
                    v.tensor_tensor(a_pair[:, par, j, CAP:A_LOW], a_t[:, j % 2, 3, P:CAP], a_pair[:, par, j, P:CAP],
                                    ALU.subtract)
                    v.tensor_tensor(a_pair[:, par, j, A_LOW:A_LOW + P], a_t[:, j % 2, 3, 0:P], a_pair[:, par, j, 0:P],
                                    ALU.subtract).then_inc(a_lo, 1)
                def next_w(c):
                    if last:
                        return
                    dve_.wait_ge(est_hi, e * 6 + (10 + c))
                    w = ew[:, 1 - par, :, c * 2048:(c + 1) * 2048]
                    v.scalar_tensor_tensor(out=w[:, 1], in0=stage[(c + 2 * par) % 4], scalar=WSC, in1=w[:, 0],
                                           op0=ALU.mult, op1=ALU.subtract).then_inc(est_lo, 1)
                for j in range(4):
                    product_of(j)
                    if j < 2:
                        next_w(j)
                    a_low(j)
                if not last:
                    evac_xg(e + 1, 1 - par)
                next_w(2)
                next_w(3)
                next_w(4)
                next_w(5)
                for h in range(2):
                    dve_.wait_ge(dn_done, e * 4 + (h + 3))
                    wait(dve_, eo_out, e * 48 - 48)
                    v.tensor_scalar(eo[0:REST2, par, 1, h * HALF:(h + 1) * HALF], PU[h][0:REST2],
                                    sco[0:REST2, 1, e:e + 1] if isinstance(e, int) else sco[0:REST2, 1, bass.ds(e, 1)],
                                    None, ALU.mult).then_inc(dn_d, 1)
            dve_.wait_ge(est_lo, 9)
            dve_.wait_ge(base_out, 16 * NT)
            experts(dve_, expert)



def kernel(**inputs):
    import numpy as np
    import concourse.bacc as bacc
    from concourse.bass_utils import run_bass_kernel_spmd

    f = {k: np.asarray(v) for k, v in inputs.items()}

    def blocks(a, k):
        return np.ascontiguousarray(a.reshape(k, P, -1).transpose(1, 0, 2).reshape(P, -1))

    def trio(a):
        return np.concatenate([np.pad(a, ((0, 32 - NX), (0, 0))), np.pad(a, ((0, 32 - NX), (0, 0))), a])

    arrays = {
        "x": np.pad(f["x"], ((0, NP - N), (0, 0))),
        "src": f["src"].reshape(EPART, ECOL),
        "dst": f["dst"].reshape(EPART, ECOL),
        "etype": f["edge_type_8"].reshape(EPART, ECOL),
        "wall": np.concatenate([f["L0_gnn_weight"], f["L0_gnn_root"][None], f["L0_gnn_w_gate"][D:][None],
                                f["L0_gnn_w_gate"][:D][None]]),
        "bias": f["L0_gnn_bias"],
        "b_gate": f["L0_gnn_b_gate"],
        "gate_wT": blocks(trio(f["L0_ffn_gate_w"]).T, KD),
        "upT": np.stack([blocks(a.T, KD) for a in f["L0_ffn_up_w"]]),
        "up_b": np.ascontiguousarray(f["L0_ffn_up_b"].reshape(NX, KF, P).transpose(2, 0, 1).reshape(P, -1)),
        "gT": np.stack([blocks(a.T, KD) for a in f["L0_ffn_gw"]]),
        "gb": np.ascontiguousarray(f["L0_ffn_gb"].reshape(NX, KF, P).transpose(2, 0, 1).reshape(P, -1)),
        "downT": np.stack([blocks(a.T, KF) for a in f["L0_ffn_down_w"]]),
        "down_b": trio(f["L0_ffn_down_b"]),
        "sgT": blocks(f["L0_ffn_sh_gate_w"].T, KD),
        "suT": blocks(f["L0_ffn_sh_up_w"].T, KD),
        "sdT": blocks(f["L0_ffn_sh_down_w"].T, KS),
    }
    nc = bacc.Bacc("TRN2", target_bir_lowering=False, num_devices=1)
    aps = {n: nc.dram_tensor("in_" + n, a.shape, mybir.dt.from_np(a.dtype), kind="ExternalInput").ap()
           for n, a in arrays.items()}
    out = nc.dram_tensor("out", (N, D), FP32, kind="ExternalOutput").ap()
    build(nc, out=out, **aps)
    r = run_bass_kernel_spmd(nc, [{"in_" + n: a for n, a in arrays.items()}], core_ids=[0])
    return r.results[0]["out"]
```
